# Optimizing a Trainium2 kernel written in Bass

```python
import numpy as np
import jax
import jax.numpy as jnp

def _softmax(x, axis=-1):
    return jax.nn.softmax(x, axis=axis)

def _gelu(x):
    return jax.nn.gelu(x, approximate=True)

def _silu(x):
    return jax.nn.silu(x)

def _sigmoid(x):
    return jax.nn.sigmoid(x)

def _layernorm(x, axis=-1, eps=1e-05):
    m = jnp.mean(x, axis=axis, keepdims=True)
    v = jnp.var(x, axis=axis, keepdims=True)
    return (x - m) / jnp.sqrt(v + eps)

def _scatter_add(tgt, idx, src, axis=0):
    return tgt.at[idx].add(src)

def _segment_sum(src, seg, n):
    return jax.ops.segment_sum(src, seg, n)
kernel_name = 'mk_seq_postln_d2_jaxref_r4_680eaa'

def setup_inputs(seed: int=0):
    np.random.seed(seed)
    _w = jnp.asarray

    def _L0_attn_setup():
        import jax, jax.numpy as jnp
        import numpy as np
        DIM = 256
        NUM_HEADS = 16
        HEAD_DIM = DIM // NUM_HEADS
        EPS = 1e-06

        def layer_norm(x, gamma, beta):
            mu = jnp.mean(x, axis=-1, keepdims=True)
            var = jnp.mean(jnp.square(x - mu), axis=-1, keepdims=True)
            return (x - mu) / jnp.sqrt(var + EPS) * gamma + beta

        def apply_rope(q, k):
            seq_len, head_dim = (q.shape[1], q.shape[3])
            half = head_dim // 2
            freq_range = jnp.arange(half, dtype=jnp.float32) / half
            inv_freq = 1.0 / 10000.0 ** freq_range
            t = jnp.arange(seq_len, dtype=jnp.float32)
            freqs = jnp.outer(t, inv_freq)
            emb = jnp.concatenate([freqs, freqs], axis=-1)
            cos = jnp.cos(emb)[None, :, None, :]
            sin = jnp.sin(emb)[None, :, None, :]

            def rotate_half(x):
                x1, x2 = (x[..., :half], x[..., half:])
                return jnp.concatenate([-x2, x1], axis=-1)
            return (q * cos + rotate_half(q) * sin, k * cos + rotate_half(k) * sin)
        key = jax.random.key(seed)
        ks = jax.random.split(key, 4)
        B, S = (2, 512)
        x = jax.random.normal(ks[0], (B, S, DIM), dtype=jnp.float32)
        lim_qkv = float(np.sqrt(6.0 / (DIM + 3 * DIM)))
        w_qkv = jax.random.uniform(ks[1], (3 * DIM, DIM), dtype=jnp.float32, minval=-lim_qkv, maxval=lim_qkv)
        lim_p = float(np.sqrt(6.0 / (DIM + DIM)))
        w_proj = jax.random.uniform(ks[2], (DIM, DIM), dtype=jnp.float32, minval=-lim_p, maxval=lim_p)
        b_proj = jnp.zeros((DIM,), dtype=jnp.float32)
        q_gamma = jnp.ones((HEAD_DIM,), dtype=jnp.float32)
        q_beta = jnp.zeros((HEAD_DIM,), dtype=jnp.float32)
        k_gamma = jnp.ones((HEAD_DIM,), dtype=jnp.float32)
        k_beta = jnp.zeros((HEAD_DIM,), dtype=jnp.float32)
        return {'x': x, 'w_qkv': w_qkv, 'w_proj': w_proj, 'b_proj': b_proj, 'q_gamma': q_gamma, 'q_beta': q_beta, 'k_gamma': k_gamma, 'k_beta': k_beta}
    _L0_attn_in = _L0_attn_setup()

    def _L0_ffn_setup():
        import jax, jax.numpy as jnp
        import numpy as np
        DIM = 256
        HIDDEN = 768
        SCALE = 1.0 / 127.0

        def _dequant(w_int, dtype):
            return w_int.astype(dtype) * jnp.asarray(SCALE, dtype)
        key = jax.random.key(seed)
        k_x, k_g, k_u, k_d = jax.random.split(key, 4)
        x = jax.random.normal(k_x, (4, 512, DIM), dtype=jnp.float32)
        w_gate = jax.random.randint(k_g, (HIDDEN, DIM), -127, 128, dtype=jnp.int32)
        w_up = jax.random.randint(k_u, (HIDDEN, DIM), -127, 128, dtype=jnp.int32)
        w_down = jax.random.randint(k_d, (DIM, HIDDEN), -127, 128, dtype=jnp.int32)
        return {'x': x, 'w_gate': w_gate, 'w_up': w_up, 'w_down': w_down}
    _L0_ffn_in = _L0_ffn_setup()

    def _L1_attn_setup():
        import jax, jax.numpy as jnp
        import numpy as np
        import math
        N_HEADS = 8

        def _head_dirs():
            t = np.array([[(i >> 2 & 1) * 2 - 1, (i >> 1 & 1) * 2 - 1, (i & 1) * 2 - 1] for i in range(8)], dtype=np.float32)
            return jnp.asarray(t / np.sqrt(3.0, dtype=np.float32))
        key = jax.random.key(seed)
        k1, k2, k3, k4 = jax.random.split(key, 4)
        B, T, C = (2, 512, 256)
        x = jax.random.normal(k1, (B, T, C), dtype=jnp.float32)
        w_qkv = jax.random.normal(k2, (C, 3 * C), dtype=jnp.float32) * (1.0 / math.sqrt(C))
        w_out = jax.random.normal(k3, (C, C), dtype=jnp.float32) * (1.0 / math.sqrt(C))
        head_scales = jax.random.normal(k4, (N_HEADS,), dtype=jnp.float32) * 0.1
        return {'x': x, 'w_qkv': w_qkv, 'w_out': w_out, 'head_scales': head_scales}
    _L1_attn_in = _L1_attn_setup()

    def _L1_ffn_setup():
        import math
        import jax, jax.numpy as jnp
        import numpy as np
        B, S, H = (4, 1024, 256)
        FFN = 1024
        E = 16
        N_ZERO, N_COPY, N_CONST = (1, 1, 2)
        MLP_START = N_ZERO + N_COPY + N_CONST
        E_MLP = E - MLP_START
        TOP_K = 2
        CAP_FACTOR = 1.0
        EPS = 1e-05

        def _rmsnorm(x, w, eps):
            return x * jax.lax.rsqrt(jnp.mean(x * x, axis=-1, keepdims=True) + eps) * w
        key = jax.random.key(seed)
        ks = jax.random.split(key, 6)
        std = jnp.float32(0.02)
        return {'x': jax.random.normal(ks[0], (B, S, H), jnp.float32), 'norm_weight': jnp.ones((H,), jnp.float32), 'router_weight': jax.random.normal(ks[1], (E, H), jnp.float32) * std, 'router_bias': jnp.zeros((E,), jnp.float32), 'fc1_weight': jax.random.normal(ks[2], (E_MLP, FFN, H), jnp.float32) * std, 'fc1_bias': jnp.zeros((E_MLP, FFN), jnp.float32), 'fc2_weight': jax.random.normal(ks[3], (E_MLP, H, FFN), jnp.float32) * std, 'fc2_bias': jnp.zeros((E_MLP, H), jnp.float32), 'constant_vectors': jax.random.normal(ks[4], (N_CONST, H), jnp.float32) * std}
    _L1_ffn_in = _L1_ffn_setup()
    _d = {'L0_attn_x': _L0_attn_in['x'], 'L0_attn_w_qkv': _L0_attn_in['w_qkv'], 'L0_attn_w_proj': _L0_attn_in['w_proj'], 'L0_attn_b_proj': _L0_attn_in['b_proj'], 'L0_attn_q_gamma': _L0_attn_in['q_gamma'], 'L0_attn_q_beta': _L0_attn_in['q_beta'], 'L0_attn_k_gamma': _L0_attn_in['k_gamma'], 'L0_attn_k_beta': _L0_attn_in['k_beta'], 'L0_ffn_w_gate': _L0_ffn_in['w_gate'], 'L0_ffn_w_up': _L0_ffn_in['w_up'], 'L0_ffn_w_down': _L0_ffn_in['w_down'], 'L1_attn_w_qkv': _L1_attn_in['w_qkv'], 'L1_attn_w_out': _L1_attn_in['w_out'], 'L1_attn_head_scales': _L1_attn_in['head_scales'], 'L1_ffn_norm_weight': _L1_ffn_in['norm_weight'], 'L1_ffn_router_weight': _L1_ffn_in['router_weight'], 'L1_ffn_router_bias': _L1_ffn_in['router_bias'], 'L1_ffn_fc1_weight': _L1_ffn_in['fc1_weight'], 'L1_ffn_fc1_bias': _L1_ffn_in['fc1_bias'], 'L1_ffn_fc2_weight': _L1_ffn_in['fc2_weight'], 'L1_ffn_fc2_bias': _L1_ffn_in['fc2_bias'], 'L1_ffn_constant_vectors': _L1_ffn_in['constant_vectors']}
    _x0 = _d['L0_attn_x']
    _d['L0_attn_x'] = jax.random.normal(jax.random.fold_in(jax.random.key(seed), 1), (4, 1024, 256), dtype=_x0.dtype)
    del _x0
    return _d

def reference(L0_attn_x, L0_attn_w_qkv, L0_attn_w_proj, L0_attn_b_proj, L0_attn_q_gamma, L0_attn_q_beta, L0_attn_k_gamma, L0_attn_k_beta, L0_ffn_w_gate, L0_ffn_w_up, L0_ffn_w_down, L1_attn_w_qkv, L1_attn_w_out, L1_attn_head_scales, L1_ffn_norm_weight, L1_ffn_router_weight, L1_ffn_router_bias, L1_ffn_fc1_weight, L1_ffn_fc1_bias, L1_ffn_fc2_weight, L1_ffn_fc2_bias, L1_ffn_constant_vectors):

    def _L0_attn_ref(x, w_qkv, w_proj, b_proj, q_gamma, q_beta, k_gamma, k_beta):
        import jax, jax.numpy as jnp
        import numpy as np
        DIM = 256
        NUM_HEADS = 16
        HEAD_DIM = DIM // NUM_HEADS
        EPS = 1e-06

        def layer_norm(x, gamma, beta):
            mu = jnp.mean(x, axis=-1, keepdims=True)
            var = jnp.mean(jnp.square(x - mu), axis=-1, keepdims=True)
            return (x - mu) / jnp.sqrt(var + EPS) * gamma + beta

        def apply_rope(q, k):
            seq_len, head_dim = (q.shape[1], q.shape[3])
            half = head_dim // 2
            freq_range = jnp.arange(half, dtype=jnp.float32) / half
            inv_freq = 1.0 / 10000.0 ** freq_range
            t = jnp.arange(seq_len, dtype=jnp.float32)
            freqs = jnp.outer(t, inv_freq)
            emb = jnp.concatenate([freqs, freqs], axis=-1)
            cos = jnp.cos(emb)[None, :, None, :]
            sin = jnp.sin(emb)[None, :, None, :]

            def rotate_half(x):
                x1, x2 = (x[..., :half], x[..., half:])
                return jnp.concatenate([-x2, x1], axis=-1)
            return (q * cos + rotate_half(q) * sin, k * cos + rotate_half(k) * sin)
        B, S, C = x.shape
        H, D = (NUM_HEADS, HEAD_DIM)
        qkv = jnp.einsum('bsc,oc->bso', x, w_qkv).reshape(B, S, 3, H, D)
        q = layer_norm(qkv[:, :, 0], q_gamma, q_beta)
        k = layer_norm(qkv[:, :, 1], k_gamma, k_beta)
        v = qkv[:, :, 2]
        q, k = apply_rope(q, k)
        scale = D ** (-0.5)
        q = q.astype(jnp.float32) * scale
        k = k.astype(jnp.float32)
        v = v.astype(jnp.float32)
        attn = jnp.einsum('bqhd,bkhd->bhqk', q, k)
        attn = jax.nn.softmax(attn, axis=-1)
        out = jnp.einsum('bhqk,bkhd->bqhd', attn, v).reshape(B, S, C)
        out = jnp.einsum('bsc,oc->bso', out, w_proj) + b_proj
        return out

    def _L0_ffn_ref(x, w_gate, w_up, w_down):
        import jax, jax.numpy as jnp
        import numpy as np
        DIM = 256
        HIDDEN = 768
        SCALE = 1.0 / 127.0

        def _dequant(w_int, dtype):
            return w_int.astype(dtype) * jnp.asarray(SCALE, dtype)
        wg = _dequant(w_gate, x.dtype)
        wu = _dequant(w_up, x.dtype)
        wd = _dequant(w_down, x.dtype)
        gate = jnp.einsum('bsd,hd->bsh', x, wg)
        up = jnp.einsum('bsd,hd->bsh', x, wu)
        h = jax.nn.silu(gate) * up
        return jnp.einsum('bsh,dh->bsd', h, wd)

    def _L1_attn_ref(x, w_qkv, w_out, head_scales):
        import jax, jax.numpy as jnp
        import numpy as np
        import math
        N_HEADS = 8

        def _head_dirs():
            t = np.array([[(i >> 2 & 1) * 2 - 1, (i >> 1 & 1) * 2 - 1, (i & 1) * 2 - 1] for i in range(8)], dtype=np.float32)
            return jnp.asarray(t / np.sqrt(3.0, dtype=np.float32))
        B, T, C = x.shape
        H = N_HEADS
        hd = C // H
        scale = 1.0 / math.sqrt(hd)
        dirs = _head_dirs()
        qkv = (x @ w_qkv).reshape(B, T, 3, H, hd)
        q = jnp.transpose(qkv[:, :, 0], (0, 2, 1, 3))
        k = jnp.transpose(qkv[:, :, 1], (0, 2, 1, 3))
        v = jnp.transpose(qkv[:, :, 2], (0, 2, 1, 3))
        scores = jnp.einsum('bhqd,bhkd->bhqk', q, k) * scale
        causal = jnp.tril(jnp.ones((T, T), dtype=bool))
        scores = jnp.where(causal[None, None], scores, -jnp.inf)
        q_proj = jnp.einsum('bhtd,hd->bht', q[..., :3], dirs)
        k_proj = jnp.einsum('bhtd,hd->bht', k[..., :3], dirs)
        geo = q_proj[..., :, None] * k_proj[..., None, :]
        scores = scores + head_scales[None, :, None, None] * geo
        attn = jax.nn.softmax(scores, axis=-1)
        out = jnp.einsum('bhqk,bhkd->bqhd', attn, v).reshape(B, T, C)
        return out @ w_out

    def _L1_ffn_ref(x, norm_weight, router_weight, router_bias, fc1_weight, fc1_bias, fc2_weight, fc2_bias, constant_vectors):
        import math
        import jax, jax.numpy as jnp
        import numpy as np
        B, S, H = (4, 1024, 256)
        FFN = 1024
        E = 16
        N_ZERO, N_COPY, N_CONST = (1, 1, 2)
        MLP_START = N_ZERO + N_COPY + N_CONST
        E_MLP = E - MLP_START
        TOP_K = 2
        CAP_FACTOR = 1.0
        EPS = 1e-05

        def _rmsnorm(x, w, eps):
            return x * jax.lax.rsqrt(jnp.mean(x * x, axis=-1, keepdims=True) + eps) * w
        Bsz, Sl, Hd = x.shape
        N = Bsz * Sl
        CAP = int(math.ceil(CAP_FACTOR * N * TOP_K / E))
        x_flat = x.reshape(N, Hd)
        xn = _rmsnorm(x_flat, norm_weight, EPS)
        logits = xn @ router_weight.T + router_bias
        probs = jax.nn.softmax(logits, axis=-1)
        gate_vals, expert_idx = jax.lax.top_k(probs, TOP_K)
        e_flat = expert_idx.reshape(-1)
        g_flat = gate_vals.reshape(-1)
        oh = jax.nn.one_hot(e_flat, E, dtype=jnp.int32)
        pos = jnp.sum(jnp.cumsum(oh, axis=0) * oh, axis=-1) - 1
        keep = pos < CAP
        slot = jnp.clip(pos, 0, CAP - 1)
        tok = jnp.repeat(jnp.arange(N), TOP_K)
        contrib = xn[tok] * keep[:, None].astype(x.dtype)
        dispatch = jnp.zeros((E, CAP, Hd), x.dtype).at[e_flat, slot].add(contrib)
        out_zero = jnp.zeros((N_ZERO, CAP, Hd), x.dtype)
        out_copy = dispatch[N_ZERO:N_ZERO + N_COPY]
        out_const = jnp.broadcast_to(constant_vectors[:, None, :], (N_CONST, CAP, Hd))
        dm = dispatch[MLP_START:]
        h = jnp.einsum('ech,efh->ecf', dm, fc1_weight) + fc1_bias[:, None, :]
        h = jax.nn.gelu(h, approximate=False)
        out_mlp = jnp.einsum('ecf,ehf->ech', h, fc2_weight) + fc2_bias[:, None, :]
        expert_out = jnp.concatenate([out_zero, out_copy, out_const, out_mlp], axis=0)
        gathered = expert_out[e_flat, slot]
        w = g_flat * keep.astype(g_flat.dtype)
        combined = (gathered * w[:, None]).reshape(N, TOP_K, Hd).sum(axis=1)
        gate_sums = w.reshape(N, TOP_K).sum(axis=1, keepdims=True)
        out = combined / jnp.where(gate_sums > 0, gate_sums, 1.0)
        return out.reshape(Bsz, Sl, Hd)
    x = L0_attn_x
    x = _layernorm(x + _L0_attn_ref(x, L0_attn_w_qkv, L0_attn_w_proj, L0_attn_b_proj, L0_attn_q_gamma, L0_attn_q_beta, L0_attn_k_gamma, L0_attn_k_beta), axis=-1)
    x = _layernorm(x + _L0_ffn_ref(x, L0_ffn_w_gate, L0_ffn_w_up, L0_ffn_w_down), axis=-1)
    x = _layernorm(x + _L1_attn_ref(x, L1_attn_w_qkv, L1_attn_w_out, L1_attn_head_scales), axis=-1)
    x = _layernorm(x + _L1_ffn_ref(x, L1_ffn_norm_weight, L1_ffn_router_weight, L1_ffn_router_bias, L1_ffn_fc1_weight, L1_ffn_fc1_bias, L1_ffn_fc2_weight, L1_ffn_fc2_bias, L1_ffn_constant_vectors), axis=-1)
    return x

_drawn_inputs = setup_inputs


def setup_inputs(seed=0):
    import zlib

    import numpy as np

    out = dict(_drawn_inputs(seed))
    spreads = {'L0_attn_b_proj': (0.0, 0.1),
     'L0_attn_q_gamma': (1.0, 0.6),
     'L0_attn_q_beta': (0.0, 0.561),
     'L0_attn_k_gamma': (1.0, 0.6),
     'L0_attn_k_beta': (0.0, 0.547),
     'L1_ffn_norm_weight': (1.0, 0.2),
     'L1_ffn_router_bias': (0.0, 0.1),
     'L1_ffn_fc1_bias': (0.0, 0.336),
     'L1_ffn_fc2_bias': (0.0, 0.1)}
    factors = {'L1_attn_head_scales': 2.702, 'L1_ffn_constant_vectors': 8.0}
    for name, (base, spread) in spreads.items():
        noise = np.random.default_rng([zlib.crc32(name.encode()), seed]).standard_normal(out[name].shape)
        drawn = base * np.exp(spread * noise) if base else spread * noise
        out[name] = jnp.asarray(drawn.astype(out[name].dtype))
    for name, factor in factors.items():
        out[name] = (out[name] * factor).astype(out[name].dtype)
    return out
```

```python
from contextlib import ExitStack

import numpy as np
import concourse.bass as bass
from concourse import mybir

F32 = mybir.dt.float32
BF16 = mybir.dt.bfloat16
I32 = mybir.dt.int32
U32 = mybir.dt.uint32
ALU = mybir.AluOpType
ACT = mybir.ActivationFunctionType
AX = mybir.AxisListType

P = 128
BATCH, SEQ, DIM = 4, 1024, 256
TOKENS = BATCH * SEQ
TILES = TOKENS // P
TPB = SEQ // P
CD = DIM // P
BLK = 512
TPK = BLK // P
BLOCKS = TOKENS // BLK
PARTS = 3
COMBOS = [(0, 0), (0, 1), (0, 2), (1, 0), (1, 1), (2, 0)]
MASKED = -1.0e30
LN_EPS = 1e-5

H0, D0 = 16, 16
G0 = 4
HG0 = H0 // G0
QK0_EPS = 1e-6
VS0 = 32
QK_COLS = 2 * H0 * D0
QK_BLK = QK_COLS // P

C_IDENT, C_MASK_Q, C_MASK_K, C_BEFORE, C_COS, C_SIN, C_IOTA, C_DIRS, C_MOVES = np.cumsum(
    [0, P, P, P, P, TPB * D0, TPB * D0, 16, 24]).tolist()
C_COLS = C_MOVES + 16


def constants():
    c = np.zeros((P, C_COLS), np.float32)
    i = np.arange(P)
    c[:, C_IDENT:C_IDENT + P] = np.eye(P)
    c[:, C_MASK_Q:C_MASK_Q + P] = np.where(i[None, :] > i[:, None], MASKED, 0.0)
    c[:, C_MASK_K:C_MASK_K + P] = np.where(i[None, :] < i[:, None], MASKED, 0.0)
    c[:, C_BEFORE:C_BEFORE + P] = i[:, None] < i[None, :]
    half = D0 // 2
    inv_freq = np.float32(1.0) / np.float32(10000.0) ** (np.arange(half, dtype=np.float32) / np.float32(half))
    freqs = np.outer(np.arange(SEQ, dtype=np.float32), inv_freq.astype(np.float32)).astype(np.float32)
    cos = np.cos(np.concatenate([freqs, freqs], -1)).astype(np.float32)
    sin = np.sin(np.concatenate([-freqs, freqs], -1)).astype(np.float32)
    for at, table in ((C_COS, cos), (C_SIN, sin)):
        c[:, at:at + TPB * D0] = table.reshape(TPB, P, D0).transpose(1, 0, 2).reshape(P, TPB * D0)
    c[:, C_IOTA:C_IOTA + 16] = np.arange(16)
    dirs = np.array([[(n >> 2 & 1) * 2 - 1, (n >> 1 & 1) * 2 - 1, (n & 1) * 2 - 1] for n in range(8)], np.float32)
    c[:, C_DIRS:C_DIRS + 24] = (dirs / np.sqrt(3.0, dtype=np.float32)).reshape(1, 24)
    c[:, C_MOVES:C_MOVES + 16] = [0, 1, 0, 0] + [1] * 12
    return c


class Alloc:

    def __init__(self, nc, ctx, phase):
        self.nc, self.ctx, self.phase = nc, ctx, phase
        self.sems = []
        ctx.callback(self.clear)

    def sb(self, name, shape, dt=F32):
        return self.ctx.enter_context(self.nc.sbuf_tensor(f"{self.phase}_{name}", shape, dt))

    def ps(self, name, shape, dt=F32):
        return self.ctx.enter_context(self.nc.psum_tensor(f"{self.phase}_{name}", shape, dt))

    def sem(self, name):
        self.sems.append(self.nc.alloc_semaphore(f"{self.phase}_{name}"))
        return self.sems[-1]

    def clear(self):
        self.nc.clear_and_free_semaphores(self.sems)
        self.nc.all_engine_barrier()


def phase_qkv0(nc, d, keep):
    with ExitStack() as ctx:
        a = Alloc(nc, ctx, "a")
        const = keep["const"]
        ident = const[:, C_IDENT:C_IDENT + P]
        wT = a.sb("wT", [P, CD, 3 * DIM])
        wmean = a.sb("wmean", [P, CD, 2 * H0])
        gb = a.sb("gb", [P, 4, D0])
        gbs = a.sb("gbs", [P, 4, D0])
        ropeA = a.sb("ropeA", [P, TPB, 2, D0])
        ropeB = a.sb("ropeB", [P, TPB, 2, D0])
        ropeC = a.sb("ropeC", [P, TPB, 2, D0])
        ropeD = a.sb("ropeD", [P, TPB, 2, D0])
        eps = a.sb("eps", [P, 1])
        xT = a.sb("xT", [P, 2, CD, BLK])
        sq = a.sb("sq", [P, 2, QK_COLS])
        ss = a.sb("ss", [P, 2, 2 * H0])
        std = a.sb("std", [P, 2, 2 * H0])
        rstd = a.sb("rstd", [P, 2, 2 * H0])
        z = a.sb("z", [P, 4, 2, H0, D0])
        za = a.sb("za", [P, 2, 2, H0, D0])
        zb = a.sb("zb", [P, 2, 2, H0, D0])
        zs = a.sb("zs", [P, 2, 2, H0, D0])
        y = a.sb("y", [P, 4, QK_COLS])
        rest = a.sb("rest", [P, 2, QK_BLK, P])
        parts = a.sb("parts", [P, 2, PARTS, QK_BLK, BLK], BF16)
        vaug = a.sb("vaug", [P, 4, H0, VS0])
        QK = [a.ps(f"QK{i}", [P, QK_COLS]) for i in range(2)]
        V = [a.ps(f"V{i}", [P, DIM]) for i in range(2)]
        YT = [a.ps(f"YT{i}", [P, QK_BLK, P]) for i in range(2)]

        w_in = a.sem("w_in")
        x_in = [a.sem(f"x_in{i}") for i in range(2)]
        prep = a.sem("prep")
        ones_set = a.sem("ones_set")
        qk_ready, v_ready, v_free = a.sem("qk_ready"), a.sem("v_ready"), a.sem("v_free")
        sq_done, red_done, std_done, rstd_done = (a.sem(n) for n in ("sq_done", "red_done", "std_done", "rstd_done"))
        z_done, za_done, zb_done, zs_done, y_done = (a.sem(n) for n in ("z_done", "za_done", "zb_done", "zs_done", "y_done"))
        yt_ready, hi_done, rest_done, mid_done, lo_done = (
            a.sem(n) for n in ("yt_ready", "hi_done", "rest_done", "mid_done", "lo_done"))
        v_done = a.sem("v_done")
        parts_out = [a.sem(f"parts_out{i}") for i in range(2)]
        v_out = [a.sem(f"v_out{i}") for i in range(4)]
        zeroed, consts_in, zero_out = a.sem("zeroed"), a.sem("consts_in"), a.sem("zero_out")
        zero = a.sb("zero", [P, 4096])
        LAG = 3
        block = ctx.enter_context(nc.Block())

        @block.sync
        def _(sp):
            sp.dma_start(const[:], d["constants"]).then_inc(w_in, 16)
            sp.dma_start(wT[:], d["L0_wqkvT"].rearrange("(c p) n -> p c n", p=P)).then_inc(w_in, 16)
            half = D0 // 2
            for i, name in enumerate(("q_gamma", "q_beta", "k_gamma", "k_beta")):
                row = d["L0_attn_" + name].rearrange("(o n) -> o n", o=1)
                sp.dma_start(gb[:, i, :], row.to_broadcast([P, D0])).then_inc(w_in, 16)
                sp.dma_start(gbs[:, i, 0:half], row[:, half:D0].to_broadcast([P, half])).then_inc(w_in, 16)
                sp.dma_start(gbs[:, i, half:D0], row[:, 0:half].to_broadcast([P, half])).then_inc(w_in, 16)

            def load(b, h):
                if not first(b):
                    sp.wait_ge(v_ready, (b - 1) * TPB + (h + 1) * TPK)
                src = d["xT"][:, bass.ds(b * SEQ + h * BLK, BLK)].rearrange("(c p) n -> p c n", p=P)
                sp.dma_start(xT[:, h], src).then_inc(x_in[h], 16)

            def store(b, h):
                sp.wait_ge(lo_done, b * TPB + (h + 1) * TPK)
                dst = d["qk0"][:, :, bass.ds(b * SEQ + h * BLK, BLK)].rearrange("a p n -> p a n")
                sp.dma_start(dst, parts[:, h].rearrange("p s k n -> p (s k) n")).then_inc(parts_out[h], 16)

            for h in range(2):
                load(0, h)
            with sp.Fori(0, BATCH - 1) as b:
                for h in range(2):
                    load(b + 1, h)
                    store(b, h)
            for h in range(2):
                store(BATCH - 1, h)
            sp.wait_ge(zeroed, 1)
            sl = d["slots"].rearrange("(n p r) c -> n p (r c)", p=P, r=16)
            for n in range(4):
                sp.dma_start(sl[n], zero[:]).then_inc(zero_out, 16)
            sp.wait_ge(zero_out, 64)
            for n in range(2):
                row = d["L1_ffn_constant_vectors"][n:n + 1, :].to_broadcast([CAP, DIM])
                sp.dma_start(d["slots"][(2 + n) * CAP:(3 + n) * CAP, :], row).then_inc(consts_in, 16)
            sp.wait_ge(consts_in, 32)
            for h in range(2):
                sp.wait_ge(parts_out[h], 16 * BATCH + 16)

        @block.gpsimd
        def _(pool):
            pool.memset(zero[:], 0.0).then_inc(zeroed, 1)
            pool.wait_ge(prep, 14)

            def steps(b, lo, hi):
                for k in range(lo, hi):
                    n = b * TPB + k
                    if k < TPB:
                        pool.wait_ge(z_done, n + 1)
                        tab = ropeA[:, k % TPB].unsqueeze(2).to_broadcast([P, 2, H0, D0])
                        pool.tensor_tensor(za[:, k % 2], z[:, k % 4], tab, ALU.mult).then_inc(za_done, 1)
                    m = k - 1
                    if (not first(b) or m >= 0) and m < TPB:
                        pool.wait_ge(zs_done, n)
                        if not (first(b) and m < 4):
                            pool.wait_ge(yt_ready, n - 4)
                        tab = ropeC[:, m % TPB].unsqueeze(2).to_broadcast([P, 2, H0, D0])
                        out = y[:, m % 4].rearrange("p (x h c) -> p x h c", x=2, h=H0)
                        pool.tensor_tensor(out, zs[:, m % 2], tab, ALU.add).then_inc(y_done, 1)
                    m = k - 3
                    if (not first(b) or m >= 0) and m < TPB:
                        pool.wait_ge(mid_done, n - 2)
                        t = m % TPB
                        at = parts[:, t // TPK, :, :, (t % TPK) * P:(t % TPK + 1) * P]
                        pool.tensor_tensor(at[:, 2], rest[:, m % 2], at[:, 1], ALU.subtract).then_inc(lo_done, 1)

            pipeline(pool, steps, LAG)

        @block.tensor
        def _(pe):
            pe.wait_ge(prep, 14)

            def qkv(b, t):
                n = b * TPB + t
                h, at = t // TPK, (t % TPK) * P
                if t % TPK == 0:
                    pe.wait_ge(x_in[h], b * 16 + 16)
                if not (first(b) and t < 2):
                    pe.wait_ge(z_done, n - 1)
                    pe.wait_ge(v_done, n - 1)
                for c in range(CD):
                    mm = pe.matmul(QK[t % 2][:], xT[:, h, c, at:at + P], wT[:, c, 0:QK_COLS],
                                   start=(c == 0), stop=(c == CD - 1))
                mm.then_inc(qk_ready, 1)
                for c in range(CD):
                    mm = pe.matmul(V[t % 2][:], xT[:, h, c, at:at + P], wT[:, c, QK_COLS:3 * DIM],
                                   start=(c == 0), stop=(c == CD - 1))
                mm.then_inc(v_ready, 1)

            def turn(b, t):
                n = b * TPB + t
                pe.wait_ge(y_done, n + 1)
                if not (first(b) and t < 2):
                    pe.wait_ge(rest_done, n - 1)
                for i in range(QK_BLK):
                    mm = pe.transpose(YT[t % 2][:, i], y[:, t % 4, i * P:(i + 1) * P], ident)
                mm.then_inc(yt_ready, 1)

            def steps(b, lo, hi):
                for k in range(lo, hi):
                    if k < TPB:
                        qkv(b, k)
                    m = k - 2
                    if (not first(b) or m >= 0) and m < TPB:
                        if m >= 0:
                            turn(b, m)
                        else:
                            turn(b - 1, m + TPB)

            pipeline(pe, steps, LAG)

        @block.scalar
        def _(act):
            for h in range(2):
                act.sem_inc(parts_out[h], 16)
            act.wait_ge(prep, 14)

            def steps(b, lo, hi):
                for k in range(lo, hi):
                    n = b * TPB + k
                    old = not (first(b) and k < 3) and k - 3 < TPB
                    t = (k - 3) % TPB
                    at = parts[:, t // TPK, :, :, (t % TPK) * P:(t % TPK + 1) * P]
                    if k < TPB:
                        act.wait_ge(qk_ready, n + 1)
                        if not (first(b) and k < 2):
                            act.wait_ge(red_done, n - 1)
                        act.activation(sq[:, k % 2], QK[k % 2][:], ACT.Square).then_inc(sq_done, 1)
                    if old:
                        act.wait_ge(yt_ready, n - 2)
                        if t % TPK == 0:
                            act.wait_ge(parts_out[t // TPK], b * 16 + 16 if k >= 3 else b * 16)
                        act.activation(at[:, 0], YT[t % 2][:], ACT.Copy).then_inc(hi_done, 1)
                    if k < TPB:
                        act.wait_ge(red_done, n + 1)
                        act.activation(std[:, k % 2], ss[:, k % 2], ACT.Sqrt, bias=eps[:, 0:1],
                                       scale=1.0 / D0).then_inc(std_done, 1)
                        act.wait_ge(v_ready, n + 1)
                        if not (first(b) and k < 4):
                            act.wait_ge(v_out[k % 4], (b * 2 + k // 4) * 16)
                        act.activation(vaug[:, k % 4, :, 0:D0], V[k % 2][:].rearrange("p (h c) -> p h c", h=H0),
                                       ACT.Copy).then_inc(v_done, 1)
                        act.wait_ge(v_done, n + 1)
                        act.dma_start(d["v0"][bass.ds(b * SEQ + k * P, P), :],
                                      vaug[:, k % 4].rearrange("p h c -> p (h c)")).then_inc(v_out[k % 4], 16)
                    if old:
                        act.wait_ge(rest_done, n - 2)
                        act.activation(at[:, 1], rest[:, t % 2], ACT.Copy).then_inc(mid_done, 1)

            pipeline(act, steps, LAG)
            for i in range(4):
                act.wait_ge(v_out[i], 16 * TILES // 4)

        @block.vector
        def _(dve):
            dve.memset(eps[:], QK0_EPS).then_inc(prep, 1)
            for i in range(4):
                last = dve.memset(vaug[:, i], 0.0)
            last.then_inc(ones_set, 1)
            dve.wait_ge(ones_set, 1)
            dve.memset(vaug[:, :, :, D0:D0 + 1], 1.0).then_inc(prep, 1)
            dve.wait_ge(w_in, 16 * 14)
            for c in range(CD):
                last = dve.tensor_reduce(wmean[:, c], wT[:, c, 0:QK_COLS].rearrange("p (h c) -> p h c", c=D0),
                                         AX.X, ALU.add)
            last.then_inc(prep, 1)
            for x in range(2):
                if x == 0:
                    for g in (gb, gbs):
                        last = dve.tensor_scalar(g[:, 0:2], g[:, 0:2], float(D0) ** -0.5, None, ALU.mult)
                    last.then_inc(prep, 1)
            dve.wait_ge(prep, 4)
            dve.tensor_scalar(wmean[:], wmean[:], 1.0 / D0, None, ALU.mult).then_inc(prep, 1)
            dve.wait_ge(prep, 5)
            for c in range(CD):
                w = wT[:, c, 0:QK_COLS].rearrange("p (h c) -> p h c", c=D0)
                last = dve.tensor_tensor(w, w, wmean[:, c].unsqueeze(2).to_broadcast([P, 2 * H0, D0]), ALU.subtract)
            last.then_inc(prep, 1)
            cos = const[:, C_COS:C_COS + TPB * D0].rearrange("p (t c) -> p t c", t=TPB)
            sin = const[:, C_SIN:C_SIN + TPB * D0].rearrange("p (t c) -> p t c", t=TPB)
            for x in range(2):
                def row(g, i):
                    return g[:, 2 * x + i].unsqueeze(1).to_broadcast([P, TPB, D0])
                dve.tensor_tensor(ropeA[:, :, x], cos, row(gb, 0), ALU.mult).then_inc(prep, 1)
                dve.tensor_tensor(ropeB[:, :, x], sin, row(gbs, 0), ALU.mult).then_inc(prep, 1)
                dve.tensor_tensor(ropeC[:, :, x], cos, row(gb, 1), ALU.mult).then_inc(prep, 1)
                dve.tensor_tensor(ropeD[:, :, x], sin, row(gbs, 1), ALU.mult).then_inc(ones_set, 1)
                dve.wait_ge(prep, 9 + 4 * x)
                dve.wait_ge(ones_set, 2 + x)
                dve.tensor_tensor(ropeC[:, :, x], ropeC[:, :, x], ropeD[:, :, x], ALU.add).then_inc(prep, 1)
            dve.wait_ge(prep, 14)
            half = D0 // 2

            def steps(b, lo, hi):
                for k in range(lo, hi):
                    n = b * TPB + k
                    if k < TPB:
                        dve.wait_ge(sq_done, n + 1)
                        if not (first(b) and k < 2):
                            dve.wait_ge(std_done, n - 1)
                        dve.tensor_reduce(ss[:, k % 2], sq[:, k % 2].rearrange("p (h c) -> p h c", c=D0), AX.X,
                                          ALU.add).then_inc(red_done, 1)
                    if not (first(b) and k < 3) and k - 3 < TPB:
                        t = (k - 3) % TPB
                        at = parts[:, t // TPK, :, :, (t % TPK) * P:(t % TPK + 1) * P]
                        dve.wait_ge(hi_done, n - 2)
                        if not (first(b) and k < 5):
                            dve.wait_ge(lo_done, n - 4)
                        dve.tensor_tensor(rest[:, t % 2], YT[t % 2][:], at[:, 0], ALU.subtract).then_inc(rest_done, 1)
                    if k < TPB:
                        dve.wait_ge(std_done, n + 1)
                        dve.reciprocal(rstd[:, k % 2], std[:, k % 2]).then_inc(rstd_done, 1)
                        dve.wait_ge(rstd_done, n + 1)
                        dve.tensor_tensor(z[:, k % 4].rearrange("p x h c -> p (x h) c"),
                                          QK[k % 2][:].rearrange("p (h c) -> p h c", c=D0),
                                          rstd[:, k % 2].unsqueeze(2).to_broadcast([P, 2 * H0, D0]),
                                          ALU.mult).then_inc(z_done, 1)
                        dve.wait_ge(z_done, n + 1)
                        tab = ropeB[:, k].unsqueeze(2).to_broadcast([P, 2, H0, D0])
                        zk, zbk = z[:, k % 4], zb[:, k % 2]
                        dve.tensor_tensor(zbk[:, :, :, 0:half], zk[:, :, :, half:D0], tab[:, :, :, 0:half], ALU.mult)
                        dve.tensor_tensor(zbk[:, :, :, half:D0], zk[:, :, :, 0:half], tab[:, :, :, half:D0],
                                          ALU.mult).then_inc(zb_done, 1)
                    m = k - 1
                    if (not first(b) or m >= 0) and m < TPB:
                        dve.wait_ge(za_done, n)
                        dve.wait_ge(zb_done, n)
                        if not (first(b) and m < 2):
                            dve.wait_ge(y_done, n - 2)
                        dve.tensor_tensor(zs[:, m % 2], za[:, m % 2], zb[:, m % 2], ALU.add).then_inc(zs_done, 1)

            pipeline(dve, steps, LAG)


def first(b):
    return isinstance(b, int) and b == 0


def pipeline(eng, steps, lag):
    steps(0, 0, TPB)
    with eng.Fori(1, BATCH) as b:
        steps(b, 0, TPB)
    steps(BATCH, 0, 0) if lag == 0 else tail(steps, lag)


def tail(steps, lag):
    steps(BATCH - 1, TPB, TPB + lag)


CAP = 512
E = 16

def phase_attention0(nc, d, keep):
    UNITS = 2 * (TPB // 2) * G0
    MAXES = G0 * TPB * 2
    RING = 8
    SLOTS_FOR_MAX = 27
    K = len(COMBOS) * D0
    KM = K + PARTS
    BUFS = HG0
    with ExitStack() as ctx:
        a = Alloc(nc, ctx, "b")
        qst = [a.sb(f"qst{i}", [P, G0, SEQ], BF16) for i in range(BUFS)]
        kst = [a.sb(f"kst{i}", [P, G0, SEQ], BF16) for i in range(BUFS)]
        vst = [a.sb(f"vst{i}", [P, TPB, G0, VS0]) for i in range(BUFS)]
        probs = a.sb("probs", [P, RING, 2, BLK])
        outT = a.sb("outT", [P, 2, BLK])
        mx = a.sb("mx", [P, G0, TPB, 2])
        m = a.sb("m", [P, G0, TPB])
        mrest = a.sb("mrest", [P, G0, TPB])
        mparts = a.sb("mparts", [P, TPB, G0, 32], BF16)
        identb = a.sb("identb", [P, P], BF16)
        PM = [a.ps(f"PM{i}", [P, BLK]) for i in range(2)]
        PS = [a.ps(f"PS{i}", [P, 2, BLK]) for i in range(2)]
        PO = a.ps("PO", [P, BLK])
        PT = a.ps("PT", [P, TPB, P], BF16)

        setup = a.sem("setup")
        q_in = [a.sem(f"q_in{i}") for i in range(BUFS)]
        v_in = [a.sem(f"v_in{i}") for i in range(BUFS)]
        max_scores, max_taken = a.sem("max_scores"), a.sem("max_taken")
        m_step, m_parts, m_turned, m_rows_dve, m_rows_act = (
            a.sem(n) for n in ("m_step", "m_parts", "m_turned", "m_rows_dve", "m_rows_act"))
        scores, exped, pv_done, out_copied = (a.sem(n) for n in ("scores", "exped", "pv_done", "out_copied"))
        out_stored = [a.sem(f"out_stored{i}") for i in range(2)]
        block = ctx.enter_context(nc.Block())

        def over_groups(eng, body):
            with eng.Fori(0, BATCH - 1) as b:
                for hg in range(HG0):
                    body(b, hg, True)
            for hg in range(HG0):
                body(BATCH - 1, hg, hg < HG0 - 1)

        @block.sync
        def _(sp):
            def load(b, hg, again):
                if again:
                    sp.wait_ge(pv_done, ((b - 1) * HG0 + hg + 1) * (UNITS // G0) + 2)
                tok = bass.ds(b * SEQ, SEQ)
                for stack, side, first_blk in ((qst, 0, 0), (kst, 1, QK_BLK // 2)):
                    for s, combo in enumerate(COMBOS):
                        rows = d["qk0"][combo[side] * QK_BLK + first_blk + hg // 2, (hg % 2) * 64:(hg % 2) * 64 + 64, tok]
                        sp.dma_start(stack[hg][s * D0:(s + 1) * D0], rows.rearrange("(j p) n -> p j n", p=D0))\
                          .then_inc(q_in[hg], 16)
                src = d["v0"][tok, hg * G0 * VS0:(hg + 1) * G0 * VS0].rearrange("(t p) c -> p t c", p=P)
                sp.dma_start(vst[hg][:].rearrange("p t j c -> p t (j c)"), src).then_inc(v_in[hg], 16)

            for hg in range(HG0):
                load(0, hg, False)
            with sp.Fori(1, BATCH) as b:
                for hg in range(HG0):
                    load(b, hg, True)

        @block.tensor
        def _(pe):
            pe.sem_inc(pv_done, 2)
            pe.wait_ge(setup, 1)

            def max_product(g, nxt, u):
                j, qt, kh = u // (2 * TPB), u // 2 % TPB, u % 2
                pe.wait_ge(max_taken, g * MAXES + u + 1)
                pe.matmul(PM[u % 2][:], qst[nxt][0:K, j, qt * P:(qt + 1) * P],
                          kst[nxt][0:K, j, kh * BLK:(kh + 1) * BLK], start=True, stop=True).then_inc(max_scores, 1)

            def turn_max(g):
                pe.wait_ge(m_parts, g + 1)
                for qt in range(TPB):
                    mm = pe.transpose(PT[:, qt], mparts[:, qt].rearrange("p j c -> p (j c)"), identb[:])
                mm.then_inc(m_turned, 1)

            def values(g, hg, n):
                half, pair = n // (TPB // 2), n % (TPB // 2)
                pe.wait_ge(exped, g * UNITS + (n + 1) * G0 + 2)
                if pair == 0:
                    pe.wait_ge(out_copied, g * 2 + half + 1)
                for i in range(2):
                    for j in range(G0):
                        mm = pe.matmul(PO[j * VS0:(j + 1) * VS0, :], vst[hg][:, 2 * pair + i, j, :],
                                       probs[:, (n * G0 + j) % RING, i], start=(pair == 0 and i == 0),
                                       stop=(pair == TPB // 2 - 1 and i == 1), tile_position=(0, j * VS0))
                mm.then_inc(pv_done, 1)

            def group(b, hg, follows):
                g = b * HG0 + hg
                nxt = (hg + 1) % BUFS
                taken = 0
                pe.wait_ge(v_in[hg], b * 16 + 16)
                if follows:
                    turns = 16 * 2 * len(COMBOS)
                    pe.wait_ge(q_in[nxt], (b + (hg + 1) // BUFS) * turns + turns)
                for s in range(UNITS):
                    half, pair, j = s // (UNITS // 2), s // G0 % (TPB // 2), s % G0
                    if s < G0:
                        if j < 2:
                            pe.wait_ge(m_rows_dve, g * 2 + j + 1)
                        else:
                            pe.wait_ge(m_rows_act, g * 2 + j - 1)
                    pe.wait_ge(exped, g * UNITS + s + 1)
                    for i in range(2):
                        kt = 2 * pair + i
                        mm = pe.matmul(PS[s % 2][:, i], kst[hg][0:KM, j, kt * P:(kt + 1) * P],
                                       qst[hg][0:KM, j, half * BLK:(half + 1) * BLK], start=True, stop=True)
                    mm.then_inc(scores, 1)
                    if follows:
                        upto = min(MAXES, MAXES * (s + 1) // SLOTS_FOR_MAX)
                        for u in range(taken, upto):
                            max_product(g + 1, nxt, u)
                        taken = upto
                        if s == UNITS - 2:
                            turn_max(g + 1)
                    if s % G0 == 1 and s > G0:
                        values(g, hg, s // G0 - 1)
                values(g, hg, UNITS // G0 - 1)

            pe.wait_ge(q_in[0], 16 * 2 * len(COMBOS))
            for u in range(MAXES):
                max_product(0, 0, u)
            turn_max(0)
            over_groups(pe, group)

        @block.scalar
        def _(act):
            act.sem_inc(exped, 2)
            act.sem_inc(out_copied, 1)
            for half in range(2):
                act.sem_inc(out_stored[half], 16)

            def max_rows(g, nxt):
                act.wait_ge(m_turned, g + 1)
                for j in (2, 3):
                    act.activation(qst[nxt][K:KM, j, :], PT[32 * j:32 * j + PARTS].rearrange("p t n -> p (t n)"),
                                   ACT.Copy).then_inc(m_rows_act, 1)

            def copy_out(b, g, hg, half):
                act.wait_ge(pv_done, g * (UNITS // G0) + (half + 1) * (TPB // 2) + 2)
                act.wait_ge(out_stored[half], g * 16 + 16)
                act.activation(outT[:, half], PO[:], ACT.Copy).then_inc(out_copied, 1)
                act.wait_ge(out_copied, g * 2 + half + 2)
                act.dma_start(d["att0"][hg, :, bass.ds(b * SEQ + half * BLK, BLK)], outT[:, half])\
                   .then_inc(out_stored[half], 16)

            def group(b, hg, follows):
                g = b * HG0 + hg
                for s in range(UNITS):
                    act.wait_ge(scores, g * UNITS + s + 1)
                    if s % G0 == 0:
                        act.wait_ge(pv_done, g * (UNITS // G0) + s // G0 + 1)
                    act.activation(probs[:, s % RING], PS[s % 2][:], ACT.Exp).then_inc(exped, 1)
                    if s == UNITS // 2 + 2:
                        copy_out(b, g, hg, 0)
                if follows:
                    max_rows(g + 1, (hg + 1) % BUFS)
                copy_out(b, g, hg, 1)

            max_rows(0, 0)
            over_groups(act, group)
            for half in range(2):
                act.wait_ge(out_stored[half], 16 * (BATCH * HG0 + 1))

        @block.vector
        def _(dve):
            dve.sem_inc(max_taken, 2)
            for i in range(BUFS):
                dve.memset(kst[i][K:KM], 1.0)
            dve.tensor_copy(identb[:], keep["const"][:, C_IDENT:C_IDENT + P])
            dve.memset(mparts[:], 0.0).then_inc(setup, 1)
            dve.wait_ge(setup, 1)

            def maxima(g, nxt):
                for u in range(MAXES):
                    dve.wait_ge(max_scores, g * MAXES + u + 1)
                    dve.tensor_reduce(mx[:, u // (2 * TPB), u // 2 % TPB, u % 2:u % 2 + 1], PM[u % 2][:], AX.X, ALU.max)\
                       .then_inc(max_taken, 1)
                dve.wait_ge(max_taken, g * MAXES + MAXES + 2)
                dve.tensor_tensor(m[:], mx[:, :, :, 0], mx[:, :, :, 1], ALU.max).then_inc(m_step, 1)
                part = [mparts[:, :, :, i].rearrange("p t j -> p j t") for i in range(PARTS)]
                dve.wait_ge(m_step, g * 4 + 1)
                dve.tensor_scalar(part[0], m[:], -1.0, None, ALU.mult).then_inc(m_step, 1)
                dve.wait_ge(m_step, g * 4 + 2)
                dve.scalar_tensor_tensor(out=mrest[:], in0=m[:], scalar=-1.0, in1=part[0], op0=ALU.mult,
                                         op1=ALU.subtract).then_inc(m_step, 1)
                dve.wait_ge(m_step, g * 4 + 3)
                dve.tensor_copy(part[1], mrest[:]).then_inc(m_step, 1)
                dve.wait_ge(m_step, g * 4 + 4)
                dve.tensor_tensor(part[2], mrest[:], part[1], ALU.subtract).then_inc(m_parts, 1)
                dve.wait_ge(m_turned, g + 1)
                for j in (0, 1):
                    dve.tensor_copy(qst[nxt][K:KM, j, :], PT[32 * j:32 * j + PARTS].rearrange("p t n -> p (t n)"))\
                       .then_inc(m_rows_dve, 1)

            def group(b, hg, follows):
                if follows:
                    maxima(b * HG0 + hg + 1, (hg + 1) % BUFS)

            maxima(0, 0)
            over_groups(dve, group)

HID = 768
HC = HID // P
INT8_SCALE = float(np.float32(1.0 / 127.0))
H1, D1 = 8, 32
G1 = 2
HG1 = H1 // G1
VS1 = 64
HPS = SEQ // BLK


def lagged(b, h, lag):
    m = h - lag
    if m >= HPS or (first(b) and m < 0):
        return None
    return b * HPS + m, m % 2, first(b)


def block_pipeline(eng, step, lag):
    for h in range(HPS):
        step(0, h)
    with eng.Fori(1, BATCH) as b:
        for h in range(HPS):
            step(b, h)
    for h in range(HPS, HPS + lag):
        step(BATCH - 1, h)


def phase_ffn0(nc, d, keep):
    with ExitStack() as ctx:
        a = Alloc(nc, ctx, "c")
        const = keep["const"]
        ident = const[:, C_IDENT:C_IDENT + P]
        wproj = a.sb("wproj", [P, CD, DIM])
        bproj = a.sb("bproj", [P, DIM])
        ints = a.sb("ints", [P, 3, CD * HID], I32)
        wgate = a.sb("wgate", [P, CD, HID])
        wup = a.sb("wup", [P, CD, HID])
        wdown = a.sb("wdown", [P, HC, DIM])
        wqkv = a.sb("wqkv", [P, CD, 3 * DIM])
        hscale = a.sb("hscale", [P, H1])
        geo = a.sb("geo", [P, CD, H1, 3])
        geo1 = a.sb("geo1", [P, CD, H1])
        eps = a.sb("eps", [P, 1])
        attT = a.sb("attT", [P, 2, HG0, BLK])
        xin = a.sb("xin", [P, 2, TPK, DIM])
        rec = a.sb("rec", [P, 2, H0])
        att = a.sb("att", [P, 2, TPK, DIM])
        att2T = a.sb("att2T", [P, 2, CD, BLK])
        s1 = a.sb("s1", [P, 2, TPK, DIM])
        x1 = a.sb("x1", [P, 2, TPK, DIM])
        x1T = a.sb("x1T", [P, 2, CD, BLK])
        gate = a.sb("gate", [P, 2, BLK])
        hT = a.sb("hT", [P, 2, HC, BLK])
        s2 = a.sb("s2", [P, TPK, DIM])
        x2 = a.sb("x2", [P, 2, TPK, DIM])
        x2T = a.sb("x2T", [P, 2, CD, BLK])
        stats = a.sb("stats", [P, 2, TPK, 6])
        moments = a.sb("moments", [P, 2, TPK, 2])
        std = a.sb("std", [P, 2, TPK])
        rstd = a.sb("rstd", [P, 2, TPK])
        rest = a.sb("rest", [P, 2, BLK])
        parts = a.sb("parts", [P, 2, PARTS, 4, BLK], BF16)
        vaug = a.sb("vaug", [P, 2, TPK, H1, VS1])
        TR = [a.ps(f"TR{i}", [P, BLK]) for i in range(2)]
        PG = [a.ps(f"PG{i}", [P, BLK]) for i in range(2)]
        PU = [a.ps(f"PU{i}", [P, BLK]) for i in range(2)]
        PO = [a.ps(f"PO{i}", [P, BLK]) for i in range(2)]

        w_in, prep, vset = a.sem("w_in"), a.sem("prep"), a.sem("vset")
        seen = a.sem("seen")
        att_in = [a.sem(f"att_in{i}") for i in range(2)]
        xin_in = [a.sem(f"xin_in{i}") for i in range(2)]
        names = ("att_turned", "rec_done", "normed", "att2_turned", "att2_copied", "projected", "biased", "summed1",
                 "stat1", "aggr1", "std1", "rstd1", "x1_done", "x1_turned", "x1_copied", "gated", "upped", "silu", "hidden",
                 "downed", "summed2", "stat2", "aggr2", "std2", "rstd2", "x2_done", "x2_turned", "x2_copied",
                 "qk_ready", "hi_done", "rest_done", "mid_done", "lo_done", "v_ready", "v_copied")
        S = {n: a.sem(n) for n in names}
        x2_out = [a.sem(f"x2_out{i}") for i in range(2)]
        parts_out = [a.sem(f"parts_out{i}") for i in range(2)]
        v_out = [a.sem(f"v_out{i}") for i in range(2)]
        PREP = 10
        LAG = 2
        block = ctx.enter_context(nc.Block())

        @block.sync
        def _(sp):
            sp.dma_start(wproj[:], d["L0_wprojT"].rearrange("(c p) n -> p c n", p=P)).then_inc(w_in, 16)
            sp.dma_start(bproj[:], d["L0_attn_b_proj"].rearrange("(o n) -> o n", o=1).to_broadcast([P, DIM])).then_inc(w_in, 16)
            for i, name in enumerate(("w_gate", "w_up", "w_down")):
                sp.dma_start(ints[:, i].rearrange("p (c n) -> p c n", c=HC if i == 2 else CD),
                             d["L0_ffn_" + name + "T"].rearrange("(c p) n -> p c n", p=P)).then_inc(w_in, 16)
            sp.dma_start(wqkv[:], d["L1_attn_w_qkv"].rearrange("(c p) n -> p c n", p=P)).then_inc(w_in, 16)
            sp.dma_start(hscale[:], d["L1_attn_head_scales"].rearrange("(o n) -> o n", o=1).to_broadcast([P, H1])).then_inc(w_in, 16)

            def step(b, h):
                if now := lagged(b, h, 0):
                    n, i, new = now
                    tok = bass.ds(n * BLK if isinstance(b, int) else sp.snap(n * BLK), BLK)
                    if not new:
                        sp.wait_ge(S["att_turned"], (n - 1) * TPK)
                        sp.wait_ge(S["summed1"], (n - 1) * TPK)
                    sp.dma_start(attT[:, i], d["att0"][:, :, tok].rearrange("g p n -> p g n")).then_inc(att_in[i], 16)
                    sp.dma_start(xin[:, i], d["x"][tok, :].rearrange("(t p) c -> p t c", p=P)).then_inc(xin_in[i], 16)
                if now := lagged(b, h, 2):
                    n, i, new = now
                    tok = bass.ds(n * BLK if isinstance(b, int) else sp.snap(n * BLK), BLK)
                    sp.wait_ge(S["x2_done"], (n + 1) * TPK)
                    sp.dma_start(d["x2"][tok, :].rearrange("(t p) c -> p t c", p=P), x2[:, i]).then_inc(x2_out[i], 16)
            block_pipeline(sp, step, LAG)
            for i in range(2):
                for s in (x2_out, v_out, parts_out):
                    sp.wait_ge(s[i], 16 * BATCH + 16)

        @block.gpsimd
        def _(pool):
            pool.sem_inc(S["lo_done"], 2)
            pool.wait_ge(prep, PREP)

            def step(b, h):
                if now := lagged(b, h, 0):
                    n, i, new = now
                    pool.wait_ge(xin_in[i], b * 16 + 16)
                    pool.tensor_tensor(xin[:, i], xin[:, i], bproj[:].unsqueeze(1).to_broadcast([P, TPK, DIM]),
                                       ALU.add).then_inc(S["biased"], 1)
                if now := lagged(b, h, 2):
                    n, i, new = now
                    for k in range(4):
                        pool.wait_ge(S["mid_done"], n * 4 + k + 1)
                        pool.tensor_tensor(parts[:, i, 2, k], rest[:, k % 2], parts[:, i, 1, k], ALU.subtract)\
                            .then_inc(S["lo_done"], 1)

            block_pipeline(pool, step, LAG)

        @block.tensor
        def _(pe):
            pe.wait_ge(prep, PREP)

            def turn(src, count):
                for c in range(CD):
                    for t in range(TPK):
                        mm = pe.transpose(TR[c][:, t * P:(t + 1) * P], src[:, t, c * P:(c + 1) * P], ident)
                    mm.then_inc(count, 1)

            def step(b, h):
                if now := lagged(b, h, 0):
                    n, i, new = now
                    pe.wait_ge(att_in[i], (b * 16 + 16))
                    for t in range(TPK):
                        if t < 2 and not (first(b) and h == 0):
                            pe.wait_ge(S["x1_copied"], n * CD)
                        if t >= 2:
                            pe.wait_ge(S["normed"], n * TPK + t - 1)
                        for g in range(HG0):
                            mm = pe.transpose(TR[t % 2][:, g * P:(g + 1) * P], attT[:, i, g, t * P:(t + 1) * P], ident)
                        mm.then_inc(S["att_turned"], 1)
                if now := lagged(b, h, 1):
                    n, i, new = now
                    pe.wait_ge(S["x1_copied"], (n + 1) * CD)
                    for k in range(HC):
                        if not (new and i == 0 and k < 2):
                            pe.wait_ge(S["hidden"], n * HC + k - 1)
                        for w, out, done in ((wgate, PG, "gated"), (wup, PU, "upped")):
                            for c in range(CD):
                                mm = pe.matmul(out[k % 2][:], w[:, c, k * P:(k + 1) * P], x1T[:, i, c, :],
                                               start=(c == 0), stop=(c == CD - 1))
                            mm.then_inc(S[done], 1)
                if now := lagged(b, h, 2):
                    n, i, new = now
                    pe.wait_ge(S["x2_done"], (n + 1) * TPK)
                    if lagged(b, h, 0):
                        pe.wait_ge(S["normed"], (n + 3) * TPK)
                    else:
                        pe.wait_ge(S["x1_copied"], BLOCKS * CD)
                        if h == HPS + 1:
                            pe.wait_ge(S["x2_copied"], n * CD)
                    turn(x2[:, i], S["x2_turned"])
                if now := lagged(b, h, 0):
                    n, i, new = now
                    pe.wait_ge(S["normed"], (n + 1) * TPK)
                    if lagged(b, h, 2):
                        pe.wait_ge(S["x2_copied"], (n - 1) * CD)
                    turn(att[:, i], S["att2_turned"])
                    pe.wait_ge(S["att2_copied"], (n + 1) * CD)
                    for t in range(TPK):
                        if t < 2 and not (first(b) and h < 2):
                            pe.wait_ge(S["summed2"], (n - 1) * TPK)
                        if t >= 2:
                            pe.wait_ge(S["summed1"], n * TPK + t - 1)
                        for c in range(CD):
                            mm = pe.matmul(PO[t % 2][:, 0:DIM], att2T[:, i, c, t * P:(t + 1) * P], wproj[:, c, :],
                                           start=(c == 0), stop=(c == CD - 1))
                        mm.then_inc(S["projected"], 1)
                if now := lagged(b, h, 2):
                    n, i, new = now
                    pe.wait_ge(S["x2_copied"], (n + 1) * CD)
                    for k in range(4):
                        if k < 2:
                            if lagged(b, h, 0):
                                pe.wait_ge(S["summed1"], (n + 3) * TPK)
                            else:
                                pe.wait_ge(S["summed2"], (n + 1) * TPK)
                        else:
                            pe.wait_ge(S["rest_done"], n * 4 + k - 1)
                        for c in range(CD):
                            mm = pe.matmul(PO[k % 2][:], wqkv[:, c, k * P:(k + 1) * P], x2T[:, i, c, :],
                                           start=(c == 0), stop=(c == CD - 1))
                        mm.then_inc(S["qk_ready"], 1)
                    for t in range(TPK):
                        if t < 2:
                            pe.wait_ge(S["rest_done"], n * 4 + t + 3)
                        else:
                            pe.wait_ge(S["v_copied"], n * TPK + t - 1)
                        for c in range(CD):
                            mm = pe.matmul(PO[t % 2][:, 0:DIM], x2T[:, i, c, t * P:(t + 1) * P],
                                           wqkv[:, c, 2 * DIM:3 * DIM], start=(c == 0), stop=(c == CD - 1))
                        mm.then_inc(S["v_ready"], 1)
                if now := lagged(b, h, 1):
                    n, i, new = now
                    pe.wait_ge(S["hidden"], (n + 1) * HC)
                    for t in range(TPK):
                        if t < 2:
                            if lagged(b, h, 2):
                                pe.wait_ge(S["v_copied"], (n - 1) * TPK + t + 3)
                            elif lagged(b, h, 0):
                                pe.wait_ge(S["summed1"], (n + 2) * TPK)
                        else:
                            pe.wait_ge(S["summed2"], n * TPK + t - 1)
                        for k in range(HC):
                            mm = pe.matmul(PO[t % 2][:, 0:DIM], hT[:, i, k, t * P:(t + 1) * P], wdown[:, k, :],
                                           start=(k == 0), stop=(k == HC - 1))
                        mm.then_inc(S["downed"], 1)
                if now := lagged(b, h, 0):
                    n, i, new = now
                    pe.wait_ge(S["x1_done"], (n + 1) * TPK)
                    turn(x1[:, i], S["x1_turned"])

            block_pipeline(pe, step, LAG)

        @block.scalar
        def _(act):
            for i in range(2):
                act.sem_inc(parts_out[i], 16)
                act.sem_inc(v_out[i], 16)
            act.wait_ge(prep, PREP)

            def deviation(which, i, n, count, done):
                act.wait_ge(S[count], (n + 1) * TPK)
                act.activation(std[:, which], moments[:, which, :, 1], ACT.Sqrt, bias=eps[:, 0:1]).then_inc(S[done], 1)

            def step(b, h):
                if now := lagged(b, h, 1):
                    n, i, new = now
                    for k in range(HC):
                        act.wait_ge(S["gated"], n * HC + k + 1)
                        if not (new and i == 0 and k < 2):
                            act.wait_ge(S["hidden"], n * HC + k - 1)
                        act.activation(gate[:, k % 2], PG[k % 2][:], ACT.Silu).then_inc(S["silu"], 1)
                if now := lagged(b, h, 2):
                    n, i, new = now
                    for c in range(CD):
                        act.wait_ge(S["x2_turned"], n * CD + c + 1)
                        act.activation(x2T[:, i, c], TR[c][:], ACT.Copy).then_inc(S["x2_copied"], 1)
                if now := lagged(b, h, 0):
                    n, i, new = now
                    for c in range(CD):
                        act.wait_ge(S["att2_turned"], n * CD + c + 1)
                        act.activation(att2T[:, i, c], TR[c][:], ACT.Copy).then_inc(S["att2_copied"], 1)
                if now := lagged(b, h, 2):
                    n, i, new = now
                    act.wait_ge(parts_out[i], stored(b, h, 2))
                    act.wait_ge(v_out[i], stored(b, h, 2))
                    for k in range(4):
                        act.wait_ge(S["qk_ready"], n * 4 + k + 1)
                        act.activation(parts[:, i, 0, k], PO[k % 2][:], ACT.Copy).then_inc(S["hi_done"], 1)
                        act.wait_ge(S["rest_done"], n * 4 + k + 1)
                        act.activation(parts[:, i, 1, k], rest[:, k % 2], ACT.Copy).then_inc(S["mid_done"], 1)
                    for t in range(TPK):
                        act.wait_ge(S["v_ready"], n * TPK + t + 1)
                        act.activation(vaug[:, i, t, :, 0:D1], PO[t % 2][:, 0:DIM].rearrange("p (h c) -> p h c", h=H1),
                                       ACT.Copy).then_inc(S["v_copied"], 1)
                if now := lagged(b, h, 0):
                    n, i, new = now
                    deviation(0, i, n, "aggr1", "std1")
                    for c in range(CD):
                        act.wait_ge(S["x1_turned"], n * CD + c + 1)
                        act.activation(x1T[:, i, c], TR[c][:], ACT.Copy).then_inc(S["x1_copied"], 1)
                if now := lagged(b, h, 1):
                    n, i, new = now
                    deviation(1, i, n, "aggr2", "std2")
                if now := lagged(b, h, 2):
                    n, i, new = now
                    tok = bass.ds(n * BLK if isinstance(b, int) else act.snap(n * BLK), BLK)
                    act.wait_ge(S["v_copied"], (n + 1) * TPK)
                    act.dma_start(d["v1"][tok, :].rearrange("(t p) c -> p t c", p=P),
                                  vaug[:, i].rearrange("p t h c -> p t (h c)")).then_inc(v_out[i], 16)
                    act.wait_ge(S["lo_done"], (n + 1) * 4 + 2)
                    act.dma_start(d["qk1"][:, :, tok].rearrange("a p n -> p a n"),
                                  parts[:, i].rearrange("p s k n -> p (s k) n")).then_inc(parts_out[i], 16)

            block_pipeline(act, step, LAG)

        @block.vector
        def _(dve):
            for i in range(2):
                dve.sem_inc(x2_out[i], 16)
            dve.memset(eps[:], LN_EPS).then_inc(prep, 1)
            for i in range(2):
                last = dve.memset(vaug[:, i], 0.0)
            last.then_inc(vset, 1)
            dve.wait_ge(vset, 1)
            for i in range(2):
                last = dve.memset(vaug[:, i, :, :, D1:D1 + 1], 1.0)
            last.then_inc(prep, 1)
            dve.wait_ge(w_in, 16 * 7)
            for i, w in enumerate((wgate, wup, wdown)):
                dve.tensor_scalar(w[:].rearrange("p c n -> p (c n)"), ints[:, i], INT8_SCALE, None, ALU.mult).then_inc(prep, 1)
            dirs = const[:, C_DIRS:C_DIRS + 24].rearrange("p (h c) -> p h c", c=3)
            wq = [wqkv[:, c, 0:DIM].rearrange("p (h c) -> p h c", c=D1) for c in range(CD)]
            for c in range(CD):
                last = dve.tensor_tensor(geo[:, c], wq[c][:, :, 0:3], dirs, ALU.mult)
            last.then_inc(prep, 1)
            dve.wait_ge(prep, 6)
            dve.tensor_reduce(geo1[:], geo[:], AX.X, ALU.add).then_inc(prep, 1)
            for c in range(CD):
                last = dve.tensor_scalar(wqkv[:, c, 0:DIM], wqkv[:, c, 0:DIM], float(1.0 / np.sqrt(D1)), None, ALU.mult)
            dve.wait_ge(prep, 7)
            dve.tensor_tensor(geo1[:], geo1[:], hscale[:].unsqueeze(1).to_broadcast([P, CD, H1]), ALU.mult).then_inc(prep, 1)
            dve.wait_ge(prep, 8)
            for c in range(CD):
                last = dve.tensor_tensor(geo[:, c], dirs, geo1[:, c].unsqueeze(2).to_broadcast([P, H1, 3]), ALU.mult)
            last.then_inc(prep, 1)
            dve.wait_ge(prep, 9)
            for c in range(CD):
                last = dve.tensor_tensor(wq[c][:, :, 0:3], wq[c][:, :, 0:3], geo[:, c], ALU.add)
            last.then_inc(prep, 1)
            dve.wait_ge(prep, PREP)

            def moments_of(which, src, n, count, done):
                for t in range(TPK):
                    dve.wait_ge(S[count], n * TPK + t + 1)
                    dve.bn_stats(stats[:, which, t], src[:, t]).then_inc(S["stat" + done], 1)
                dve.wait_ge(S["stat" + done], (n + 1) * TPK)
                dve.sem_inc(seen, 1)
                for t in range(TPK):
                    dve.bn_aggr(moments[:, which, t], stats[:, which, t]).then_inc(S["aggr" + done], 1)

            def norm(which, src, out, n, done, x_done):
                dve.wait_ge(S["std" + done], n + 1)
                dve.reciprocal(rstd[:, which], std[:, which]).then_inc(S["rstd" + done], 1)
                dve.wait_ge(S["rstd" + done], n + 1)
                for t in range(TPK):
                    dve.tensor_scalar(out[:, t], src[:, t], moments[:, which, t, 0:1], rstd[:, which, t:t + 1],
                                      ALU.subtract, ALU.mult).then_inc(S[x_done], 1)

            def step(b, h):
                if now := lagged(b, h, 0):
                    n, i, new = now
                    for t in range(TPK):
                        dve.wait_ge(S["att_turned"], n * TPK + t + 1)
                        heads = TR[t % 2][:].rearrange("p (h c) -> p h c", h=H0)
                        dve.reciprocal(rec[:, t % 2], heads[:, :, D0]).then_inc(S["rec_done"], 1)
                        dve.wait_ge(S["rec_done"], n * TPK + t + 1)
                        dve.tensor_tensor(att[:, i, t].rearrange("p (h c) -> p h c", h=H0), heads[:, :, 0:D0],
                                          rec[:, t % 2].unsqueeze(2).to_broadcast([P, H0, D0]), ALU.mult)\
                           .then_inc(S["normed"], 1)
                if now := lagged(b, h, 1):
                    n, i, new = now
                    for k in range(HC):
                        dve.wait_ge(S["silu"], n * HC + k + 1)
                        dve.wait_ge(S["upped"], n * HC + k + 1)
                        dve.tensor_tensor(hT[:, i, k], gate[:, k % 2], PU[k % 2][:], ALU.mult).then_inc(S["hidden"], 1)
                if now := lagged(b, h, 0):
                    n, i, new = now
                    dve.wait_ge(S["biased"], n + 1)
                    for t in range(TPK):
                        dve.wait_ge(S["projected"], n * TPK + t + 1)
                        dve.tensor_tensor(s1[:, i, t], xin[:, i, t], PO[t % 2][:, 0:DIM], ALU.add).then_inc(S["summed1"], 1)
                    moments_of(0, s1[:, i], n, "summed1", "1")
                if now := lagged(b, h, 2):
                    n, i, new = now
                    for k in range(4):
                        dve.wait_ge(S["hi_done"], n * 4 + k + 1)
                        dve.wait_ge(S["lo_done"], n * 4 + k + 1)
                        dve.tensor_tensor(rest[:, k % 2], PO[k % 2][:], parts[:, i, 0, k], ALU.subtract)\
                           .then_inc(S["rest_done"], 1)
                if now := lagged(b, h, 0):
                    n, i, new = now
                    norm(0, s1[:, i], x1[:, i], n, "1", "x1_done")
                if now := lagged(b, h, 1):
                    n, i, new = now
                    for t in range(TPK):
                        dve.wait_ge(S["downed"], n * TPK + t + 1)
                        dve.tensor_tensor(s2[:, t], x1[:, i, t], PO[t % 2][:, 0:DIM], ALU.add).then_inc(S["summed2"], 1)
                    moments_of(1, s2[:], n, "summed2", "2")
                    dve.wait_ge(x2_out[i], stored(b, h, 1))
                    norm(1, s2[:], x2[:, i], n, "2", "x2_done")

            block_pipeline(dve, step, LAG)


def stored(b, h, lag):
    return b * 16 + 16 if h - lag >= 0 else b * 16

def phase_attention1(nc, d, keep):
    CHUNK = len(COMBOS) // 2
    K = CHUNK * D1
    KM = K + PARTS
    BUFS = HG1
    RING = 8
    MAXES = [(j, qt, kh) for j in range(G1) for qt in range(TPB) for kh in range(qt // TPK + 1)]
    UNITS = [(half, kt, j) for half in range(HPS) for kt in range((half + 1) * TPK) for j in range(G1)]
    PAIRS = len(UNITS) // G1
    NM, NU = len(MAXES), len(UNITS)
    SLOTS_FOR_MAX = 20
    SBANKS = 3
    with ExitStack() as ctx:
        a = Alloc(nc, ctx, "d")
        const = keep["const"]
        qst = [a.sb(f"qst{i}", [P, 2, G1, SEQ], BF16) for i in range(BUFS)]
        kst = [a.sb(f"kst{i}", [P, 2, G1, SEQ], BF16) for i in range(BUFS)]
        vst = [a.sb(f"vst{i}", [P, TPB, G1, VS1]) for i in range(BUFS)]
        probs = a.sb("probs", [P, RING, BLK])
        outT = a.sb("outT", [P, HPS, BLK])
        mx = a.sb("mx", [P, G1, TPB, 2])
        m = a.sb("m", [P, G1, TPB])
        mrest = a.sb("mrest", [P, G1, TPB])
        mparts = a.sb("mparts", [P, TPB, 4, 32], BF16)
        fixed = a.sb("fixed", [P, 3, P], BF16)
        identb, mask_q, mask_k = (fixed[:, i] for i in range(3))
        PM = [a.ps(f"PM{i}", [P, BLK]) for i in range(2)]
        PS = [a.ps(f"PS{i}", [P, BLK]) for i in range(SBANKS)]
        PO = [a.ps(f"PO{i}", [P, BLK]) for i in range(HPS)]
        PT = a.ps("PT", [P, TPB, P], BF16)

        setup = a.sem("setup")
        q_in = [a.sem(f"q_in{i}") for i in range(BUFS)]
        v_in = [a.sem(f"v_in{i}") for i in range(BUFS)]
        max_scores, max_taken = a.sem("max_scores"), a.sem("max_taken")
        m_step, m_parts, m_turned, m_rows = (a.sem(n) for n in ("m_step", "m_parts", "m_turned", "m_rows"))
        scores, exped, pv_done, out_copied = (a.sem(n) for n in ("scores", "exped", "pv_done", "out_copied"))
        out_stored = [a.sem(f"out_stored{i}") for i in range(HPS)]
        block = ctx.enter_context(nc.Block())

        def over_groups(eng, body):
            with eng.Fori(0, BATCH - 1) as b:
                for hg in range(HG1):
                    body(b, hg, True)
            for hg in range(HG1):
                body(BATCH - 1, hg, hg < HG1 - 1)

        def queries(half, kt):
            q0 = max(half * BLK, kt * P)
            return q0, (half + 1) * BLK - q0

        def keys(qt, kh):
            return min(BLK, (qt + 1) * P - kh * BLK)

        @block.sync
        def _(sp):
            def load(b, hg, again):
                if again:
                    sp.wait_ge(pv_done, ((b - 1) * HG1 + hg + 1) * PAIRS + RING // G1)
                tok = bass.ds(b * SEQ, SEQ)
                for stack, side, first_blk in ((qst, 0, 0), (kst, 1, 2)):
                    for s, combo in enumerate(COMBOS):
                        rows = d["qk1"][combo[side] * 4 + first_blk + hg // 2, (hg % 2) * 64:(hg % 2) * 64 + 64, tok]
                        r = s % CHUNK * D1
                        sp.dma_start(stack[hg][r:r + D1, s // CHUNK], rows.rearrange("(j p) n -> p j n", p=D1))\
                          .then_inc(q_in[hg], 16)
                src = d["v1"][tok, hg * G1 * VS1:(hg + 1) * G1 * VS1].rearrange("(t p) c -> p t c", p=P)
                sp.dma_start(vst[hg][:].rearrange("p t j c -> p t (j c)"), src).then_inc(v_in[hg], 16)

            for hg in range(HG1):
                load(0, hg, False)
            with sp.Fori(1, BATCH) as b:
                for hg in range(HG1):
                    load(b, hg, True)

        @block.tensor
        def _(pe):
            pe.sem_inc(pv_done, RING // G1)
            pe.wait_ge(setup, 2)

            def max_product(g, nxt, u):
                j, qt, kh = MAXES[u]
                w = keys(qt, kh)
                diagonal = kh == qt // TPK
                pe.wait_ge(max_taken, g * NM + u + 1)
                for c in range(2):
                    mm = pe.matmul(PM[u % 2][:, 0:w], qst[nxt][0:K, c, j, qt * P:(qt + 1) * P],
                                   kst[nxt][0:K, c, j, kh * BLK:kh * BLK + w], start=(c == 0),
                                   stop=(c == 1 and not diagonal))
                if diagonal:
                    mm = pe.matmul(PM[u % 2][:, w - P:w], identb, mask_q, start=False, stop=True)
                mm.then_inc(max_scores, 1)

            def turn_max(g):
                pe.wait_ge(m_parts, g + 1)
                for qt in range(TPB):
                    mm = pe.transpose(PT[:, qt], mparts[:, qt].rearrange("p j c -> p (j c)"), identb)
                mm.then_inc(m_turned, 1)

            def values(g, hg, n):
                half, kt, _ = UNITS[n * G1]
                q0, w = queries(half, kt)
                pe.wait_ge(exped, g * NU + (n + 1) * G1 + SBANKS)
                if kt == 0:
                    pe.wait_ge(out_copied, g * HPS + half + 1)
                for j in range(G1):
                    mm = pe.matmul(PO[half][j * VS1:(j + 1) * VS1, q0 - half * BLK:q0 - half * BLK + w],
                                   vst[hg][:, kt, j, :], probs[:, (n * G1 + j) % RING, 0:w], start=(kt == 0),
                                   stop=(kt == (half + 1) * TPK - 1), tile_position=(0, j * VS1))
                mm.then_inc(pv_done, 1)

            def group(b, hg, follows):
                g = b * HG1 + hg
                nxt = (hg + 1) % BUFS
                taken = 0
                pe.wait_ge(v_in[hg], b * 16 + 16)
                if follows:
                    turns = 16 * 2 * len(COMBOS)
                    pe.wait_ge(q_in[nxt], (b + (hg + 1) // BUFS) * turns + turns)
                pe.wait_ge(m_rows, (g + 1) * G1)
                for s, (half, kt, j) in enumerate(UNITS):
                    q0, w = queries(half, kt)
                    diagonal = q0 == kt * P
                    pe.wait_ge(exped, g * NU + s + 1)
                    out = PS[s % SBANKS]
                    for c in range(2):
                        rows = KM if c == 0 else K
                        mm = pe.matmul(out[:, 0:w], kst[hg][0:rows, c, j, kt * P:(kt + 1) * P],
                                       qst[hg][0:rows, c, j, q0:q0 + w], start=(c == 0), stop=(c == 1 and not diagonal))
                    if diagonal:
                        mm = pe.matmul(out[:, 0:P], identb, mask_k, start=False, stop=True)
                    mm.then_inc(scores, 1)
                    if follows:
                        upto = min(NM, NM * (s + 1) // SLOTS_FOR_MAX)
                        for u in range(taken, upto):
                            max_product(g + 1, nxt, u)
                        taken = upto
                        if s == NU - 1:
                            turn_max(g + 1)
                    if s % G1 == 1 and s >= 2 * G1:
                        values(g, hg, s // G1 - 2)
                for n in (PAIRS - 2, PAIRS - 1):
                    values(g, hg, n)

            pe.wait_ge(q_in[0], 16 * 2 * len(COMBOS))
            for u in range(NM):
                max_product(0, 0, u)
            turn_max(0)
            over_groups(pe, group)

        @block.scalar
        def _(act):
            act.sem_inc(exped, SBANKS)
            act.sem_inc(out_copied, HPS)
            for half in range(HPS):
                act.sem_inc(out_stored[half], 16)
            act.wait_ge(setup, 2)

            def copy_out(b, g, hg, half):
                pairs = sum(1 for u in UNITS if u[0] <= half) // G1
                act.wait_ge(pv_done, g * PAIRS + pairs + RING // G1)
                act.wait_ge(out_stored[half], g * 16 + 16)
                act.activation(outT[:, half], PO[half][:], ACT.Copy).then_inc(out_copied, 1)
                act.wait_ge(out_copied, g * HPS + half + 1 + HPS)
                act.dma_start(d["att1"][hg, :, bass.ds(b * SEQ + half * BLK, BLK)], outT[:, half])\
                   .then_inc(out_stored[half], 16)

            def group(b, hg, follows):
                g = b * HG1 + hg
                for s, (half, kt, j) in enumerate(UNITS):
                    w = queries(half, kt)[1]
                    act.wait_ge(scores, g * NU + s + 1)
                    if j == 0:
                        act.wait_ge(pv_done, g * PAIRS + s // G1 + 1)
                    act.activation(probs[:, s % RING, 0:w], PS[s % SBANKS][:, 0:w], ACT.Exp).then_inc(exped, 1)
                    if s == TPK * G1 + 6:
                        copy_out(b, g, hg, 0)
                copy_out(b, g, hg, 1)

            over_groups(act, group)
            for half in range(HPS):
                act.wait_ge(out_stored[half], 16 * (BATCH * HG1 + 1))

        @block.vector
        def _(dve):
            dve.sem_inc(max_taken, 2)
            for i in range(BUFS):
                dve.memset(kst[i][K:KM, 0], 1.0)
            for i, at in enumerate((C_IDENT, C_MASK_Q, C_MASK_K)):
                dve.tensor_copy(fixed[:, i], const[:, at:at + P])
            dve.memset(mx[:], -3.0e38).then_inc(setup, 1)
            dve.memset(mparts[:], 0.0).then_inc(setup, 1)
            dve.wait_ge(setup, 2)

            def maxima(g, nxt):
                for u, (j, qt, kh) in enumerate(MAXES):
                    dve.wait_ge(max_scores, g * NM + u + 1)
                    dve.tensor_reduce(mx[:, j, qt, kh:kh + 1], PM[u % 2][:, 0:keys(qt, kh)], AX.X, ALU.max)\
                       .then_inc(max_taken, 1)
                dve.wait_ge(max_taken, g * NM + NM + 2)
                dve.tensor_tensor(m[:], mx[:, :, :, 0], mx[:, :, :, 1], ALU.max).then_inc(m_step, 1)
                part = [mparts[:, :, 0:G1, i].rearrange("p t j -> p j t") for i in range(PARTS)]
                dve.wait_ge(m_step, g * 4 + 1)
                dve.tensor_scalar(part[0], m[:], -1.0, None, ALU.mult).then_inc(m_step, 1)
                dve.wait_ge(m_step, g * 4 + 2)
                dve.scalar_tensor_tensor(out=mrest[:], in0=m[:], scalar=-1.0, in1=part[0], op0=ALU.mult,
                                         op1=ALU.subtract).then_inc(m_step, 1)
                dve.wait_ge(m_step, g * 4 + 3)
                dve.tensor_copy(part[1], mrest[:]).then_inc(m_step, 1)
                dve.wait_ge(m_step, g * 4 + 4)
                dve.tensor_tensor(part[2], mrest[:], part[1], ALU.subtract).then_inc(m_parts, 1)
                dve.wait_ge(m_turned, g + 1)
                for j in range(G1):
                    dve.tensor_copy(qst[nxt][K:KM, 0, j, :], PT[32 * j:32 * j + PARTS].rearrange("p t n -> p (t n)"))\
                       .then_inc(m_rows, 1)

            def group(b, hg, follows):
                if follows:
                    maxima(b * HG1 + hg + 1, (hg + 1) % BUFS)

            maxima(0, 0)
            over_groups(dve, group)

E_COPY, E_MLP = 1, 4
MLPS = E - E_MLP
TOP_K = 2
SLOTS = E * CAP
NOWHERE = float(2 * SLOTS)


def phase_route(nc, d, keep):
    with ExitStack() as ctx:
        a = Alloc(nc, ctx, "e")
        const = keep["const"]
        ident = const[:, C_IDENT:C_IDENT + P]
        iota = const[:, C_IOTA:C_IOTA + E]
        wout = a.sb("wout", [P, CD, DIM])
        wr = a.sb("wr", [P, CD, E])
        br = a.sb("br", [P, E])
        nw = a.sb("nw", [P, DIM])
        before = a.sb("before", [P, P], BF16)
        ones = a.sb("ones", [P, P], BF16)
        eps = a.sb("eps", [P, 1])
        attT = a.sb("attT", [P, 2, HG1, BLK])
        x2 = a.sb("x2", [P, 2, TPK, DIM])
        rec = a.sb("rec", [P, 2, H1])
        att = a.sb("att", [P, 2, TPK, DIM])
        att2T = a.sb("att2T", [P, 2, CD, BLK])
        s3 = a.sb("s3", [P, 2, TPK, DIM])
        x3 = a.sb("x3", [P, 2, TPK, DIM])
        square = a.sb("square", [P, TPK, DIM])
        xn = a.sb("xn", [P, 2, TPK, DIM])
        xnT = a.sb("xnT", [P, 2, CD, BLK])
        stats = a.sb("stats", [P, TPK, 6])
        moments = a.sb("moments", [P, TPK, 2])
        std = a.sb("std", [P, TPK])
        rstd = a.sb("rstd", [P, TPK])
        meansq = a.sb("meansq", [P, TPK])
        rms = a.sb("rms", [P, TPK])
        rrms = a.sb("rrms", [P, TPK])
        logits = a.sb("logits", [P, TPK, E])
        top = a.sb("top", [P, TPK])
        below = a.sb("below", [P, TPK, E])
        expd = a.sb("expd", [P, TPK, E])
        total = a.sb("total", [P, TPK])
        rtotal = a.sb("rtotal", [P, TPK])
        prob = a.sb("prob", [P, TPK, E])
        best = a.sb("best", [P, TPK, 8])
        besti = a.sb("besti", [P, TPK, 8], U32)
        expert = a.sb("expert", [P, TPK, TOP_K])
        onehot = a.sb("onehot", [P, TPK, TOP_K, E])
        chosen = a.sb("chosen", [P, TPK, E], BF16)
        count = a.sb("count", [P, 2, TPK + 1, E], BF16)
        ranked = a.sb("ranked", [P, TPK, TOP_K, E])
        rank = a.sb("rank", [P, TPK, TOP_K])
        kept = a.sb("kept", [P, TPK, TOP_K])
        slot = a.sb("slot", [P, TPK, TOP_K])
        moves = a.sb("moves", [P, TPK, TOP_K])
        moves2 = a.sb("moves2", [P, TPK, TOP_K])
        target = a.sb("target", [P, TPK, TOP_K])
        weight = a.sb("weight", [P, TPK, TOP_K])
        wsum = a.sb("wsum", [P, TPK])
        wzero = a.sb("wzero", [P, TPK])
        rwsum = a.sb("rwsum", [P, TPK])
        to_slot = a.sb("to_slot", [P, 2, TPK, TOP_K], I32)
        from_slot = a.sb("from_slot", [P, 2, TPK, TOP_K], I32)
        coef = a.sb("coef", [P, 2, TPK, TOP_K])
        TR = [a.ps(f"TR{i}", [P, BLK]) for i in range(2)]
        PX = [a.ps(f"PX{i}", [P, BLK]) for i in range(2)]
        PL = a.ps("PL", [P, TPK, E])
        PR = a.ps("PR", [P, TPK, E])

        w_in, prep = a.sem("w_in"), a.sem("prep")
        seen, pool_seen = a.sem("seen"), a.sem("pool_seen")
        att_in = [a.sem(f"att_in{i}") for i in range(2)]
        x2_in = [a.sem(f"x2_in{i}") for i in range(2)]
        names = ("att_turned", "rec_done", "normed", "att2_turned", "att2_copied", "projected", "summed", "stat", "aggr",
                 "std_done", "rstd_done", "x3_done", "squared", "rms_done", "rrms_done", "xn_done", "xn_turned", "xn_copied",
                 "logits_ready", "step", "expd_done", "counted", "ranks_ready", "routed", "ranks_taken")
        S = {n: a.sem(n) for n in names}
        x3_out = [a.sem(f"x3_out{i}") for i in range(2)]
        route_out = [a.sem(f"route_out{i}") for i in range(2)]
        scattered = [a.sem(f"scattered{i}") for i in range(2)]
        PREP = 3
        LAG = 0
        block = ctx.enter_context(nc.Block())

        @block.sync
        def _(sp):
            sp.dma_start(wout[:], d["L1_attn_w_out"].rearrange("(c p) n -> p c n", p=P)).then_inc(w_in, 16)
            sp.dma_start(wr[:], d["L1_ffn_router_weightT"].rearrange("(c p) n -> p c n", p=P)).then_inc(w_in, 16)
            for out, name in ((br, "router_bias"), (nw, "norm_weight")):
                sp.dma_start(out[:], d["L1_ffn_" + name].rearrange("(o n) -> o n", o=1).to_broadcast(list(out.shape)))\
                  .then_inc(w_in, 16)

            def step(b, h):
                n, i, new = lagged(b, h, 0)
                tok = bass.ds(n * BLK if isinstance(b, int) else sp.snap(n * BLK), BLK)
                if not new:
                    sp.wait_ge(S["att_turned"], (n - 1) * TPK)
                    sp.wait_ge(S["summed"], (n - 1) * TPK)
                sp.dma_start(attT[:, i], d["att1"][:, :, tok].rearrange("g p n -> p g n")).then_inc(att_in[i], 16)
                sp.dma_start(x2[:, i], d["x2"][tok, :].rearrange("(t p) c -> p t c", p=P)).then_inc(x2_in[i], 16)

            block_pipeline(sp, step, LAG)

        @block.tensor
        def _(pe):
            pe.wait_ge(w_in, 16 * 4)
            pe.wait_ge(prep, PREP)

            def turn(src, count):
                for c in range(CD):
                    for t in range(TPK):
                        mm = pe.transpose(TR[c][:, t * P:(t + 1) * P], src[:, t, c * P:(c + 1) * P], ident)
                    mm.then_inc(count, 1)

            def step(b, h):
                n, i, new = lagged(b, h, 0)
                pe.wait_ge(att_in[i], b * 16 + 16)
                for t in range(TPK):
                    if t < 2 and not (first(b) and h == 0):
                        pe.wait_ge(S["xn_copied"], n * CD)
                    if t >= 2:
                        pe.wait_ge(S["normed"], n * TPK + t - 1)
                    for g in range(HG1):
                        mm = pe.transpose(TR[t % 2][:, g * P:(g + 1) * P], attT[:, i, g, t * P:(t + 1) * P], ident)
                    mm.then_inc(S["att_turned"], 1)
                pe.wait_ge(S["normed"], (n + 1) * TPK)
                turn(att[:, i], S["att2_turned"])
                pe.wait_ge(S["att2_copied"], (n + 1) * CD)
                for t in range(TPK):
                    if t >= 2 or not (first(b) and h == 0):
                        pe.wait_ge(S["summed"], n * TPK + t - 1)
                    for c in range(CD):
                        mm = pe.matmul(PX[t % 2][:, 0:DIM], att2T[:, i, c, t * P:(t + 1) * P], wout[:, c, :],
                                       start=(c == 0), stop=(c == CD - 1))
                    mm.then_inc(S["projected"], 1)
                pe.wait_ge(S["xn_done"], (n + 1) * TPK)
                turn(xn[:, i], S["xn_turned"])
                pe.wait_ge(S["xn_copied"], (n + 1) * CD)
                for t in range(TPK):
                    for c in range(CD):
                        mm = pe.matmul(PL[:, t], xnT[:, i, c, t * P:(t + 1) * P], wr[:, c, :], start=(c == 0),
                                       stop=(c == CD - 1))
                mm.then_inc(S["logits_ready"], 1)
                pe.wait_ge(S["counted"], n + 1)
                for t in range(TPK):
                    pe.matmul(PR[:, t], before[:], chosen[:, t], start=True, stop=False)
                    mm = pe.matmul(PR[:, t], ones[:], count[:, i, t], start=False, stop=True)
                mm.then_inc(S["ranks_ready"], 1)

            block_pipeline(pe, step, LAG)

        @block.scalar
        def _(act):
            act.wait_ge(prep, PREP)

            def step(b, h):
                n, i, new = lagged(b, h, 0)
                for c in range(CD):
                    act.wait_ge(S["att2_turned"], n * CD + c + 1)
                    act.activation(att2T[:, i, c], TR[c][:], ACT.Copy).then_inc(S["att2_copied"], 1)
                act.wait_ge(S["aggr"], (n + 1) * TPK)
                act.activation(std[:], moments[:, :, 1], ACT.Sqrt, bias=eps[:, 0:1]).then_inc(S["std_done"], 1)
                for t in range(TPK):
                    act.wait_ge(S["x3_done"], n * TPK + t + 1)
                    act.activation(square[:, t], x3[:, i, t], ACT.Square, accum_out=meansq[:, t:t + 1])\
                       .then_inc(S["squared"], 1)
                act.wait_ge(S["squared"], (n + 1) * TPK)
                act.activation(rms[:], meansq[:], ACT.Sqrt, bias=eps[:, 0:1], scale=1.0 / DIM).then_inc(S["rms_done"], 1)
                for c in range(CD):
                    act.wait_ge(S["xn_turned"], n * CD + c + 1)
                    act.activation(xnT[:, i, c], TR[c][:], ACT.Copy).then_inc(S["xn_copied"], 1)
                act.wait_ge(S["step"], n * STEPS + 3)
                act.activation(expd[:], below[:], ACT.Exp).then_inc(S["expd_done"], 1)

            STEPS = ROUTE_STEPS
            block_pipeline(act, step, LAG)

        @block.vector
        def _(dve):
            dve.memset(eps[:], LN_EPS).then_inc(prep, 1)
            dve.memset(ones[:], 1.0)
            dve.memset(count[:], 0.0).then_inc(prep, 1)
            dve.tensor_copy(before[:], const[:, C_BEFORE:C_BEFORE + P]).then_inc(prep, 1)
            dve.wait_ge(w_in, 16 * 4)
            dve.wait_ge(prep, PREP)

            def step(b, h):
                n, i, new = lagged(b, h, 0)
                done = 0

                def chain(instruction):
                    nonlocal done
                    done += 1
                    instruction.then_inc(S["step"], 1)
                    dve.wait_ge(S["step"], n * ROUTE_STEPS + done)

                for t in range(TPK):
                    dve.wait_ge(S["att_turned"], n * TPK + t + 1)
                    heads = TR[t % 2][:].rearrange("p (h c) -> p h c", h=H1)
                    dve.reciprocal(rec[:, t % 2], heads[:, :, D1]).then_inc(S["rec_done"], 1)
                    dve.wait_ge(S["rec_done"], n * TPK + t + 1)
                    dve.tensor_tensor(att[:, i, t].rearrange("p (h c) -> p h c", h=H1), heads[:, :, 0:D1],
                                      rec[:, t % 2].unsqueeze(2).to_broadcast([P, H1, D1]), ALU.mult)\
                       .then_inc(S["normed"], 1)
                dve.wait_ge(x2_in[i], b * 16 + 16)
                for t in range(TPK):
                    dve.wait_ge(S["projected"], n * TPK + t + 1)
                    dve.tensor_tensor(s3[:, i, t], x2[:, i, t], PX[t % 2][:, 0:DIM], ALU.add).then_inc(S["summed"], 1)
                for t in range(TPK):
                    dve.wait_ge(S["summed"], n * TPK + t + 1)
                    dve.bn_stats(stats[:, t], s3[:, i, t]).then_inc(S["stat"], 1)
                dve.wait_ge(S["stat"], (n + 1) * TPK)
                dve.sem_inc(seen, 1)
                for t in range(TPK):
                    dve.bn_aggr(moments[:, t], stats[:, t]).then_inc(S["aggr"], 1)
                dve.wait_ge(S["std_done"], n + 1)
                dve.reciprocal(rstd[:], std[:]).then_inc(S["rstd_done"], 1)
                dve.wait_ge(S["rstd_done"], n + 1)
                if not new:
                    dve.wait_ge(x3_out[i], b * 16)
                for t in range(TPK):
                    dve.tensor_scalar(x3[:, i, t], s3[:, i, t], moments[:, t, 0:1], rstd[:, t:t + 1], ALU.subtract,
                                      ALU.mult).then_inc(S["x3_done"], 1)
                dve.wait_ge(S["rms_done"], n + 1)
                dve.reciprocal(rrms[:], rms[:]).then_inc(S["rrms_done"], 1)
                dve.wait_ge(S["rrms_done"], n + 1)
                if not new:
                    dve.wait_ge(scattered[i], b * 16 * TPK * TOP_K)
                for t in range(TPK):
                    dve.scalar_tensor_tensor(out=xn[:, i, t], in0=x3[:, i, t], scalar=rrms[:, t:t + 1], in1=nw[:],
                                             op0=ALU.mult, op1=ALU.mult).then_inc(S["xn_done"], 1)
                dve.wait_ge(S["logits_ready"], n + 1)
                chain(dve.tensor_tensor(logits[:], PL[:], br[:].unsqueeze(1).to_broadcast([P, TPK, E]), ALU.add))
                chain(dve.tensor_reduce(top[:], logits[:], AX.X, ALU.max))
                chain(dve.tensor_tensor(below[:], logits[:], top[:].unsqueeze(2).to_broadcast([P, TPK, E]), ALU.subtract))
                dve.wait_ge(S["expd_done"], n + 1)
                chain(dve.tensor_reduce(total[:], expd[:], AX.X, ALU.add))
                chain(dve.reciprocal(rtotal[:], total[:]))
                chain(dve.tensor_tensor(prob[:], expd[:], rtotal[:].unsqueeze(2).to_broadcast([P, TPK, E]), ALU.mult))
                dve.sem_inc(seen, 1)
                for t in range(TPK):
                    last = dve.max(best[:, t], prob[:, t])
                chain(last)
                dve.sem_inc(seen, 1)
                for t in range(TPK):
                    last = dve.max_index(besti[:, t], best[:, t], prob[:, t])
                chain(last)
                chain(dve.tensor_copy(expert[:], besti[:, :, 0:TOP_K]))
                flat = [P, TPK * TOP_K, E]
                oh = onehot[:].rearrange("p t k e -> p (t k) e")
                chain(dve.tensor_tensor(oh, iota.unsqueeze(1).to_broadcast(flat),
                                        expert[:].rearrange("p t k -> p (t k)").unsqueeze(2).to_broadcast(flat), ALU.is_equal))
                chain(dve.tensor_tensor(chosen[:], onehot[:, :, 0], onehot[:, :, 1], ALU.add))
                for t in range(TPK):
                    chain(dve.tensor_tensor(count[:, i, t + 1], count[:, i, t], chosen[:, t], ALU.add))
                dve.tensor_copy(count[:, 1 - i, 0], count[:, i, TPK]).then_inc(S["counted"], 1)
                chain(dve.tensor_scalar(moves[:], expert[:], float(E_COPY), None, ALU.is_equal))
                chain(dve.tensor_scalar(moves2[:], expert[:], float(E_MLP), None, ALU.is_ge))
                chain(dve.tensor_tensor(moves[:], moves[:], moves2[:], ALU.add))
                dve.wait_ge(S["ranks_ready"], n + 1)
                for k in range(TOP_K):
                    last = dve.tensor_tensor(ranked[:, :, k], onehot[:, :, k], PR[:], ALU.mult)
                chain(last)
                chain(dve.tensor_reduce(rank[:], ranked[:], AX.X, ALU.add))
                chain(dve.tensor_scalar(kept[:], rank[:], float(CAP), None, ALU.is_lt))
                chain(dve.tensor_scalar(slot[:], rank[:], float(CAP - 1), None, ALU.min))
                chain(dve.scalar_tensor_tensor(out=slot[:], in0=expert[:], scalar=float(CAP), in1=slot[:], op0=ALU.mult,
                                               op1=ALU.add))
                chain(dve.tensor_tensor(moves[:], moves[:], kept[:], ALU.mult))
                chain(dve.tensor_scalar(target[:], moves[:], -NOWHERE, NOWHERE, ALU.mult, ALU.add))
                if not new:
                    dve.wait_ge(route_out[i], b * 2 * 16)
                chain(dve.tensor_tensor(to_slot[:, i], target[:], slot[:], ALU.add))
                chain(dve.tensor_copy(from_slot[:, i], slot[:]))
                chain(dve.tensor_tensor(weight[:], best[:, :, 0:TOP_K], kept[:], ALU.mult))
                chain(dve.tensor_tensor(wsum[:], weight[:, :, 0], weight[:, :, 1], ALU.add))
                chain(dve.tensor_scalar(wzero[:], wsum[:], 0.0, None, ALU.is_le))
                chain(dve.tensor_tensor(wsum[:], wsum[:], wzero[:], ALU.add))
                chain(dve.reciprocal(rwsum[:], wsum[:]))
                dve.tensor_tensor(coef[:, i], weight[:], rwsum[:].unsqueeze(2).to_broadcast([P, TPK, TOP_K]), ALU.mult)\
                   .then_inc(S["routed"], 1)
                assert done == ROUTE_STEPS, done

            block_pipeline(dve, step, LAG)

        @block.gpsimd
        def _(pool):
            def step(b, h):
                n, i, new = lagged(b, h, 0)
                tok = bass.ds(n * BLK if isinstance(b, int) else pool.snap(n * BLK), BLK)
                at = bass.ds(n * TPK * TOP_K if isinstance(b, int) else pool.snap(n * TPK * TOP_K), TPK * TOP_K)
                pool.wait_ge(S["x3_done"], (n + 1) * TPK)
                pool.sem_inc(pool_seen, 1)
                pool.dma_start(d["x3"][tok, :].rearrange("(t p) c -> p t c", p=P), x3[:, i]).then_inc(x3_out[i], 16)
                pool.wait_ge(S["routed"], n + 1)
                pool.sem_inc(pool_seen, 1)
                for t in range(TPK):
                    for k in range(TOP_K):
                        pool.indirect_dma_start(out=d["slots"], out_offset=bass.IndirectOffsetOnAxis(
                            ap=to_slot[:, i, t, k:k + 1].bitcast(U32), axis=0), in_=xn[:, i, t], in_offset=None,
                            bounds_check=SLOTS - 1, oob_is_err=False).then_inc(scattered[i], 16)
                pool.dma_start(d["from_slot"][:, at], from_slot[:, i].rearrange("p t k -> p (t k)")).then_inc(route_out[i], 16)
                pool.dma_start(d["coef"][:, at], coef[:, i].rearrange("p t k -> p (t k)")).then_inc(route_out[i], 16)

            block_pipeline(pool, step, LAG)
            for i in range(2):
                pool.wait_ge(x3_out[i], 16 * BATCH)
                pool.wait_ge(route_out[i], 2 * 16 * BATCH)
                pool.wait_ge(scattered[i], 16 * TPK * TOP_K * BATCH)


ROUTE_STEPS = 32
FFN = 1024
FC = FFN // P


def phase_experts(nc, d, keep):
    ST = CAP // P
    with ExitStack() as ctx:
        a = Alloc(nc, ctx, "f")
        ident = keep["const"][:, C_IDENT:C_IDENT + P]
        w1 = a.sb("w1", [P, 2, CD, FFN])
        w2 = a.sb("w2", [P, 2, FC, DIM])
        b1 = a.sb("b1", [P, 2, FC])
        b2 = a.sb("b2", [P, 2, DIM])
        x = a.sb("x", [P, 2, ST, DIM])
        xT = a.sb("xT", [P, 2, CD, CAP])
        hT = a.sb("hT", [P, 2, FC, CAP])
        y = a.sb("y", [P, 2, ST, DIM])
        TR = [a.ps(f"TR{i}", [P, CAP]) for i in range(CD)]
        PH = [a.ps(f"PH{i}", [P, CAP]) for i in range(3)]
        PY = [a.ps(f"PY{i}", [P, DIM]) for i in range(2)]
        load_in = [a.sem(f"load_in{i}") for i in range(2)]
        turned, copied, h_ready, h_done, y_ready, y_done = (
            a.sem(n) for n in ("turned", "copied", "h_ready", "h_done", "y_ready", "y_done"))
        y_out = [a.sem(f"y_out{i}") for i in range(2)]
        LOADS = 5
        block = ctx.enter_context(nc.Block())

        def over_experts(eng, body):
            for i in range(2):
                body(0, i)
            with eng.Fori(1, MLPS // 2) as e:
                for i in range(2):
                    body(e, i)

        @block.sync
        def _(sp):
            def load(s, i):
                n = s * 2 + i
                if not first(s):
                    sp.wait_ge(y_done, (n - 1) * ST)
                e = n if isinstance(s, int) else sp.snap(n)
                at = bass.ds(e * CAP + E_MLP * CAP if isinstance(s, int) else sp.snap(n * CAP + E_MLP * CAP), CAP)
                one = bass.ds(e, 1)
                sp.dma_start(x[:, i], d["slots"][at, :].rearrange("(t p) c -> p t c", p=P)).then_inc(load_in[i], 16)
                sp.dma_start(w1[:, i], d["L1_ffn_fc1T"][one].rearrange("o (c p) f -> p (o c) f", p=P)).then_inc(load_in[i], 16)
                sp.dma_start(b1[:, i], d["L1_ffn_fc1_biasT"][one].rearrange("o p c -> p (o c)")).then_inc(load_in[i], 16)
                sp.dma_start(w2[:, i], d["L1_ffn_fc2T"][one].rearrange("o (c p) n -> p (o c) n", p=P)).then_inc(load_in[i], 16)
                sp.dma_start(b2[:, i], d["L1_ffn_fc2_bias"][one].to_broadcast([P, DIM])).then_inc(load_in[i], 16)

            over_experts(sp, load)

        @block.tensor
        def _(pe):
            def turn(s, i):
                n = s * 2 + i
                pe.wait_ge(load_in[i], (s + 1) * 16 * LOADS)
                for c in range(CD):
                    if not (first(s) and i == 0):
                        pe.wait_ge(copied, (n - 1) * CD + c + 1)
                    for t in range(ST):
                        mm = pe.transpose(TR[c][:, t * P:(t + 1) * P], x[:, i, t, c * P:(c + 1) * P], ident)
                    mm.then_inc(turned, 1)

            def up(s, i):
                n = s * 2 + i
                pe.wait_ge(copied, (n + 1) * CD)
                for f in range(FC):
                    bank = (i * FC + f) % 2
                    if not (first(s) and i == 0 and f < 2):
                        pe.wait_ge(h_done, n * FC + f - 1)
                    for c in range(CD):
                        mm = pe.matmul(PH[bank][:], w1[:, i, c, f * P:(f + 1) * P], xT[:, i, c, :], start=(c == 0),
                                       stop=(c == CD - 1))
                    mm.then_inc(h_ready, 1)

            def down(s, i):
                n = s * 2 + i
                pe.wait_ge(h_done, (n + 1) * FC)
                for t in range(ST):
                    if not (first(s) and i == 0 and t < 2):
                        pe.wait_ge(y_done, n * ST + t - 1)
                    for f in range(FC):
                        mm = pe.matmul(PY[t % 2][:], hT[:, i, f, t * P:(t + 1) * P], w2[:, i, f, :], start=(f == 0),
                                       stop=(f == FC - 1))
                    mm.then_inc(y_ready, 1)

            def body(s, i):
                turn(s, i)
                up(s, i)
                down(s, i)

            over_experts(pe, body)

        @block.scalar
        def _(act):
            def body(s, i):
                n = s * 2 + i
                for c in range(CD):
                    act.wait_ge(turned, n * CD + c + 1)
                    act.activation(xT[:, i, c], TR[c][:], ACT.Copy).then_inc(copied, 1)
                for f in range(FC):
                    act.wait_ge(h_ready, n * FC + f + 1)
                    act.activation(hT[:, i, f], PH[(i * FC + f) % 2][:], ACT.Gelu, bias=b1[:, i, f:f + 1]).then_inc(h_done, 1)

            over_experts(act, body)

        @block.vector
        def _(dve):
            def body(s, i):
                n = s * 2 + i
                if not first(s):
                    dve.wait_ge(y_out[i], s * 16)
                for t in range(ST):
                    dve.wait_ge(y_ready, n * ST + t + 1)
                    dve.tensor_tensor(y[:, i, t], b2[:, i], PY[t % 2][:], ALU.add).then_inc(y_done, 1)

            over_experts(dve, body)

        @block.gpsimd
        def _(pool):
            def store(s, i):
                n = s * 2 + i
                at = bass.ds(n * CAP + E_MLP * CAP if isinstance(s, int) else pool.snap(n * CAP + E_MLP * CAP), CAP)
                pool.wait_ge(y_done, (n + 1) * ST)
                pool.dma_start(d["slots"][at, :].rearrange("(t p) c -> p t c", p=P), y[:, i]).then_inc(y_out[i], 16)

            over_experts(pool, store)
            for i in range(2):
                pool.wait_ge(y_out[i], 16 * MLPS // 2)


def phase_combine(nc, d, keep):
    with ExitStack() as ctx:
        a = Alloc(nc, ctx, "g")
        NBUF = 4
        from_slot = a.sb("from_slot", [P, TILES * TOP_K], I32)
        coef = a.sb("coef", [P, TILES * TOP_K])
        x3 = a.sb("x3", [P, TILES, DIM])
        got = a.sb("got", [P, TILES, TOP_K, DIM])
        s4 = a.sb("s4", [P, NBUF, DIM])
        s5 = a.sb("s5", [P, NBUF, DIM])
        y = a.sb("y", [P, TILES, DIM])
        eps = a.sb("eps", [P, 1])
        stats = a.sb("stats", [P, TILES, 6])
        moments = a.sb("moments", [P, TILES, 2])
        std = a.sb("std", [P, TILES])
        rstd = a.sb("rstd", [P, TILES])
        idx_in, x3_in, prep, out_done = (a.sem(n) for n in ("idx_in", "x3_in", "prep", "out_done"))
        gathered = [a.sem(f"gathered{i}") for i in range(BLOCKS)]
        added, summed, stat, aggr, std_done, rstd_done, y_done = (
            a.sem(n) for n in ("added", "summed", "stat", "aggr", "std_done", "rstd_done", "y_done"))
        block = ctx.enter_context(nc.Block())

        @block.sync
        def _(sp):
            sp.dma_start(from_slot[:], d["from_slot"]).then_inc(idx_in, 16)
            sp.dma_start(coef[:], d["coef"]).then_inc(x3_in, 16)
            sp.dma_start(x3[:], d["x3"].rearrange("(t p) c -> p t c", p=P)).then_inc(x3_in, 16)
            for n in range(BLOCKS):
                sp.wait_ge(y_done, (n + 1) * TPK)
                sp.dma_start(d["out"][n * BLK:(n + 1) * BLK, :].rearrange("(t p) c -> p t c", p=P),
                             y[:, n * TPK:(n + 1) * TPK]).then_inc(out_done, 16)
            sp.wait_ge(out_done, 16 * BLOCKS)

        @block.gpsimd
        def _(pool):
            pool.wait_ge(idx_in, 16)
            for t in range(TILES):
                for k in range(TOP_K):
                    pool.indirect_dma_start(out=got[:, t, k], out_offset=None, in_=d["slots"],
                                            in_offset=bass.IndirectOffsetOnAxis(
                                                ap=from_slot[:, t * TOP_K + k:t * TOP_K + k + 1].bitcast(U32), axis=0),
                                            bounds_check=SLOTS - 1, oob_is_err=False).then_inc(gathered[t // TPK], 16)

        @block.scalar
        def _(act):
            act.wait_ge(prep, 1)
            for n in range(BLOCKS):
                act.wait_ge(aggr, (n + 1) * TPK)
                act.activation(std[:, n * TPK:(n + 1) * TPK], moments[:, n * TPK:(n + 1) * TPK, 1], ACT.Sqrt,
                               bias=eps[:, 0:1]).then_inc(std_done, 1)

        @block.vector
        def _(dve):
            dve.memset(eps[:], LN_EPS).then_inc(prep, 1)
            dve.wait_ge(x3_in, 32)
            for n in range(BLOCKS):
                tiles = range(n * TPK, (n + 1) * TPK)
                dve.wait_ge(gathered[n], 16 * TPK * TOP_K)
                for t in tiles:
                    dve.scalar_tensor_tensor(out=s4[:, t % NBUF], in0=got[:, t, 0], scalar=coef[:, 2 * t:2 * t + 1],
                                             in1=x3[:, t], op0=ALU.mult, op1=ALU.add).then_inc(added, 1)
                for t in tiles:
                    dve.wait_ge(added, t + 1)
                    dve.scalar_tensor_tensor(out=s5[:, t % NBUF], in0=got[:, t, 1], scalar=coef[:, 2 * t + 1:2 * t + 2],
                                             in1=s4[:, t % NBUF], op0=ALU.mult, op1=ALU.add).then_inc(summed, 1)
                for t in tiles:
                    dve.wait_ge(summed, t + 1)
                    dve.bn_stats(stats[:, t], s5[:, t % NBUF]).then_inc(stat, 1)
                for t in tiles:
                    dve.wait_ge(stat, t + 1)
                    dve.bn_aggr(moments[:, t], stats[:, t]).then_inc(aggr, 1)
                dve.wait_ge(std_done, n + 1)
                dve.reciprocal(rstd[:, n * TPK:(n + 1) * TPK], std[:, n * TPK:(n + 1) * TPK]).then_inc(rstd_done, 1)
                dve.wait_ge(rstd_done, n + 1)
                for t in tiles:
                    dve.tensor_scalar(y[:, t], s5[:, t % NBUF], moments[:, t, 0:1], rstd[:, t:t + 1], ALU.subtract,
                                      ALU.mult).then_inc(y_done, 1)


def program(nc, d):
    with ExitStack() as ctx:
        keep = {"const": ctx.enter_context(nc.sbuf_tensor("const", [P, C_COLS], F32))}
        phase_qkv0(nc, d, keep)
        phase_attention0(nc, d, keep)
        phase_ffn0(nc, d, keep)
        phase_attention1(nc, d, keep)
        phase_route(nc, d, keep)
        phase_experts(nc, d, keep)
        phase_combine(nc, d, keep)


def layout(inputs):
    a = {name: np.ascontiguousarray(inputs[name]) for name in inputs}
    out = {"constants": constants()}
    x = a["L0_attn_x"].reshape(TOKENS, DIM)
    out["x"] = x
    out["xT"] = x.T
    out["L0_wqkvT"] = a["L0_attn_w_qkv"].T
    out["L0_wprojT"] = a["L0_attn_w_proj"].T
    for name in ("b_proj", "q_gamma", "q_beta", "k_gamma", "k_beta"):
        out["L0_attn_" + name] = a["L0_attn_" + name]
    for name in ("w_gate", "w_up", "w_down"):
        out["L0_ffn_" + name + "T"] = a["L0_ffn_" + name].T
    for name in ("L1_attn_w_qkv", "L1_attn_w_out", "L1_attn_head_scales", "L1_ffn_norm_weight", "L1_ffn_router_bias",
                 "L1_ffn_fc2_bias", "L1_ffn_constant_vectors"):
        out[name] = a[name]
    out["L1_ffn_router_weightT"] = a["L1_ffn_router_weight"].T
    out["L1_ffn_fc1_biasT"] = a["L1_ffn_fc1_bias"].reshape(MLPS, FC, P).transpose(0, 2, 1)
    out["L1_ffn_fc1T"] = a["L1_ffn_fc1_weight"].transpose(0, 2, 1)
    out["L1_ffn_fc2T"] = a["L1_ffn_fc2_weight"].transpose(0, 2, 1)
    return {name: np.ascontiguousarray(v) for name, v in out.items()}


SCRATCH = {
    "qk0": ([PARTS * QK_BLK, P, TOKENS], BF16),
    "v0": ([TOKENS, H0 * VS0], F32),
    "att0": ([HG0, P, TOKENS], F32),
    "x2": ([TOKENS, DIM], F32),
    "qk1": ([PARTS * 4, P, TOKENS], BF16),
    "v1": ([TOKENS, H1 * VS1], F32),
    "att1": ([HG1, P, TOKENS], F32),
    "x3": ([TOKENS, DIM], F32),
    "from_slot": ([P, TILES * TOP_K], I32),
    "coef": ([P, TILES * TOP_K], F32),
    "slots": ([E * CAP, DIM], F32),
}


def kernel(**inputs):
    import concourse.bacc as bacc
    from concourse.bass_utils import run_bass_kernel_spmd

    nc = bacc.Bacc("TRN2", target_bir_lowering=False, num_devices=1)
    arrays = layout(inputs)
    d = {name: nc.dram_tensor(name, v.shape, mybir.dt.from_np(v.dtype), kind="ExternalInput").ap()
         for name, v in arrays.items()}
    for name, (shape, dt) in SCRATCH.items():
        d[name] = nc.dram_tensor(name, shape, dt).ap()
    d["out"] = nc.dram_tensor("out", [TOKENS, DIM], F32, kind="ExternalOutput").ap()
    program(nc, d)
    result = run_bass_kernel_spmd(nc, [arrays], core_ids=[0])
    return result.results[0]["out"].reshape(BATCH, SEQ, DIM)
```

```python
from contextlib import ExitStack

import numpy as np
import concourse.bass as bass
from concourse import mybir

F32 = mybir.dt.float32
BF16 = mybir.dt.bfloat16
I32 = mybir.dt.int32
U32 = mybir.dt.uint32
ALU = mybir.AluOpType
ACT = mybir.ActivationFunctionType
AX = mybir.AxisListType

P = 128
BATCH, SEQ, DIM = 4, 1024, 256
TOKENS = BATCH * SEQ
TILES = TOKENS // P
TPB = SEQ // P
CD = DIM // P
BLK = 512
TPK = BLK // P
BLOCKS = TOKENS // BLK
PARTS = 3
COMBOS = [(0, 0), (0, 1), (0, 2), (1, 0), (1, 1), (2, 0)]
MASKED = -1.0e30
LN_EPS = 1e-5

E, CAP = 16, 512
H0, D0 = 16, 16
G0 = 4
HG0 = H0 // G0
QK0_EPS = 1e-6
VS0 = 32
QK_COLS = 2 * H0 * D0
QK_BLK = QK_COLS // P

C_IDENT, C_MASK_Q, C_MASK_K, C_BEFORE, C_COS, C_SIN, C_IOTA, C_DIRS, C_MOVES = np.cumsum(
    [0, P, P, P, P, TPB * D0, TPB * D0, 16, 24]).tolist()
C_COLS = C_MOVES + 16


def constants():
    c = np.zeros((P, C_COLS), np.float32)
    i = np.arange(P)
    c[:, C_IDENT:C_IDENT + P] = np.eye(P)
    c[:, C_MASK_Q:C_MASK_Q + P] = np.where(i[None, :] > i[:, None], MASKED, 0.0)
    c[:, C_MASK_K:C_MASK_K + P] = np.where(i[None, :] < i[:, None], MASKED, 0.0)
    c[:, C_BEFORE:C_BEFORE + P] = i[:, None] < i[None, :]
    half = D0 // 2
    inv_freq = np.float32(1.0) / np.float32(10000.0) ** (np.arange(half, dtype=np.float32) / np.float32(half))
    freqs = np.outer(np.arange(SEQ, dtype=np.float32), inv_freq.astype(np.float32)).astype(np.float32)
    cos = np.cos(np.concatenate([freqs, freqs], -1)).astype(np.float32)
    sin = np.sin(np.concatenate([-freqs, freqs], -1)).astype(np.float32)
    for at, table in ((C_COS, cos), (C_SIN, sin)):
        c[:, at:at + TPB * D0] = table.reshape(TPB, P, D0).transpose(1, 0, 2).reshape(P, TPB * D0)
    c[:, C_IOTA:C_IOTA + 16] = np.arange(16)
    dirs = np.array([[(n >> 2 & 1) * 2 - 1, (n >> 1 & 1) * 2 - 1, (n & 1) * 2 - 1] for n in range(8)], np.float32)
    c[:, C_DIRS:C_DIRS + 24] = (dirs / np.sqrt(3.0, dtype=np.float32)).reshape(1, 24)
    c[:, C_MOVES:C_MOVES + 16] = [0, 1, 0, 0] + [1] * 12
    return c


class Alloc:

    def __init__(self, nc, ctx, phase):
        self.nc, self.ctx, self.phase = nc, ctx, phase
        self.sems = []
        ctx.callback(self.clear)

    def sb(self, name, shape, dt=F32):
        return self.ctx.enter_context(self.nc.sbuf_tensor(f"{self.phase}_{name}", shape, dt))

    def ps(self, name, shape, dt=F32):
        return self.ctx.enter_context(self.nc.psum_tensor(f"{self.phase}_{name}", shape, dt))

    def sem(self, name):
        self.sems.append(self.nc.alloc_semaphore(f"{self.phase}_{name}"))
        return self.sems[-1]

    def clear(self):
        self.nc.clear_and_free_semaphores(self.sems)
        self.nc.all_engine_barrier()


def phase_qkv0(nc, d, keep):
    with ExitStack() as ctx:
        a = Alloc(nc, ctx, "a")
        const = keep["const"]
        ident = const[:, C_IDENT:C_IDENT + P]
        wT = a.sb("wT", [P, CD, 3 * DIM])
        wmean = a.sb("wmean", [P, CD, 2 * H0])
        gb = a.sb("gb", [P, 4, D0])
        gbs = a.sb("gbs", [P, 4, D0])
        ropeA = a.sb("ropeA", [P, TPB, 2, D0])
        ropeB = a.sb("ropeB", [P, TPB, 2, D0])
        ropeC = a.sb("ropeC", [P, TPB, 2, D0])
        ropeD = a.sb("ropeD", [P, TPB, 2, D0])
        eps = a.sb("eps", [P, 1])
        xT = a.sb("xT", [P, 2, CD, BLK])
        sq = a.sb("sq", [P, 2, QK_COLS])
        ss = a.sb("ss", [P, 2, 2 * H0])
        std = a.sb("std", [P, 2, 2 * H0])
        rstd = a.sb("rstd", [P, 2, 2 * H0])
        z = a.sb("z", [P, 4, 2, H0, D0])
        za = a.sb("za", [P, 2, 2, H0, D0])
        zb = a.sb("zb", [P, 2, 2, H0, D0])
        zs = a.sb("zs", [P, 2, 2, H0, D0])
        y = a.sb("y", [P, 4, QK_COLS])
        rest = a.sb("rest", [P, 2, QK_BLK, P])
        parts = a.sb("parts", [P, 2, PARTS, QK_BLK, BLK], BF16)
        vaug = a.sb("vaug", [P, 4, H0, VS0])
        QK = [a.ps(f"QK{i}", [P, QK_COLS]) for i in range(2)]
        V = [a.ps(f"V{i}", [P, DIM]) for i in range(2)]
        YT = [a.ps(f"YT{i}", [P, QK_BLK, P]) for i in range(2)]

        w_in = a.sem("w_in")
        x_in = [a.sem(f"x_in{i}") for i in range(2)]
        prep = a.sem("prep")
        ones_set = a.sem("ones_set")
        qk_ready, v_ready, v_free = a.sem("qk_ready"), a.sem("v_ready"), a.sem("v_free")
        sq_done, red_done, std_done, rstd_done = (a.sem(n) for n in ("sq_done", "red_done", "std_done", "rstd_done"))
        z_done, za_done, zb_done, zs_done, y_done = (a.sem(n) for n in ("z_done", "za_done", "zb_done", "zs_done", "y_done"))
        yt_ready, hi_done, rest_done, mid_done, lo_done = (
            a.sem(n) for n in ("yt_ready", "hi_done", "rest_done", "mid_done", "lo_done"))
        v_done = a.sem("v_done")
        parts_out = [a.sem(f"parts_out{i}") for i in range(2)]
        v_out = [a.sem(f"v_out{i}") for i in range(4)]
        LAG = 3
        block = ctx.enter_context(nc.Block())

        @block.sync
        def _(sp):
            sp.dma_start(const[:], d["constants"]).then_inc(w_in, 16)
            sp.dma_start(wT[:], d["L0_wqkvT"].rearrange("(c p) n -> p c n", p=P)).then_inc(w_in, 16)
            half = D0 // 2
            for i, name in enumerate(("q_gamma", "q_beta", "k_gamma", "k_beta")):
                row = d["L0_attn_" + name].rearrange("(o n) -> o n", o=1)
                sp.dma_start(gb[:, i, :], row.to_broadcast([P, D0])).then_inc(w_in, 16)
                sp.dma_start(gbs[:, i, 0:half], row[:, half:D0].to_broadcast([P, half])).then_inc(w_in, 16)
                sp.dma_start(gbs[:, i, half:D0], row[:, 0:half].to_broadcast([P, half])).then_inc(w_in, 16)

            def load(b, h):
                if not first(b):
                    sp.wait_ge(v_ready, (b - 1) * TPB + (h + 1) * TPK)
                src = d["xT"][:, bass.ds(b * SEQ + h * BLK, BLK)].rearrange("(c p) n -> p c n", p=P)
                sp.dma_start(xT[:, h], src).then_inc(x_in[h], 16)

            def store(b, h):
                sp.wait_ge(lo_done, b * TPB + (h + 1) * TPK)
                dst = d["qk0"][:, :, bass.ds(b * SEQ + h * BLK, BLK)].rearrange("a p n -> p a n")
                sp.dma_start(dst, parts[:, h].rearrange("p s k n -> p (s k) n")).then_inc(parts_out[h], 16)

            for h in range(2):
                load(0, h)
            with sp.Fori(0, BATCH - 1) as b:
                for h in range(2):
                    load(b + 1, h)
                    store(b, h)
            for h in range(2):
                store(BATCH - 1, h)
            for h in range(2):
                sp.wait_ge(parts_out[h], 16 * BATCH + 16)

        @block.gpsimd
        def _(pool):
            pool.wait_ge(prep, 14)

            def steps(b, lo, hi):
                for k in range(lo, hi):
                    n = b * TPB + k
                    if k < TPB:
                        pool.wait_ge(z_done, n + 1)
                        tab = ropeA[:, k % TPB].unsqueeze(2).to_broadcast([P, 2, H0, D0])
                        pool.tensor_tensor(za[:, k % 2], z[:, k % 4], tab, ALU.mult).then_inc(za_done, 1)
                    m = k - 1
                    if (not first(b) or m >= 0) and m < TPB:
                        pool.wait_ge(zs_done, n)
                        if not (first(b) and m < 4):
                            pool.wait_ge(yt_ready, n - 4)
                        tab = ropeC[:, m % TPB].unsqueeze(2).to_broadcast([P, 2, H0, D0])
                        out = y[:, m % 4].rearrange("p (x h c) -> p x h c", x=2, h=H0)
                        pool.tensor_tensor(out, zs[:, m % 2], tab, ALU.add).then_inc(y_done, 1)
                    m = k - 3
                    if (not first(b) or m >= 0) and m < TPB:
                        pool.wait_ge(mid_done, n - 2)
                        t = m % TPB
                        at = parts[:, t // TPK, :, :, (t % TPK) * P:(t % TPK + 1) * P]
                        pool.tensor_tensor(at[:, 2], rest[:, m % 2], at[:, 1], ALU.subtract).then_inc(lo_done, 1)

            pipeline(pool, steps, LAG)

        @block.tensor
        def _(pe):
            pe.wait_ge(prep, 14)

            def qkv(b, t):
                n = b * TPB + t
                h, at = t // TPK, (t % TPK) * P
                if t % TPK == 0:
                    pe.wait_ge(x_in[h], b * 16 + 16)
                if not (first(b) and t < 2):
                    pe.wait_ge(z_done, n - 1)
                    pe.wait_ge(v_done, n - 1)
                for c in range(CD):
                    mm = pe.matmul(QK[t % 2][:], xT[:, h, c, at:at + P], wT[:, c, 0:QK_COLS],
                                   start=(c == 0), stop=(c == CD - 1))
                mm.then_inc(qk_ready, 1)
                for c in range(CD):
                    mm = pe.matmul(V[t % 2][:], xT[:, h, c, at:at + P], wT[:, c, QK_COLS:3 * DIM],
                                   start=(c == 0), stop=(c == CD - 1))
                mm.then_inc(v_ready, 1)

            def turn(b, t):
                n = b * TPB + t
                pe.wait_ge(y_done, n + 1)
                if not (first(b) and t < 2):
                    pe.wait_ge(rest_done, n - 1)
                for i in range(QK_BLK):
                    mm = pe.transpose(YT[t % 2][:, i], y[:, t % 4, i * P:(i + 1) * P], ident)
                mm.then_inc(yt_ready, 1)

            def steps(b, lo, hi):
                for k in range(lo, hi):
                    if k < TPB:
                        qkv(b, k)
                    m = k - 2
                    if (not first(b) or m >= 0) and m < TPB:
                        if m >= 0:
                            turn(b, m)
                        else:
                            turn(b - 1, m + TPB)

            pipeline(pe, steps, LAG)

        @block.scalar
        def _(act):
            for h in range(2):
                act.sem_inc(parts_out[h], 16)
            act.wait_ge(prep, 14)

            def steps(b, lo, hi):
                for k in range(lo, hi):
                    n = b * TPB + k
                    old = not (first(b) and k < 3) and k - 3 < TPB
                    t = (k - 3) % TPB
                    at = parts[:, t // TPK, :, :, (t % TPK) * P:(t % TPK + 1) * P]
                    if k < TPB:
                        act.wait_ge(qk_ready, n + 1)
                        if not (first(b) and k < 2):
                            act.wait_ge(red_done, n - 1)
                        act.activation(sq[:, k % 2], QK[k % 2][:], ACT.Square).then_inc(sq_done, 1)
                    if old:
                        act.wait_ge(yt_ready, n - 2)
                        if t % TPK == 0:
                            act.wait_ge(parts_out[t // TPK], b * 16 + 16 if k >= 3 else b * 16)
                        act.activation(at[:, 0], YT[t % 2][:], ACT.Copy).then_inc(hi_done, 1)
                    if k < TPB:
                        act.wait_ge(red_done, n + 1)
                        act.activation(std[:, k % 2], ss[:, k % 2], ACT.Sqrt, bias=eps[:, 0:1],
                                       scale=1.0 / D0).then_inc(std_done, 1)
                        act.wait_ge(v_ready, n + 1)
                        if not (first(b) and k < 4):
                            act.wait_ge(v_out[k % 4], (b * 2 + k // 4) * 16)
                        act.activation(vaug[:, k % 4, :, 0:D0], V[k % 2][:].rearrange("p (h c) -> p h c", h=H0),
                                       ACT.Copy).then_inc(v_done, 1)
                        act.wait_ge(v_done, n + 1)
                        act.dma_start(d["v0"][bass.ds(b * SEQ + k * P, P), :],
                                      vaug[:, k % 4].rearrange("p h c -> p (h c)")).then_inc(v_out[k % 4], 16)
                    if old:
                        act.wait_ge(rest_done, n - 2)
                        act.activation(at[:, 1], rest[:, t % 2], ACT.Copy).then_inc(mid_done, 1)

            pipeline(act, steps, LAG)
            for i in range(4):
                act.wait_ge(v_out[i], 16 * TILES // 4)

        @block.vector
        def _(dve):
            dve.memset(eps[:], QK0_EPS).then_inc(prep, 1)
            for i in range(4):
                last = dve.memset(vaug[:, i], 0.0)
            last.then_inc(ones_set, 1)
            dve.wait_ge(ones_set, 1)
            dve.memset(vaug[:, :, :, D0:D0 + 1], 1.0).then_inc(prep, 1)
            dve.wait_ge(w_in, 16 * 14)
            for c in range(CD):
                last = dve.tensor_reduce(wmean[:, c], wT[:, c, 0:QK_COLS].rearrange("p (h c) -> p h c", c=D0),
                                         AX.X, ALU.add)
            last.then_inc(prep, 1)
            for x in range(2):
                if x == 0:
                    for g in (gb, gbs):
                        last = dve.tensor_scalar(g[:, 0:2], g[:, 0:2], float(D0) ** -0.5, None, ALU.mult)
                    last.then_inc(prep, 1)
            dve.wait_ge(prep, 4)
            dve.tensor_scalar(wmean[:], wmean[:], 1.0 / D0, None, ALU.mult).then_inc(prep, 1)
            dve.wait_ge(prep, 5)
            for c in range(CD):
                w = wT[:, c, 0:QK_COLS].rearrange("p (h c) -> p h c", c=D0)
                last = dve.tensor_tensor(w, w, wmean[:, c].unsqueeze(2).to_broadcast([P, 2 * H0, D0]), ALU.subtract)
            last.then_inc(prep, 1)
            cos = const[:, C_COS:C_COS + TPB * D0].rearrange("p (t c) -> p t c", t=TPB)
            sin = const[:, C_SIN:C_SIN + TPB * D0].rearrange("p (t c) -> p t c", t=TPB)
            for x in range(2):
                def row(g, i):
                    return g[:, 2 * x + i].unsqueeze(1).to_broadcast([P, TPB, D0])
                dve.tensor_tensor(ropeA[:, :, x], cos, row(gb, 0), ALU.mult).then_inc(prep, 1)
                dve.tensor_tensor(ropeB[:, :, x], sin, row(gbs, 0), ALU.mult).then_inc(prep, 1)
                dve.tensor_tensor(ropeC[:, :, x], cos, row(gb, 1), ALU.mult).then_inc(prep, 1)
                dve.tensor_tensor(ropeD[:, :, x], sin, row(gbs, 1), ALU.mult).then_inc(ones_set, 1)
                dve.wait_ge(prep, 9 + 4 * x)
                dve.wait_ge(ones_set, 2 + x)
                dve.tensor_tensor(ropeC[:, :, x], ropeC[:, :, x], ropeD[:, :, x], ALU.add).then_inc(prep, 1)
            dve.wait_ge(prep, 14)
            half = D0 // 2

            def steps(b, lo, hi):
                for k in range(lo, hi):
                    n = b * TPB + k
                    if k < TPB:
                        dve.wait_ge(sq_done, n + 1)
                        if not (first(b) and k < 2):
                            dve.wait_ge(std_done, n - 1)
                        dve.tensor_reduce(ss[:, k % 2], sq[:, k % 2].rearrange("p (h c) -> p h c", c=D0), AX.X,
                                          ALU.add).then_inc(red_done, 1)
                    if not (first(b) and k < 3) and k - 3 < TPB:
                        t = (k - 3) % TPB
                        at = parts[:, t // TPK, :, :, (t % TPK) * P:(t % TPK + 1) * P]
                        dve.wait_ge(hi_done, n - 2)
                        if not (first(b) and k < 5):
                            dve.wait_ge(lo_done, n - 4)
                        dve.tensor_tensor(rest[:, t % 2], YT[t % 2][:], at[:, 0], ALU.subtract).then_inc(rest_done, 1)
                    if k < TPB:
                        dve.wait_ge(std_done, n + 1)
                        dve.reciprocal(rstd[:, k % 2], std[:, k % 2]).then_inc(rstd_done, 1)
                        dve.wait_ge(rstd_done, n + 1)
                        dve.tensor_tensor(z[:, k % 4].rearrange("p x h c -> p (x h) c"),
                                          QK[k % 2][:].rearrange("p (h c) -> p h c", c=D0),
                                          rstd[:, k % 2].unsqueeze(2).to_broadcast([P, 2 * H0, D0]),
                                          ALU.mult).then_inc(z_done, 1)
                        dve.wait_ge(z_done, n + 1)
                        tab = ropeB[:, k].unsqueeze(2).to_broadcast([P, 2, H0, D0])
                        zk, zbk = z[:, k % 4], zb[:, k % 2]
                        dve.tensor_tensor(zbk[:, :, :, 0:half], zk[:, :, :, half:D0], tab[:, :, :, 0:half], ALU.mult)
                        dve.tensor_tensor(zbk[:, :, :, half:D0], zk[:, :, :, 0:half], tab[:, :, :, half:D0],
                                          ALU.mult).then_inc(zb_done, 1)
                    m = k - 1
                    if (not first(b) or m >= 0) and m < TPB:
                        dve.wait_ge(za_done, n)
                        dve.wait_ge(zb_done, n)
                        if not (first(b) and m < 2):
                            dve.wait_ge(y_done, n - 2)
                        dve.tensor_tensor(zs[:, m % 2], za[:, m % 2], zb[:, m % 2], ALU.add).then_inc(zs_done, 1)

            pipeline(dve, steps, LAG)


def first(b):
    return isinstance(b, int) and b == 0


def pipeline(eng, steps, lag):
    steps(0, 0, TPB)
    with eng.Fori(1, BATCH) as b:
        steps(b, 0, TPB)
    steps(BATCH, 0, 0) if lag == 0 else tail(steps, lag)


def tail(steps, lag):
    steps(BATCH - 1, TPB, TPB + lag)


def phase_attention0(nc, d, keep, weights):
    HALVES = SEQ // BLK
    ROUNDS = HALVES * TPB
    UNITS = ROUNDS * G0
    MAXES = G0 * TPB * HALVES
    AHEAD = 5 * G0
    TURN = (MAXES - AHEAD) // G0 + 1
    RING = 16
    SBANKS, MBANKS = 3, 4
    K = len(COMBOS) * D0
    TURNS = MAXES // MBANKS
    KM = K + PARTS
    BUFS = HG0
    ROW_DMAS = 16 * G0
    ZERO_ROWS = 4
    ZERO_DMAS = E * CAP // (P * ZERO_ROWS)
    with ExitStack() as ctx:
        a = Alloc(nc, ctx, "b")
        qst = [a.sb(f"qst{i}", [P, G0, SEQ], BF16) for i in range(BUFS)]
        kst = [a.sb(f"kst{i}", [P, G0, SEQ], BF16) for i in range(BUFS)]
        vst = [a.sb(f"vst{i}", [P, TPB, G0, VS0]) for i in range(BUFS)]
        probs = a.sb("probs", [P, RING, BLK])
        outT = a.sb("outT", [P, HALVES, BLK])
        mx = a.sb("mx", [P, G0, TPB, HALVES])
        m = a.sb("m", [P, G0, TPB])
        mrest = a.sb("mrest", [P, G0, TPB])
        mparts = a.sb("mparts", [P, TPB, G0, 32], BF16)
        mrows = a.sb("mrows", [P, SEQ], BF16)
        identb = a.sb("identb", [P, P], BF16)
        zero = a.sb("zero", [P, ZERO_ROWS * DIM])
        PM = [a.ps(f"PM{i}", [P, BLK]) for i in range(MBANKS)]
        PS = [a.ps(f"PS{i}", [P, BLK]) for i in range(SBANKS)]
        PO = a.ps("PO", [P, BLK])
        PT = PM[MBANKS - 1][:].bitcast(BF16)

        setup = a.sem("setup")
        q_in = [a.sem(f"q_in{i}") for i in range(BUFS)]
        v_in = [a.sem(f"v_in{i}") for i in range(BUFS)]
        max_scores = a.sem("max_scores")
        max_taken = [a.sem(f"max_taken{i}") for i in range(MBANKS)]
        m_step, m_parts, m_turned, m_copied, rows_in = (
            a.sem(n) for n in ("m_step", "m_parts", "m_turned", "m_copied", "rows_in"))
        scores, exped, pv_done, out_copied = (a.sem(n) for n in ("scores", "exped", "pv_done", "out_copied"))
        out_stored = [a.sem(f"out_stored{i}") for i in range(HALVES)]
        zeroed, zero_out, consts_in = a.sem("zeroed"), a.sem("zero_out"), a.sem("consts_in")
        block = ctx.enter_context(nc.Block())

        def over_groups(eng, body):
            with eng.Fori(0, BATCH - 1) as b:
                for hg in range(HG0):
                    body(b, hg, 2)
            for hg in range(HG0):
                body(BATCH - 1, hg, min(2, HG0 - 1 - hg))

        @block.sync
        def _(sp):
            def load(b, hg):
                tok = bass.ds(b * SEQ, SEQ)
                for stack, side, first_blk in ((qst, 0, 0), (kst, 1, QK_BLK // 2)):
                    for s, combo in enumerate(COMBOS):
                        rows = d["qk0"][combo[side] * QK_BLK + first_blk + hg // 2, (hg % 2) * 64:(hg % 2) * 64 + 64, tok]
                        sp.dma_start(stack[hg][s * D0:(s + 1) * D0], rows.rearrange("(j p) n -> p j n", p=D0))\
                          .then_inc(q_in[hg], 16)
                src = d["v0"][tok, hg * G0 * VS0:(hg + 1) * G0 * VS0].rearrange("(t p) c -> p t c", p=P)
                sp.dma_start(vst[hg][:].rearrange("p t j c -> p t (j c)"), src).then_inc(v_in[hg], 16)

            def rows(g, nxt):
                sp.wait_ge(m_copied, g + 1)
                for j in range(G0):
                    sp.dma_start(qst[nxt][K:KM, j, :], mrows[32 * j:32 * j + PARTS, :]).then_inc(rows_in, 16)

            def store(b, g, hg, half):
                sp.wait_ge(out_copied, g * HALVES + half + 2)
                sp.dma_start(d["att0"][hg, :, bass.ds(b * SEQ + half * BLK, BLK)], outT[:, half])\
                  .then_inc(out_stored[half], 16)

            def group(b, hg, left):
                g = b * HG0 + hg
                store(b, g, hg, 0)
                if left:
                    rows(g + 1, (hg + 1) % BUFS)
                store(b, g, hg, 1)
                if not isinstance(b, int):
                    sp.wait_ge(pv_done, (g + 1) * ROUNDS + RING // G0)
                    load(b + 1, hg)

            for hg in range(HG0):
                load(0, hg)
            rows(0, 0)
            over_groups(sp, group)
            for half in range(HALVES):
                sp.wait_ge(out_stored[half], 16 * (BATCH * HG0 + 1))

        @block.gpsimd
        def _(pool):
            pool.memset(zero[:], 0.0).then_inc(zeroed, 1)
            pool.wait_ge(v_in[HG0 - 1], 16)
            pool.wait_ge(zeroed, 1)
            sl = d["slots"].rearrange("(n p r) c -> n p (r c)", p=P, r=ZERO_ROWS)
            for n in range(ZERO_DMAS):
                pool.dma_start(sl[n], zero[:]).then_inc(zero_out, 16)
            pool.wait_ge(zero_out, 16 * ZERO_DMAS)
            for n in range(2):
                row = d["L1_ffn_constant_vectors"][n:n + 1, :].to_broadcast([CAP, DIM])
                pool.dma_start(d["slots"][(2 + n) * CAP:(3 + n) * CAP, :], row).then_inc(consts_in, 16)
            pool.wait_ge(consts_in, 32)
            weights.prepare(a, pool, d, keep["const"])

        @block.tensor
        def _(pe):
            pe.sem_inc(pv_done, RING // G0)
            pe.wait_ge(setup, 1)
            turns = 16 * 2 * len(COMBOS)

            def max_product(g, buf, u):
                j, qt, kh = u // (HALVES * TPB), u // HALVES % TPB, u % HALVES
                pe.wait_ge(max_taken[u % MBANKS], g * TURNS + u // MBANKS + 1)
                pe.matmul(PM[u % MBANKS][:], qst[buf][0:K, j, qt * P:(qt + 1) * P],
                          kst[buf][0:K, j, kh * BLK:(kh + 1) * BLK], start=True, stop=True).then_inc(max_scores, 1)

            def turn_max(g, behind):
                pe.wait_ge(m_parts, g + 1)
                pe.wait_ge(max_taken[MBANKS - 1], (g + 1) * TURNS + behind // MBANKS + 1)
                for qt in range(TPB):
                    mm = pe.transpose(PT[:, qt * P:(qt + 1) * P], mparts[:, qt].rearrange("p j c -> p (j c)"), identb[:])
                mm.then_inc(m_turned, 1)

            def values(g, hg, r):
                kt = r % TPB
                pe.wait_ge(exped, g * UNITS + (r + 1) * G0 + SBANKS)
                if kt == 0:
                    pe.wait_ge(out_copied, g * HALVES + r // TPB + 1)
                for j in range(G0):
                    mm = pe.matmul(PO[j * VS0:(j + 1) * VS0, :], vst[hg][:, kt, j, :], probs[:, (r * G0 + j) % RING],
                                   start=(kt == 0), stop=(kt == TPB - 1), tile_position=(0, j * VS0))
                mm.then_inc(pv_done, 1)

            def stream(s):
                pause = TURN * G0 + G0 - 1
                late = {pause + 1: 1, pause + 2: 2, pause + 3: 1}
                return AHEAD + s - late.get(s, 0)

            def group(b, hg, left):
                g = b * HG0 + hg

                def ahead(t):
                    n = 1 + t // MAXES
                    if n > left:
                        return
                    if t == MAXES:
                        pe.wait_ge(q_in[(hg + 2) % BUFS], (b + (hg + 2) // BUFS) * turns + turns)
                    if t == MAXES + 2 * MBANKS - 1:
                        pe.wait_ge(m_copied, g + 2)
                    max_product(g + n, (hg + n) % BUFS, t % MAXES)

                pe.wait_ge(v_in[hg], b * 16 + 16)
                pe.wait_ge(rows_in, (g + 1) * ROW_DMAS)
                for r in range(ROUNDS):
                    half, kt = r // TPB, r % TPB
                    for j in range(G0):
                        s = r * G0 + j
                        pe.wait_ge(exped, g * UNITS + s + 1)
                        pe.matmul(PS[s % SBANKS][:], kst[hg][0:KM, j, kt * P:(kt + 1) * P],
                                  qst[hg][0:KM, j, half * BLK:(half + 1) * BLK], start=True, stop=True).then_inc(scores, 1)
                        if r == TURN and j == G0 - 1 and left:
                            turn_max(g + 1, MBANKS if left > 1 else 0)
                        if r < ROUNDS - 1:
                            for t in range(stream(s), stream(s + 1)):
                                ahead(t)
                    if r > 0:
                        values(g, hg, r - 1)
                for j in range(G0):
                    ahead(AHEAD + UNITS - G0 + j)
                values(g, hg, ROUNDS - 1)

            pe.wait_ge(q_in[0], turns)
            for u in range(MAXES):
                max_product(0, 0, u)
            turn_max(0, 0)
            pe.wait_ge(q_in[1], turns)
            for u in range(AHEAD):
                if u == MBANKS - 1:
                    pe.wait_ge(m_copied, 1)
                max_product(1, 1, u)
            over_groups(pe, group)

        @block.scalar
        def _(act):
            act.sem_inc(exped, SBANKS)

            def group(b, hg, left):
                g = b * HG0 + hg
                for r in range(ROUNDS):
                    for j in range(G0):
                        s = r * G0 + j
                        act.wait_ge(scores, g * UNITS + s + 1)
                        if j == 0:
                            act.wait_ge(pv_done, g * ROUNDS + r + 1)
                        act.activation(probs[:, s % RING], PS[s % SBANKS][:], ACT.Exp).then_inc(exped, 1)
                        if r == TURN and j == G0 - 1 and left:
                            act.wait_ge(rows_in, (g + 1) * ROW_DMAS)
                            act.wait_ge(m_turned, g + 2)
                            act.activation(mrows[:], PT, ACT.Copy).then_inc(m_copied, 1)

            act.wait_ge(m_turned, 1)
            act.activation(mrows[:], PT, ACT.Copy).then_inc(m_copied, 1)
            over_groups(act, group)

        @block.vector
        def _(dve):
            for i in range(MBANKS):
                dve.sem_inc(max_taken[i], 1)
            dve.sem_inc(out_copied, 1)
            for half in range(HALVES):
                dve.sem_inc(out_stored[half], 16)
            for i in range(BUFS):
                dve.memset(kst[i][K:KM], 1.0)
            dve.tensor_copy(identb[:], keep["const"][:, C_IDENT:C_IDENT + P])
            dve.memset(mparts[:], 0.0).then_inc(setup, 1)
            dve.wait_ge(setup, 1)

            def take(g, u):
                dve.wait_ge(max_scores, g * MAXES + u + 1)
                j, qt, kh = u // (HALVES * TPB), u // HALVES % TPB, u % HALVES
                dve.tensor_reduce(mx[:, j, qt, kh:kh + 1], PM[u % MBANKS][:], AX.X, ALU.max)\
                   .then_inc(max_taken[u % MBANKS], 1)

            def minus_max(g):
                dve.wait_ge(max_taken[MBANKS - 1], (g + 1) * TURNS + 1)
                dve.tensor_tensor(m[:], mx[:, :, :, 0], mx[:, :, :, 1], ALU.max).then_inc(m_step, 1)
                part = [mparts[:, :, :, i].rearrange("p t j -> p j t") for i in range(PARTS)]
                dve.wait_ge(m_step, g * 4 + 1)
                if not (isinstance(g, int) and g == 0):
                    dve.wait_ge(m_turned, g)
                dve.tensor_scalar(part[0], m[:], -1.0, None, ALU.mult).then_inc(m_step, 1)
                dve.wait_ge(m_step, g * 4 + 2)
                dve.scalar_tensor_tensor(out=mrest[:], in0=m[:], scalar=-1.0, in1=part[0], op0=ALU.mult,
                                         op1=ALU.subtract).then_inc(m_step, 1)
                dve.wait_ge(m_step, g * 4 + 3)
                dve.tensor_copy(part[1], mrest[:]).then_inc(m_step, 1)
                dve.wait_ge(m_step, g * 4 + 4)
                dve.tensor_tensor(part[2], mrest[:], part[1], ALU.subtract).then_inc(m_parts, 1)

            def copy_out(g, half):
                dve.wait_ge(pv_done, g * ROUNDS + (half + 1) * TPB + RING // G0)
                dve.wait_ge(out_stored[half], g * 16 + 16)
                dve.tensor_copy(outT[:, half], PO[:]).then_inc(out_copied, 1)

            def group(b, hg, left):
                g = b * HG0 + hg
                for t in range(AHEAD, AHEAD + MAXES):
                    if t - AHEAD == (TPB + 1) * G0 + 1:
                        copy_out(g, 0)
                    if 1 + t // MAXES <= left:
                        take(g + 1 + t // MAXES, t % MAXES)
                    if t == MAXES - 1 and left:
                        minus_max(g + 1)
                copy_out(g, 1)

            for u in range(MAXES):
                take(0, u)
            minus_max(0)
            for u in range(AHEAD):
                take(1, u)
            over_groups(dve, group)

HID = 768
HC = HID // P
INT8_SCALE = float(np.float32(1.0 / 127.0))
H1, D1 = 8, 32
G1 = 2
HG1 = H1 // G1
VS1 = 64
HPS = SEQ // BLK
F32R = mybir.dt.float32r
HALVES1 = 2
HIGH_BITS = -(1 << 12)
PAIRS1 = [(0, 0), (0, 1), (1, 0)]


def high_half(eng, out, x):
    return eng.tensor_scalar(out.bitcast(I32), x.bitcast(I32), HIGH_BITS, None, ALU.bitwise_and)


def lagged(b, h, lag):
    m = h - lag
    if m >= HPS or (first(b) and m < 0):
        return None
    return b * HPS + m, m % 2, first(b)


def block_pipeline(eng, step, lag):
    for h in range(HPS):
        step(0, h)
    with eng.Fori(1, BATCH) as b:
        for h in range(HPS):
            step(b, h)
    for h in range(HPS, HPS + lag):
        step(BATCH - 1, h)


class Layer0Weights:

    def __init__(self, nc, ctx):
        a = Alloc(nc, ctx, "u")
        shapes = {"proj": (CD, DIM), "gate": (CD, HID), "up": (CD, HID), "qkv": (CD, 3 * DIM), "down": (HC, DIM)}
        self.shapes = shapes
        self.halves = {n: a.sb("w_" + n, [P, HALVES1, *shape], F32R) for n, shape in shapes.items()}

    def prepare(self, a, pool, d, const):
        raw = {n: a.sb("raw_" + n, [P, *shape]) for n, shape in self.shapes.items()}
        hscale = a.sb("hscale", [P, H1])
        geo = a.sb("geo", [P, CD, H1, 3])
        dot = a.sb("dot", [P, CD, H1])
        dot2 = a.sb("dot2", [P, CD, H1])
        w_in, scaled, geo_step, cut, low = (a.sem("w_" + n) for n in ("in", "scaled", "geo_step", "cut", "low"))
        sources = {"proj": "L0_wprojT", "gate": "L0_ffn_w_gateT", "up": "L0_ffn_w_upT", "qkv": "L1_attn_w_qkv",
                   "down": "L0_ffn_w_downT"}
        whole = ("gate", "up", "down")
        for n, source in sources.items():
            out = raw[n][:].bitcast(I32) if n in whole else raw[n][:]
            pool.dma_start(out, d[source].rearrange("(c p) n -> p c n", p=P)).then_inc(w_in, 16)
        pool.dma_start(hscale[:], d["L1_attn_head_scales"].rearrange("(o n) -> o n", o=1).to_broadcast([P, H1])).then_inc(w_in, 16)
        pool.wait_ge(w_in, 16 * 6)
        for n in whole:
            pool.tensor_scalar(raw[n][:], raw[n][:].bitcast(I32), INT8_SCALE, None, ALU.mult).then_inc(scaled, 1)
        dirs = const[:, C_DIRS:C_DIRS + 24].rearrange("p (h c) -> p h c", c=3)
        wq = [raw["qkv"][:, c, 0:DIM].rearrange("p (h c) -> p h c", c=D1) for c in range(CD)]
        done = 0

        def steps(*instructions):
            nonlocal done
            done += 1
            instructions[-1].then_inc(geo_step, 1)
            pool.wait_ge(geo_step, done)
        steps(*[pool.tensor_tensor(geo[:, c], wq[c][:, :, 0:3], dirs, ALU.mult) for c in range(CD)])
        steps(pool.tensor_tensor(dot[:], geo[:, :, :, 0], geo[:, :, :, 1], ALU.add),
              *[pool.tensor_scalar(raw["qkv"][:, c, 0:DIM], raw["qkv"][:, c, 0:DIM], float(1.0 / np.sqrt(D1)), None, ALU.mult)
                for c in range(CD)])
        steps(pool.tensor_tensor(dot2[:], dot[:], geo[:, :, :, 2], ALU.add))
        steps(pool.tensor_tensor(dot[:], dot2[:], hscale[:].unsqueeze(1).to_broadcast([P, CD, H1]), ALU.mult))
        steps(*[pool.tensor_tensor(geo[:, c], dirs, dot[:, c].unsqueeze(2).to_broadcast([P, H1, 3]), ALU.mult)
                for c in range(CD)])
        steps(*[pool.tensor_tensor(wq[c][:, :, 0:3], wq[c][:, :, 0:3], geo[:, c], ALU.add) for c in range(CD)])
        pool.wait_ge(scaled, len(whole))
        for k, n in enumerate(self.shapes):
            pool.tensor_copy(self.halves[n][:, 0], raw[n][:]).then_inc(cut, 1)
        for k, n in enumerate(self.shapes):
            pool.wait_ge(cut, k + 1)
            pool.tensor_tensor(self.halves[n][:, 1], raw[n][:], self.halves[n][:, 0].bitcast(F32), ALU.subtract).then_inc(low, 1)
        pool.wait_ge(low, len(self.shapes))


def phase_ffn0(nc, d, keep, weights):
    with ExitStack() as ctx:
        a = Alloc(nc, ctx, "c")
        const = keep["const"]
        ident = const[:, C_IDENT:C_IDENT + P]
        bproj = a.sb("bproj", [P, DIM])
        wproj, wgate, wup, wdown, wqkv = (weights.halves[name] for name in ("proj", "gate", "up", "down", "qkv"))
        eps = a.sb("eps", [P, 1])
        attT = a.sb("attT", [P, 2, HG0, BLK])
        xin = a.sb("xin", [P, 2, TPK, DIM])
        rec = a.sb("rec", [P, 2, H0])
        att = a.sb("att", [P, TPK, DIM])
        att2T = a.sb("att2T", [P, HALVES1, CD, BLK], F32R)
        s1 = a.sb("s1", [P, TPK, DIM])
        x1 = a.sb("x1", [P, 2, TPK, DIM])
        x1T = a.sb("x1T", [P, HALVES1, CD, BLK], F32R)
        gate = a.sb("gate", [P, 2, BLK])
        hidden = a.sb("hidden", [P, 2, BLK])
        hT = a.sb("hT", [P, HALVES1, HC, BLK], F32R)
        s2 = a.sb("s2", [P, TPK, DIM])
        x2 = a.sb("x2", [P, 2, TPK, DIM])
        x2T = a.sb("x2T", [P, HALVES1, CD, BLK], F32R)
        stats = a.sb("stats", [P, 2, TPK, 6])
        moments = a.sb("moments", [P, 2, TPK, 2])
        std = a.sb("std", [P, 2, TPK])
        rstd = a.sb("rstd", [P, 2, TPK])
        halves = a.sb("halves", [P, HALVES1, 4, BLK])
        vaug = a.sb("vaug", [P, 2, TPK, H1, VS1])
        TR = [a.ps(f"TR{i}", [P, BLK]) for i in range(2)]
        PG = [a.ps(f"PG{i}", [P, BLK]) for i in range(2)]
        PU = [a.ps(f"PU{i}", [P, BLK]) for i in range(2)]
        PO = [a.ps(f"PO{i}", [P, BLK]) for i in range(2)]
        QK = [PG[0], PG[1], PU[0], PU[1]]

        w_in, prep, vset = a.sem("w_in"), a.sem("prep"), a.sem("vset")
        seen = a.sem("seen")
        att_in = [a.sem(f"att_in{i}") for i in range(2)]
        xin_in = [a.sem(f"xin_in{i}") for i in range(2)]
        names = ("att_turned", "rec_done", "normed", "att2_turned", "att2_high", "att2_low", "projected", "biased", "summed1",
                 "stat1", "aggr1", "std1", "rstd1", "x1_done", "x1_turned", "x1_high", "x1_low", "gated", "upped", "silu", "hidden", "h_high", "h_low",
                 "downed", "summed2", "stat2", "aggr2", "std2", "rstd2", "x2_done", "x2_turned", "x2_high", "x2_low",
                 "qk_ready", "hi_done", "lo_done", "v_ready", "v_copied")
        S = {n: a.sem(n) for n in names}
        x2_out = [a.sem(f"x2_out{i}") for i in range(2)]
        halves_out = a.sem("halves_out")
        v_out = [a.sem(f"v_out{i}") for i in range(2)]
        PREP = 2
        LAG = 2
        block = ctx.enter_context(nc.Block())

        @block.sync
        def _(sp):
            sp.dma_start(bproj[:], d["L0_attn_b_proj"].rearrange("(o n) -> o n", o=1).to_broadcast([P, DIM])).then_inc(w_in, 16)

            def step(b, h):
                if now := lagged(b, h, 0):
                    n, i, new = now
                    tok = bass.ds(n * BLK if isinstance(b, int) else sp.snap(n * BLK), BLK)
                    if not new:
                        sp.wait_ge(S["att_turned"], (n - 1) * TPK)
                        sp.wait_ge(S["summed1"], (n - 1) * TPK)
                    sp.dma_start(attT[:, i], d["att0"][:, :, tok].rearrange("g p n -> p g n")).then_inc(att_in[i], 16)
                    sp.dma_start(xin[:, i], d["x"][tok, :].rearrange("(t p) c -> p t c", p=P)).then_inc(xin_in[i], 16)
                if now := lagged(b, h, 2):
                    n, i, new = now
                    tok = bass.ds(n * BLK if isinstance(b, int) else sp.snap(n * BLK), BLK)
                    sp.wait_ge(S["x2_done"], (n + 1) * TPK)
                    sp.dma_start(d["x2"][tok, :].rearrange("(t p) c -> p t c", p=P), x2[:, i]).then_inc(x2_out[i], 16)
            block_pipeline(sp, step, LAG)
            for i in range(2):
                for s in (x2_out, v_out):
                    sp.wait_ge(s[i], 16 * BATCH + 16)
            sp.wait_ge(halves_out, 16 * BLOCKS + 16)

        @block.gpsimd
        def _(pool):
            pool.wait_ge(w_in, 16)

            def step(b, h):
                if now := lagged(b, h, 0):
                    n, i, new = now
                    pool.wait_ge(xin_in[i], b * 16 + 16)
                    pool.tensor_tensor(xin[:, i], xin[:, i], bproj[:].unsqueeze(1).to_broadcast([P, TPK, DIM]),
                                       ALU.add).then_inc(S["biased"], 1)
                if now := lagged(b, h, 1):
                    n, i, new = now
                    for k in range(HC):
                        pool.wait_ge(S["h_high"], n * HC + k + 1)
                        pool.tensor_tensor(hT[:, 1, k], hidden[:, k % 2], hT[:, 0, k].bitcast(F32), ALU.subtract)\
                            .then_inc(S["h_low"], 1)

            block_pipeline(pool, step, LAG)

        @block.tensor
        def _(pe):

            def turn(out, src, count):
                for c in range(CD):
                    for t in range(TPK):
                        mm = pe.transpose(out[c][:, t * P:(t + 1) * P], src[:, t, c * P:(c + 1) * P], ident)
                    mm.then_inc(count, 1)

            def product(out, lhs, rhs, chunks):
                for k, (left, right) in enumerate(PAIRS1):
                    for c in range(chunks):
                        mm = pe.matmul(out, lhs(left, c), rhs(right, c), start=(k == 0 and c == 0),
                                       stop=(k == len(PAIRS1) - 1 and c == chunks - 1))
                return mm

            def turn_sums(b, h, tiles):
                if now := lagged(b, h, 0):
                    n, i, new = now
                    if 0 in tiles:
                        pe.wait_ge(att_in[i], b * 16 + 16)
                    for t in tiles:
                        if t >= 2:
                            pe.wait_ge(S["normed"], n * TPK + t - 1)
                        elif not (new and i == 0):
                            pe.wait_ge(S["att2_low"], n * CD)
                        for g in range(HG0):
                            mm = pe.transpose(TR[t % 2][:, g * P:(g + 1) * P], attT[:, i, g, t * P:(t + 1) * P], ident)
                        mm.then_inc(S["att_turned"], 1)

            def turn_x2(b, h):
                if now := lagged(b, h, 2):
                    n, i, new = now
                    pe.wait_ge(S["x2_done"], (n + 1) * TPK)
                    if lagged(b, h, 0):
                        pe.wait_ge(S["normed"], (n + 3) * TPK)
                    else:
                        pe.wait_ge(S["att2_low"], BLOCKS * CD)
                        if h == HPS + 1:
                            pe.wait_ge(S["x2_low"], n * CD)
                    turn(TR, x2[:, i], S["x2_turned"])

            def turn_att(b, h):
                if now := lagged(b, h, 0):
                    n, i, new = now
                    pe.wait_ge(S["normed"], (n + 1) * TPK)
                    if lagged(b, h, 2):
                        pe.wait_ge(S["x2_low"], (n - 1) * CD)
                    turn(TR, att[:], S["att2_turned"])

            def turn_x1(b, h):
                if now := lagged(b, h, 0):
                    n, i, new = now
                    pe.wait_ge(S["x1_done"], (n + 1) * TPK)
                    if lagged(b, h, 2):
                        pe.wait_ge(S["lo_done"], n * 4)
                    turn(PG, x1[:, i], S["x1_turned"])

            def step(b, h):
                turn_sums(b, h, (0, 1))
                now = lagged(b, h, 1)
                if now:
                    n, i, new = now
                    pe.wait_ge(S["x1_low"], (n + 1) * CD)
                    if not (new and i == 0):
                        pe.wait_ge(S["lo_done"], n * 4)
                for k in range(HC):
                    if k == 2:
                        turn_sums(b, h, (2, 3))
                    elif k == 3:
                        turn_x2(b, h)
                    elif k == 5:
                        turn_att(b, h)
                    if now:
                        if not (new and i == 0 and k < 2):
                            pe.wait_ge(S["hidden"], n * HC + k - 1)
                        for w, out, done in ((wgate, PG, "gated"), (wup, PU, "upped")):
                            product(out[k % 2][:], lambda s, c: w[:, s, c, k * P:(k + 1) * P], lambda s, c: x1T[:, s, c, :],
                                    CD).then_inc(S[done], 1)
                if now := lagged(b, h, 0):
                    n, i, new = now
                    pe.wait_ge(S["att2_low"], (n + 1) * CD)
                    for t in range(TPK):
                        if t < 2 and not (first(b) and h < 2):
                            pe.wait_ge(S["summed2"], (n - 1) * TPK)
                        if t >= 2:
                            pe.wait_ge(S["summed1"], n * TPK + t - 1)
                        product(PO[t % 2][:, 0:DIM], lambda s, c: att2T[:, s, c, t * P:(t + 1) * P],
                                lambda s, c: wproj[:, s, c, :], CD).then_inc(S["projected"], 1)
                if now := lagged(b, h, 2):
                    n, i, new = now
                    pe.wait_ge(S["x2_low"], (n + 1) * CD)
                    pe.wait_ge(S["hidden"], (n + 2) * HC if lagged(b, h, 1) else BLOCKS * HC)
                    for k in range(4):
                        product(QK[k][:], lambda s, c: wqkv[:, s, c, k * P:(k + 1) * P], lambda s, c: x2T[:, s, c, :],
                                CD).then_inc(S["qk_ready"], 1)
                    for t in range(TPK):
                        if t < 2:
                            if lagged(b, h, 0):
                                pe.wait_ge(S["summed1"], (n + 3) * TPK)
                            else:
                                pe.wait_ge(S["summed2"], (n + 1) * TPK)
                        else:
                            pe.wait_ge(S["v_copied"], n * TPK + t - 1)
                        product(PO[t % 2][:, 0:DIM], lambda s, c: x2T[:, s, c, t * P:(t + 1) * P],
                                lambda s, c: wqkv[:, s, c, 2 * DIM:3 * DIM], CD).then_inc(S["v_ready"], 1)
                if now := lagged(b, h, 1):
                    pe.wait_ge(S["h_low"], (now[0] + 1) * HC)
                for t in range(TPK):
                    if t == TPK // 2:
                        turn_x1(b, h)
                    if now:
                        n, i, new = now
                        if t < 2:
                            if lagged(b, h, 2):
                                pe.wait_ge(S["v_copied"], (n - 1) * TPK + t + 3)
                            elif lagged(b, h, 0):
                                pe.wait_ge(S["summed1"], (n + 2) * TPK)
                        else:
                            pe.wait_ge(S["summed2"], n * TPK + t - 1)
                        product(PO[t % 2][:, 0:DIM], lambda s, k: hT[:, s, k, t * P:(t + 1) * P],
                                lambda s, k: wdown[:, s, k, :], HC).then_inc(S["downed"], 1)

            block_pipeline(pe, step, LAG)

        @block.scalar
        def _(act):
            for i in range(2):
                act.sem_inc(v_out[i], 16)
            act.sem_inc(halves_out, 16)
            act.wait_ge(prep, PREP)

            def deviation(which, i, n, count, done):
                act.wait_ge(S[count], (n + 1) * TPK)
                act.activation(std[:, which], moments[:, which, :, 1], ACT.Sqrt, bias=eps[:, 0:1]).then_inc(S[done], 1)

            def high_halves(n, xT, banks, name):
                for c in range(CD):
                    act.wait_ge(S[name + "_turned"], n * CD + c + 1)
                    act.activation(xT[:, 0, c], banks[c][:], ACT.Copy).then_inc(S[name + "_high"], 1)

            def step(b, h):
                gated = lagged(b, h, 1)
                for k in range(HC):
                    if k == 3 and (now := lagged(b, h, 2)):
                        high_halves(now[0], x2T, TR, "x2")
                    if k == 5 and (now := lagged(b, h, 0)):
                        high_halves(now[0], att2T, TR, "att2")
                    if gated:
                        n, i, new = gated
                        act.wait_ge(S["gated"], n * HC + k + 1)
                        if not (new and i == 0 and k < 2):
                            act.wait_ge(S["hidden"], n * HC + k - 1)
                        act.activation(gate[:, k % 2], PG[k % 2][:], ACT.Silu).then_inc(S["silu"], 1)
                if now := lagged(b, h, 2):
                    n, i, new = now
                    act.wait_ge(v_out[i], stored(b, h, 2))
                    for t in range(TPK):
                        act.wait_ge(S["v_ready"], n * TPK + t + 1)
                        act.activation(vaug[:, i, t, :, 0:D1], PO[t % 2][:, 0:DIM].rearrange("p (h c) -> p h c", h=H1),
                                       ACT.Copy).then_inc(S["v_copied"], 1)
                if now := lagged(b, h, 0):
                    n, i, new = now
                    deviation(0, i, n, "aggr1", "std1")
                    high_halves(n, x1T, PG, "x1")
                if now := lagged(b, h, 1):
                    n, i, new = now
                    deviation(1, i, n, "aggr2", "std2")
                if now := lagged(b, h, 2):
                    n, i, new = now
                    tok = bass.ds(n * BLK if isinstance(b, int) else act.snap(n * BLK), BLK)
                    act.wait_ge(S["v_copied"], (n + 1) * TPK)
                    act.dma_start(d["v1"][tok, :].rearrange("(t p) c -> p t c", p=P),
                                  vaug[:, i].rearrange("p t h c -> p t (h c)")).then_inc(v_out[i], 16)
                    act.wait_ge(S["lo_done"], (n + 1) * 4 + 4)
                    act.dma_start(d["qk1"][:, :, tok].rearrange("a p n -> p a n"),
                                  halves[:].rearrange("p s k n -> p (s k) n")).then_inc(halves_out, 16)

            block_pipeline(act, step, LAG)

        @block.vector
        def _(dve):
            for i in range(2):
                dve.sem_inc(x2_out[i], 16)
            dve.sem_inc(S["lo_done"], 4)
            dve.memset(eps[:], LN_EPS).then_inc(prep, 1)
            for i in range(2):
                last = dve.memset(vaug[:, i], 0.0)
            last.then_inc(vset, 1)
            dve.wait_ge(vset, 1)
            for i in range(2):
                last = dve.memset(vaug[:, i, :, :, D1:D1 + 1], 1.0)
            last.then_inc(prep, 1)
            dve.wait_ge(prep, PREP)

            def moments_of(which, src, n, count, done):
                for t in range(TPK):
                    dve.wait_ge(S[count], n * TPK + t + 1)
                    dve.bn_stats(stats[:, which, t], src[:, t]).then_inc(S["stat" + done], 1)
                dve.wait_ge(S["stat" + done], (n + 1) * TPK)
                dve.sem_inc(seen, 1)
                for t in range(TPK):
                    dve.bn_aggr(moments[:, which, t], stats[:, which, t]).then_inc(S["aggr" + done], 1)

            def norm(which, src, out, n, done, x_done):
                dve.wait_ge(S["std" + done], n + 1)
                dve.reciprocal(rstd[:, which], std[:, which]).then_inc(S["rstd" + done], 1)
                dve.wait_ge(S["rstd" + done], n + 1)
                for t in range(TPK):
                    dve.tensor_scalar(out[:, t], src[:, t], moments[:, which, t, 0:1], rstd[:, which, t:t + 1],
                                      ALU.subtract, ALU.mult).then_inc(S[x_done], 1)

            def low_halves(n, xT, banks, name):
                for c in range(CD):
                    dve.wait_ge(S[name + "_high"], n * CD + c + 1)
                    dve.tensor_tensor(xT[:, 1, c], banks[c][:], xT[:, 0, c].bitcast(F32), ALU.subtract)\
                       .then_inc(S[name + "_low"], 1)

            def normalise(b, h, tiles):
                if now := lagged(b, h, 0):
                    n, i, new = now
                    for t in tiles:
                        dve.wait_ge(S["att_turned"], n * TPK + t + 1)
                        heads = TR[t % 2][:].rearrange("p (h c) -> p h c", h=H0)
                        dve.reciprocal(rec[:, t % 2], heads[:, :, D0]).then_inc(S["rec_done"], 1)
                        dve.wait_ge(S["rec_done"], n * TPK + t + 1)
                        dve.tensor_tensor(att[:, t].rearrange("p (h c) -> p h c", h=H0), heads[:, :, 0:D0],
                                          rec[:, t % 2].unsqueeze(2).to_broadcast([P, H0, D0]), ALU.mult)\
                           .then_inc(S["normed"], 1)

            def step(b, h):
                gated = lagged(b, h, 1)
                for k in range(HC):
                    if k < 2:
                        normalise(b, h, (2 * k, 2 * k + 1))
                    if k == 3 and (now := lagged(b, h, 2)):
                        low_halves(now[0], x2T, TR, "x2")
                    if k == 5 and (now := lagged(b, h, 0)):
                        low_halves(now[0], att2T, TR, "att2")
                    if gated:
                        n, i, new = gated
                        dve.wait_ge(S["silu"], n * HC + k + 1)
                        dve.wait_ge(S["upped"], n * HC + k + 1)
                        if not (new and i == 0 and k < 2):
                            dve.wait_ge(S["h_low"], n * HC + k - 1)
                        dve.tensor_tensor(hidden[:, k % 2], gate[:, k % 2], PU[k % 2][:], ALU.mult).then_inc(S["hidden"], 1)
                        dve.wait_ge(S["hidden"], n * HC + k + 1)
                        dve.tensor_copy(hT[:, 0, k], hidden[:, k % 2]).then_inc(S["h_high"], 1)
                if now := lagged(b, h, 0):
                    n, i, new = now
                    dve.wait_ge(S["biased"], n + 1)
                    for t in range(TPK):
                        dve.wait_ge(S["projected"], n * TPK + t + 1)
                        dve.tensor_tensor(s1[:, t], xin[:, i, t], PO[t % 2][:, 0:DIM], ALU.add).then_inc(S["summed1"], 1)
                    moments_of(0, s1[:], n, "summed1", "1")
                if now := lagged(b, h, 2):
                    n, i, new = now
                    dve.wait_ge(halves_out, n * 16 + 16)
                    for k in range(4):
                        dve.wait_ge(S["qk_ready"], n * 4 + k + 1)
                        high_half(dve, halves[:, 0, k], QK[k][:]).then_inc(S["hi_done"], 1)
                        dve.wait_ge(S["hi_done"], n * 4 + k + 1)
                        dve.tensor_tensor(halves[:, 1, k], QK[k][:], halves[:, 0, k], ALU.subtract)\
                           .then_inc(S["lo_done"], 1)
                if now := lagged(b, h, 0):
                    n, i, new = now
                    norm(0, s1[:], x1[:, i], n, "1", "x1_done")
                now = lagged(b, h, 1)
                for t in range(TPK):
                    if t == TPK // 2 and (other := lagged(b, h, 0)):
                        low_halves(other[0], x1T, PG, "x1")
                    if now:
                        n, i, new = now
                        dve.wait_ge(S["downed"], n * TPK + t + 1)
                        dve.tensor_tensor(s2[:, t], x1[:, i, t], PO[t % 2][:, 0:DIM], ALU.add).then_inc(S["summed2"], 1)
                if now:
                    moments_of(1, s2[:], now[0], "summed2", "2")
                if now := lagged(b, h, 1):
                    n, i, new = now
                    dve.wait_ge(x2_out[i], stored(b, h, 1))
                    norm(1, s2[:], x2[:, i], n, "2", "x2_done")

            block_pipeline(dve, step, LAG)


def stored(b, h, lag):
    return b * 16 + 16 if h - lag >= 0 else b * 16

def phase_attention1(nc, d, keep, weights):
    K = len(PAIRS1) * D1
    KM = K + HALVES1
    BUFS = HG1
    RING = 8
    SBANKS, MBANKS = 3, 3
    MAXES = [(j, qt, kh) for j in range(G1) for qt in range(TPB) for kh in range(qt // TPK + 1)]
    UNITS = [(half, kt, j) for half in range(HPS) for kt in range((half + 1) * TPK) for j in range(G1)]
    NM, NU = len(MAXES), len(UNITS)
    TURNS = NM // MBANKS
    ROUNDS = NU // G1
    HALF_ROUNDS = [sum(1 for u in UNITS if u[0] <= half) // G1 for half in range(HPS)]
    AHEAD = 12
    TURN = NM + 2 * MBANKS - 1 - AHEAD
    ROW_DMAS = 16 * HALVES1
    assert NM == NU
    with ExitStack() as ctx:
        a = Alloc(nc, ctx, "d")
        const = keep["const"]
        ident = const[:, C_IDENT:C_IDENT + P]
        qst = [a.sb(f"qst{i}", [P, G1, SEQ], F32R) for i in range(BUFS)]
        kst = [a.sb(f"kst{i}", [P, G1, SEQ], F32R) for i in range(BUFS)]
        vst = [a.sb(f"vst{i}", [P, TPB, G1, VS1]) for i in range(BUFS)]
        probs = a.sb("probs", [P, RING, BLK])
        outT = a.sb("outT", [P, HPS, BLK])
        mx = a.sb("mx", [P, G1, TPB, 2])
        m = a.sb("m", [P, G1, TPB])
        minus = a.sb("minus", [P, G1, TPB])
        mhalves = a.sb("mhalves", [P, P // (G1 * TPB), G1, TPB])
        mrows = a.sb("mrows", [HALVES1 * G1 * TPB, P])
        fixed = a.sb("fixed", [P, 3, P], BF16)
        identb, mask_q, mask_k = (fixed[:, i] for i in range(3))
        PM = [a.ps(f"PM{i}", [P, BLK]) for i in range(MBANKS)]
        PS = [a.ps(f"PS{i}", [P, BLK]) for i in range(SBANKS)]
        PO = [a.ps(f"PO{i}", [P, BLK]) for i in range(HPS)]
        PT = PM[MBANKS - 1][:, 0:P]

        setup = a.sem("setup")
        q_in = [a.sem(f"q_in{i}") for i in range(BUFS)]
        v_in = [a.sem(f"v_in{i}") for i in range(BUFS)]
        max_scores = a.sem("max_scores")
        max_taken = [a.sem(f"max_taken{i}") for i in range(MBANKS)]
        m_step, m_cut, m_turned, m_copied, rows_in = (
            a.sem(n) for n in ("m_step", "m_cut", "m_turned", "m_copied", "rows_in"))
        scores, exped, pv_done, out_copied = (a.sem(n) for n in ("scores", "exped", "pv_done", "out_copied"))
        out_stored = [a.sem(f"out_stored{i}") for i in range(HPS)]
        block = ctx.enter_context(nc.Block())

        def over_groups(eng, body):
            with eng.Fori(0, BATCH - 1) as b:
                for hg in range(HG1):
                    body(b, hg, 2)
            for hg in range(HG1):
                body(BATCH - 1, hg, min(2, HG1 - 1 - hg))

        def queries(half, kt):
            q0 = max(half * BLK, kt * P)
            return q0, (half + 1) * BLK - q0

        def keys(qt, kh):
            return min(BLK, (qt + 1) * P - kh * BLK)

        @block.sync
        def _(sp):
            def load(b, hg):
                tok = bass.ds(b * SEQ, SEQ)
                for stack, side, first_blk in ((qst, 0, 0), (kst, 1, 2)):
                    for s, pair in enumerate(PAIRS1):
                        rows = d["qk1"][pair[side] * 4 + first_blk + hg // 2, (hg % 2) * 64:(hg % 2) * 64 + 64, tok]
                        sp.dma_start(stack[hg][s * D1:(s + 1) * D1].bitcast(F32), rows.rearrange("(j p) n -> p j n", p=D1))\
                          .then_inc(q_in[hg], 16)
                src = d["v1"][tok, hg * G1 * VS1:(hg + 1) * G1 * VS1].rearrange("(t p) c -> p t c", p=P)
                sp.dma_start(vst[hg][:].rearrange("p t j c -> p t (j c)"), src).then_inc(v_in[hg], 16)

            def rows(g, nxt):
                sp.wait_ge(m_copied, g + 1)
                for i in range(HALVES1):
                    sp.dma_start(qst[nxt][K + i:K + i + 1].bitcast(F32), mrows[i * G1 * TPB:(i + 1) * G1 * TPB, :])\
                      .then_inc(rows_in, 16)

            def store(b, g, hg, half):
                sp.wait_ge(out_copied, g * HPS + half + HPS + 1)
                sp.dma_start(d["att1"][hg, :, bass.ds(b * SEQ + half * BLK, BLK)], outT[:, half])\
                  .then_inc(out_stored[half], 16)

            def group(b, hg, left):
                g = b * HG1 + hg
                store(b, g, hg, 0)
                if left:
                    rows(g + 1, (hg + 1) % BUFS)
                store(b, g, hg, 1)
                if not isinstance(b, int):
                    sp.wait_ge(pv_done, (g + 1) * ROUNDS + RING // G1)
                    load(b + 1, hg)

            for hg in range(HG1):
                load(0, hg)
            rows(0, 0)
            weights.load_first(sp, d)
            over_groups(sp, group)
            for half in range(HPS):
                sp.wait_ge(out_stored[half], 16 * (BATCH * HG1 + 1))

        @block.tensor
        def _(pe):
            pe.sem_inc(pv_done, RING // G1)
            pe.wait_ge(setup, 2)
            turns = 16 * 2 * len(PAIRS1)

            def max_product(g, buf, u):
                j, qt, kh = MAXES[u]
                w = keys(qt, kh)
                diagonal = kh == qt // TPK
                out = PM[u % MBANKS]
                pe.wait_ge(max_taken[u % MBANKS], g * TURNS + u // MBANKS + 1)
                mm = pe.matmul(out[:, 0:w], qst[buf][0:K, j, qt * P:(qt + 1) * P],
                               kst[buf][0:K, j, kh * BLK:kh * BLK + w], start=True, stop=not diagonal)
                if diagonal:
                    mm = pe.matmul(out[:, w - P:w], identb, mask_q, start=False, stop=True)
                mm.then_inc(max_scores, 1)

            def turn_max(g, behind):
                pe.wait_ge(m_cut, g + 1)
                pe.wait_ge(max_taken[MBANKS - 1], (g + 1) * TURNS + behind + 1)
                pe.transpose(PT, mhalves[:].rearrange("p i j t -> p (i j t)"), ident).then_inc(m_turned, 1)

            def values(g, hg, r):
                half, kt, _ = UNITS[r * G1]
                q0, w = queries(half, kt)
                pe.wait_ge(exped, g * NU + (r + 1) * G1 + SBANKS)
                if kt == 0:
                    pe.wait_ge(out_copied, g * HPS + half + 1)
                for j in range(G1):
                    mm = pe.matmul(PO[half][j * VS1:(j + 1) * VS1, q0 - half * BLK:q0 - half * BLK + w],
                                   vst[hg][:, kt, j, :], probs[:, (r * G1 + j) % RING, 0:w], start=(kt == 0),
                                   stop=(kt == (half + 1) * TPK - 1), tile_position=(0, j * VS1))
                mm.then_inc(pv_done, 1)

            def stream(s):
                late = {TURN + 1: 1, TURN + 2: 2, TURN + 3: 1}
                return AHEAD + s - late.get(s, 0)

            def group(b, hg, left):
                g = b * HG1 + hg

                def ahead(t):
                    n = 1 + t // NM
                    if n > left:
                        return
                    if t == NM:
                        pe.wait_ge(q_in[(hg + 2) % BUFS], (b + (hg + 2) // BUFS) * turns + turns)
                    if t == NM + 2 * MBANKS - 1:
                        pe.wait_ge(m_copied, g + 2)
                    max_product(g + n, (hg + n) % BUFS, t % NM)

                pe.wait_ge(v_in[hg], b * 16 + 16)
                pe.wait_ge(rows_in, (g + 1) * ROW_DMAS)
                for s, (half, kt, j) in enumerate(UNITS):
                    q0, w = queries(half, kt)
                    diagonal = q0 == kt * P
                    pe.wait_ge(exped, g * NU + s + 1)
                    out = PS[s % SBANKS]
                    mm = pe.matmul(out[:, 0:w], kst[hg][0:KM, j, kt * P:(kt + 1) * P], qst[hg][0:KM, j, q0:q0 + w],
                                   start=True, stop=not diagonal)
                    if diagonal:
                        mm = pe.matmul(out[:, 0:P], identb, mask_k, start=False, stop=True)
                    mm.then_inc(scores, 1)
                    if s == TURN and left:
                        turn_max(g + 1, 1 if left > 1 else 0)
                    if s < NU - G1:
                        for t in range(stream(s), stream(s + 1)):
                            ahead(t)
                    if j == G1 - 1 and s >= G1:
                        values(g, hg, s // G1 - 1)
                for t in range(AHEAD + NU - G1, AHEAD + NU):
                    ahead(t)
                values(g, hg, ROUNDS - 1)

            pe.wait_ge(q_in[0], turns)
            for u in range(NM):
                max_product(0, 0, u)
            turn_max(0, 0)
            pe.wait_ge(q_in[1], turns)
            for u in range(AHEAD):
                if u == MBANKS - 1:
                    pe.wait_ge(m_copied, 1)
                max_product(1, 1, u)
            over_groups(pe, group)

        @block.scalar
        def _(act):
            act.sem_inc(exped, SBANKS)

            def copy_rows(g):
                act.wait_ge(m_turned, g + 1)
                act.activation(mrows[:], PT[0:HALVES1 * G1 * TPB], ACT.Copy).then_inc(m_copied, 1)

            def group(b, hg, left):
                g = b * HG1 + hg
                for s, (half, kt, j) in enumerate(UNITS):
                    w = queries(half, kt)[1]
                    act.wait_ge(scores, g * NU + s + 1)
                    if j == 0:
                        act.wait_ge(pv_done, g * ROUNDS + s // G1 + 1)
                    act.activation(probs[:, s % RING, 0:w], PS[s % SBANKS][:, 0:w], ACT.Exp).then_inc(exped, 1)
                    if s == TURN and left:
                        act.wait_ge(rows_in, (g + 1) * ROW_DMAS)
                        copy_rows(g + 1)

            copy_rows(0)
            over_groups(act, group)

        @block.vector
        def _(dve):
            for i in range(MBANKS):
                dve.sem_inc(max_taken[i], 1)
            dve.sem_inc(out_copied, HPS)
            for half in range(HPS):
                dve.sem_inc(out_stored[half], 16)
            for i in range(BUFS):
                dve.memset(kst[i][K:KM].bitcast(F32), 1.0)
            for i, at in enumerate((C_IDENT, C_MASK_Q, C_MASK_K)):
                dve.tensor_copy(fixed[:, i], const[:, at:at + P])
            dve.memset(mx[:], -3.0e38).then_inc(setup, 1)
            dve.memset(mhalves[:], 0.0).then_inc(setup, 1)
            dve.wait_ge(setup, 2)

            def take(g, u):
                j, qt, kh = MAXES[u]
                dve.wait_ge(max_scores, g * NM + u + 1)
                dve.tensor_reduce(mx[:, j, qt, kh:kh + 1], PM[u % MBANKS][:, 0:keys(qt, kh)], AX.X, ALU.max)\
                   .then_inc(max_taken[u % MBANKS], 1)

            def minus_max(g):
                dve.wait_ge(max_taken[MBANKS - 1], (g + 1) * TURNS + 1)
                dve.tensor_tensor(m[:], mx[:, :, :, 0], mx[:, :, :, 1], ALU.max).then_inc(m_step, 1)
                dve.wait_ge(m_step, g * 3 + 1)
                dve.tensor_scalar(minus[:], m[:], -1.0, None, ALU.mult).then_inc(m_step, 1)
                dve.wait_ge(m_step, g * 3 + 2)
                if not (isinstance(g, int) and g == 0):
                    dve.wait_ge(m_turned, g)
                high_half(dve, mhalves[:, 0], minus[:]).then_inc(m_step, 1)
                dve.wait_ge(m_step, g * 3 + 3)
                dve.tensor_tensor(mhalves[:, 1], minus[:], mhalves[:, 0], ALU.subtract).then_inc(m_cut, 1)

            def copy_out(g, half):
                dve.wait_ge(pv_done, g * ROUNDS + HALF_ROUNDS[half] + RING // G1)
                dve.wait_ge(out_stored[half], g * 16 + 16)
                dve.tensor_copy(outT[:, half], PO[half][:]).then_inc(out_copied, 1)

            def group(b, hg, left):
                g = b * HG1 + hg
                for t in range(AHEAD, AHEAD + NM):
                    if t - AHEAD == (HALF_ROUNDS[0] + 1) * G1 + 1:
                        copy_out(g, 0)
                    if 1 + t // NM <= left:
                        take(g + 1 + t // NM, t % NM)
                    if t == NM - 1 and left:
                        minus_max(g + 1)
                copy_out(g, 1)

            for u in range(NM):
                take(0, u)
            minus_max(0)
            for u in range(AHEAD):
                take(1, u)
            over_groups(dve, group)

E_COPY, E_MLP = 1, 4
MLPS = E - E_MLP
TOP_K = 2
SLOTS = E * CAP
NOWHERE = float(2 * SLOTS)


def phase_route(nc, d, keep, weights):
    with ExitStack() as ctx:
        a = Alloc(nc, ctx, "e")
        const = keep["const"]
        ident = const[:, C_IDENT:C_IDENT + P]
        iota = const[:, C_IOTA:C_IOTA + E]
        wout = a.sb("wout", [P, CD, DIM])
        wr = a.sb("wr", [P, CD, E])
        nwc = a.sb("nwc", [P, CD, 1])
        wrn = a.sb("wrn", [P, CD, E])
        br = a.sb("br", [P, E])
        nw = a.sb("nw", [P, DIM])
        before = a.sb("before", [P, P], BF16)
        ones = a.sb("ones", [P, P], BF16)
        eps = a.sb("eps", [P, 1])
        attT = a.sb("attT", [P, 2, HG1, BLK])
        x2 = a.sb("x2", [P, 2, TPK, DIM])
        rec = a.sb("rec", [P, TPK, H1])
        att = a.sb("att", [P, 2, TPK, DIM])
        att2T = a.sb("att2T", [P, 2, CD, BLK])
        s3 = a.sb("s3", [P, 2, TPK, DIM])
        x3 = a.sb("x3", [P, 2, TPK, DIM])
        square = a.sb("square", [P, TPK, DIM])
        scaled3 = a.sb("scaled3", [P, TPK, DIM])
        xn = a.sb("xn", [P, 2, TPK, DIM])
        x3T = a.sb("x3T", [P, 2, CD, BLK])
        stats = a.sb("stats", [P, TPK, 6])
        moments = a.sb("moments", [P, 2, TPK, 2])
        std = a.sb("std", [P, 2, TPK])
        rstd = a.sb("rstd", [P, 2, TPK])
        shift = a.sb("shift", [P, 2, TPK])
        meansq = a.sb("meansq", [P, TPK])
        rms = a.sb("rms", [P, 2, TPK])
        rrms = a.sb("rrms", [P, 2, TPK])
        scaled = a.sb("scaled", [P, TPK, E])
        logits = a.sb("logits", [P, TPK, E])
        top = a.sb("top", [P, TPK])
        below = a.sb("below", [P, TPK, E])
        expd = a.sb("expd", [P, TPK, E])
        total = a.sb("total", [P, TPK])
        rtotal = a.sb("rtotal", [P, TPK])
        prob = a.sb("prob", [P, TPK, E])
        best = a.sb("best", [P, TPK, 8])
        besti = a.sb("besti", [P, TPK, 8], U32)
        expert = a.sb("expert", [P, TPK, TOP_K])
        onehot = a.sb("onehot", [P, TPK, TOP_K, E])
        chosen = a.sb("chosen", [P, TPK, E], BF16)
        count = a.sb("count", [P, 2, TPK + 1, E], BF16)
        ranked = a.sb("ranked", [P, TPK, TOP_K, E])
        rank = a.sb("rank", [P, TPK, TOP_K])
        kept = a.sb("kept", [P, TPK, TOP_K])
        slot = a.sb("slot", [P, TPK, TOP_K])
        place = a.sb("place", [P, TPK, TOP_K])
        copies = a.sb("copies", [P, TPK, TOP_K])
        mlps = a.sb("mlps", [P, TPK, TOP_K])
        holds = a.sb("holds", [P, TPK, TOP_K])
        moves = a.sb("moves", [P, TPK, TOP_K])
        target = a.sb("target", [P, TPK, TOP_K])
        weight = a.sb("weight", [P, TPK, TOP_K])
        wsum = a.sb("wsum", [P, TPK])
        wzero = a.sb("wzero", [P, TPK])
        divisor = a.sb("divisor", [P, TPK])
        rwsum = a.sb("rwsum", [P, TPK])
        to_slot = a.sb("to_slot", [P, 2, TPK, TOP_K], I32)
        from_slot = a.sb("from_slot", [P, 2, TPK, TOP_K], I32)
        coef = a.sb("coef", [P, 2, TPK, TOP_K])
        TR = [a.ps(f"TR{i}", [P, BLK]) for i in range(4)]
        PX = [a.ps(f"PX{i}", [P, BLK]) for i in range(2)]
        PL = a.ps("PL", [P, TPK, E])
        PR = a.ps("PR", [P, TPK, E])

        w_in, prep = a.sem("w_in"), a.sem("prep")
        seen, pool_seen = a.sem("seen"), a.sem("pool_seen")
        att_in = [a.sem(f"att_in{i}") for i in range(2)]
        x2_in = [a.sem(f"x2_in{i}") for i in range(2)]
        names = ("att_turned", "rec_done", "normed", "att2_turned", "att2_copied", "projected", "summed", "stat", "aggr",
                 "std_done", "rstd_step", "rstd_done", "x3_done", "squared", "rms_done", "rrms_done", "scaled3_done", "xn_done",
                  "x3_turned",
                 "x3_copied", "logits_ready", "step", "expd_done", "counted", "ranks_ready", "routed", "xn_free")
        S = {n: a.sem(n) for n in names}
        x3_out = [a.sem(f"x3_out{i}") for i in range(2)]
        route_out = [a.sem(f"route_out{i}") for i in range(2)]
        scattered = a.sem("scattered")
        PREP = 4
        TURN_ORDER = (2, 3, 0, 1)
        block = ctx.enter_context(nc.Block())
        ATT, SUM, NORM, ROUTE, STORE = range(5)

        def steps(eng, step, last):
            for p in range(2):
                for h in range(HPS):
                    step(p, h)
            with eng.Fori(2, BATCH) as p:
                for h in range(HPS):
                    step(p, h)
            for h in range(last):
                step(BATCH + h // HPS, h % HPS)

        def at(p, h, stage):
            n, i, used = p * HPS + (h - stage), (h - stage) % HPS, p + (h - stage) // HPS
            if isinstance(n, int) and not 0 <= n < BLOCKS:
                return None
            return n, i, used

        def wait_if_any(eng, sem, value):
            if not isinstance(value, int) or value > 0:
                eng.wait_ge(sem, value)

        @block.sync
        def _(sp):


            def where(n, size):
                return bass.ds(n * size if isinstance(n, int) else sp.snap(n * size), size)

            def step(p, h):
                if now := at(p, h, ATT):
                    n, i, used = now
                    tok = where(n, BLK)
                    wait_if_any(sp, S["att_turned"], (n - 1) * TPK)
                    sp.dma_start(attT[:, i], d["att1"][:, :, tok].rearrange("g p n -> p g n")).then_inc(att_in[i], 16)
                if now := at(p, h, ROUTE):
                    n, i, used = now
                    sp.wait_ge(S["x3_done"], (n + 1) * TPK)
                    sp.dma_start(d["x3"][where(n, BLK), :].rearrange("(t p) c -> p t c", p=P), x3[:, i])\
                      .then_inc(x3_out[i], 16)
                if now := at(p, h, ATT):
                    n, i, used = now
                    wait_if_any(sp, S["summed"], (n - 1) * TPK)
                    sp.dma_start(x2[:, i], d["x2"][where(n, BLK), :].rearrange("(t p) c -> p t c", p=P)).then_inc(x2_in[i], 16)
                if now := at(p, h, STORE):
                    n, i, used = now
                    cols = where(n, TPK * TOP_K)
                    sp.wait_ge(S["routed"], n + 1)
                    sp.dma_start(d["from_slot"][:, cols], from_slot[:, i].rearrange("p t k -> p (t k)"))\
                      .then_inc(route_out[i], 16)
                    sp.dma_start(d["coef"][:, cols], coef[:, i].rearrange("p t k -> p (t k)")).then_inc(route_out[i], 16)
                if isinstance(p, int) and (p, h) == (0, 0):
                    sp.dma_start(wout[:], d["L1_attn_w_out"].rearrange("(c p) n -> p c n", p=P)).then_inc(w_in, 16)
                    sp.dma_start(wr[:], d["L1_ffn_router_weightT"].rearrange("(c p) n -> p c n", p=P)).then_inc(w_in, 16)
                    for c in range(CD):
                        sp.dma_start(nwc[:, c], d["L1_ffn_norm_weight"].rearrange("(c p o) -> c p o", p=P, o=1)[c])\
                          .then_inc(w_in, 16)
                    for out, name in ((br, "router_bias"), (nw, "norm_weight")):
                        sp.dma_start(out[:], d["L1_ffn_" + name].rearrange("(o n) -> o n", o=1).to_broadcast(list(out.shape)))\
                          .then_inc(w_in, 16)

            steps(sp, step, STORE)
            for i in range(2):
                sp.wait_ge(x3_out[i], 16 * (BATCH + 1))
                sp.wait_ge(route_out[i], 2 * 16 * (BATCH + 1))

        @block.tensor
        def _(pe):
            def turn(out, src, count):
                for c in range(CD):
                    for t in range(TPK):
                        mm = pe.transpose(out[c][:, t * P:(t + 1) * P], src[:, t, c * P:(c + 1) * P], ident)
                    mm.then_inc(count, 1)

            def turn_heads(i, tiles):
                for t in tiles:
                    for g in range(HG1):
                        mm = pe.transpose(TR[t][:, g * P:(g + 1) * P], attT[:, i, g, t * P:(t + 1) * P], ident)
                    mm.then_inc(S["att_turned"], 1)

            def step(p, h):
                att_block, sum_block, norm_block, route_block = (at(p, h, s) for s in (ATT, SUM, NORM, ROUTE))
                if att_block:
                    n, i, used = att_block
                    pe.wait_ge(att_in[i], used * 16 + 16)
                    wait_if_any(pe, S["normed"], (n - 1) * TPK + CD)
                    wait_if_any(pe, S["x3_copied"], (n - 2) * CD)
                    turn_heads(i, TURN_ORDER[:CD])
                if sum_block:
                    n, i, used = sum_block
                    pe.wait_ge(S["normed"], (n + 1) * TPK)
                    turn(TR, att[:, i], S["att2_turned"])
                if sum_block:
                    n, i, used = sum_block
                    if isinstance(n, int) and n == 0:
                        pe.wait_ge(w_in, 16 * (4 + CD))
                        pe.wait_ge(prep, PREP)
                    pe.wait_ge(S["att2_copied"], (n + 1) * CD)
                    wait_if_any(pe, S["summed"], n * TPK)
                    for t in range(TPK):
                        for c in range(CD):
                            mm = pe.matmul(PX[t // 2][:, t % 2 * DIM:(t % 2 + 1) * DIM], att2T[:, i, c, t * P:(t + 1) * P],
                                           wout[:, c, :], start=(c == 0), stop=(c == CD - 1))
                        mm.then_inc(S["projected"], 1)
                if norm_block:
                    n, i, used = norm_block
                    pe.wait_ge(S["x3_done"], (n + 1) * TPK)
                    if att_block:
                        pe.wait_ge(S["normed"], att_block[0] * TPK + CD)
                    turn(TR[CD:], x3[:, i], S["x3_turned"])
                if att_block:
                    n, i, used = att_block
                    turn_heads(i, TURN_ORDER[CD:])
                if route_block:
                    n, i, used = route_block
                    pe.wait_ge(S["counted"], n + 1)
                    for t in range(TPK):
                        pe.matmul(PR[:, t], before[:], chosen[:, t], start=True, stop=False)
                        mm = pe.matmul(PR[:, t], ones[:], count[:, i, t], start=False, stop=True)
                    mm.then_inc(S["ranks_ready"], 1)
                if norm_block:
                    n, i, used = norm_block
                    pe.wait_ge(S["x3_copied"], (n + 1) * CD)
                    for t in range(TPK):
                        for c in range(CD):
                            mm = pe.matmul(PL[:, t], x3T[:, i, c, t * P:(t + 1) * P], wrn[:, c, :], start=(c == 0),
                                           stop=(c == CD - 1))
                    mm.then_inc(S["logits_ready"], 1)

            steps(pe, step, ROUTE)

        @block.scalar
        def _(act):
            for i in range(2):
                act.sem_inc(x3_out[i], 16)
                act.sem_inc(route_out[i], 2 * 16)
            act.wait_ge(prep, PREP)

            def step(p, h):
                sum_block, norm_block, route_block = (at(p, h, s) for s in (SUM, NORM, ROUTE))
                if sum_block:
                    n, i, used = sum_block
                    for c in range(CD):
                        act.wait_ge(S["att2_turned"], n * CD + c + 1)
                        act.activation(att2T[:, i, c], TR[c][:], ACT.Copy).then_inc(S["att2_copied"], 1)
                if route_block:
                    n, i, used = route_block
                    act.wait_ge(S["step"], n * ROUTE_STEPS + 4)
                    act.activation(expd[:], below[:], ACT.Exp).then_inc(S["expd_done"], 1)
                if norm_block:
                    n, i, used = norm_block
                    act.wait_ge(S["rstd_done"], n + 1)
                    act.wait_ge(x3_out[i], used * 16 + 16)
                    wait_if_any(act, S["xn_done"], n)
                    for t in range(TPK):
                        act.activation(x3[:, i, t], s3[:, i, t], ACT.Identity, bias=shift[:, i, t:t + 1],
                                       scale=rstd[:, i, t:t + 1]).then_inc(S["x3_done"], 1)
                if norm_block:
                    n, i, used = norm_block
                    for t in range(TPK):
                        act.wait_ge(S["x3_done"], n * TPK + t + 1)
                        act.activation(square[:, t], x3[:, i, t], ACT.Square, accum_out=meansq[:, t:t + 1])\
                           .then_inc(S["squared"], 1)
                if route_block:
                    n, i, used = route_block
                    act.wait_ge(S["rrms_done"], n + 1)
                    act.wait_ge(S["xn_done"], n + 1)
                    for t in range(TPK):
                        act.activation(scaled3[:, t], x3[:, i, t], ACT.Copy, scale=rrms[:, i, t:t + 1])\
                           .then_inc(S["scaled3_done"], 1)
                if norm_block:
                    n, i, used = norm_block
                    for c in range(CD):
                        act.wait_ge(S["x3_turned"], n * CD + c + 1)
                        act.activation(x3T[:, i, c], TR[CD + c][:], ACT.Copy).then_inc(S["x3_copied"], 1)
                if sum_block:
                    n, i, used = sum_block
                    act.wait_ge(S["aggr"], (n + 1) * TPK)
                    act.activation(std[:, i], moments[:, i, :, 1], ACT.Sqrt, bias=eps[:, 0:1]).then_inc(S["std_done"], 1)
                if norm_block:
                    n, i, used = norm_block
                    act.wait_ge(S["squared"], (n + 1) * TPK)
                    act.activation(rms[:, i], meansq[:], ACT.Sqrt, bias=eps[:, 0:1], scale=1.0 / DIM)\
                       .then_inc(S["rms_done"], 1)

            steps(act, step, ROUTE)

        @block.vector
        def _(dve):
            dve.memset(eps[:], LN_EPS).then_inc(prep, 1)
            dve.memset(ones[:], 1.0)
            dve.memset(count[:], 0.0).then_inc(prep, 1)
            dve.tensor_copy(before[:], const[:, C_BEFORE:C_BEFORE + P]).then_inc(prep, 1)
            dve.wait_ge(w_in, 16 * (4 + CD))
            dve.tensor_tensor(wrn[:], wr[:], nwc[:].to_broadcast([P, CD, E]), ALU.mult).then_inc(prep, 1)
            dve.wait_ge(prep, PREP)

            def step(p, h):
                att_block, sum_block, norm_block, route_block = (at(p, h, s) for s in (ATT, SUM, NORM, ROUTE))
                done = 0

                def chain(instructions, meanwhile=None):
                    nonlocal done
                    done += 1
                    if route_block:
                        instructions()[-1].then_inc(S["step"], 1)
                    if meanwhile:
                        meanwhile()
                    if route_block:
                        dve.wait_ge(S["step"], route_block[0] * ROUTE_STEPS + done)

                def head(t):
                    return TR[t][:].rearrange("p (h c) -> p h c", h=H1)

                def head_sums(k):
                    if att_block:
                        n, i, used = att_block
                        dve.wait_ge(S["att_turned"], n * TPK + k + 1)
                        t = TURN_ORDER[k]
                        dve.reciprocal(rec[:, t], head(t)[:, :, D1]).then_inc(S["rec_done"], 1)

                def weigh_heads(k):
                    if att_block:
                        n, i, used = att_block
                        dve.wait_ge(S["rec_done"], n * TPK + k + 1)
                        t = TURN_ORDER[k]
                        dve.tensor_tensor(att[:, i, t].rearrange("p (h c) -> p h c", h=H1), head(t)[:, :, 0:D1],
                                          rec[:, t].unsqueeze(2).to_broadcast([P, H1, D1]), ALU.mult)\
                           .then_inc(S["normed"], 1)

                def first_heads():
                    for k in range(CD):
                        head_sums(k)
                    for k in range(CD):
                        weigh_heads(k)

                def residual(t):
                    if sum_block:
                        n, i, used = sum_block
                        if t == 0:
                            dve.wait_ge(x2_in[i], used * 16 + 16)
                        dve.wait_ge(S["projected"], n * TPK + t // 2 * 2 + 2)
                        dve.tensor_tensor(s3[:, i, t], x2[:, i, t], PX[t // 2][:, t % 2 * DIM:(t % 2 + 1) * DIM], ALU.add)\
                           .then_inc(S["summed"], 1)

                def statistics(t):
                    if sum_block:
                        n, i, used = sum_block
                        dve.wait_ge(S["summed"], n * TPK + t + 1)
                        dve.bn_stats(stats[:, t], s3[:, i, t]).then_inc(S["stat"], 1)

                if norm_block:
                    n, i, used = norm_block
                    dve.wait_ge(S["std_done"], n + 1)
                    dve.reciprocal(rstd[:, i], std[:, i]).then_inc(S["rstd_step"], 1)
                    dve.wait_ge(S["rstd_step"], n + 1)
                    dve.scalar_tensor_tensor(out=shift[:, i], in0=moments[:, i, :, 0], scalar=-1.0, in1=rstd[:, i],
                                             op0=ALU.mult, op1=ALU.mult).then_inc(S["rstd_done"], 1)
                if route_block:
                    n, i, used = route_block
                    dve.wait_ge(S["rms_done"], n + 1)
                    wait_if_any(dve, S["xn_done"], n)
                    dve.reciprocal(rrms[:, i], rms[:, i]).then_inc(S["rrms_done"], 1)
                    dve.wait_ge(S["rrms_done"], n + 1)
                    dve.wait_ge(S["logits_ready"], n + 1)
                chain(lambda: [dve.tensor_tensor(scaled[:], PL[:], rrms[:, i].unsqueeze(2).to_broadcast([P, TPK, E]),
                                                 ALU.mult)])
                chain(lambda: [dve.tensor_tensor(logits[:], scaled[:], br[:].unsqueeze(1).to_broadcast([P, TPK, E]),
                                                 ALU.add)])
                chain(lambda: [dve.tensor_reduce(top[:], logits[:], AX.X, ALU.max)])
                chain(lambda: [dve.tensor_tensor(below[:], logits[:], top[:].unsqueeze(2).to_broadcast([P, TPK, E]),
                                                 ALU.subtract)], first_heads)
                if route_block:
                    dve.wait_ge(S["expd_done"], n + 1)
                chain(lambda: [dve.tensor_reduce(total[:], expd[:], AX.X, ALU.add)])
                chain(lambda: [dve.reciprocal(rtotal[:], total[:])])
                chain(lambda: [dve.tensor_tensor(prob[:], expd[:], rtotal[:].unsqueeze(2).to_broadcast([P, TPK, E]), ALU.mult)])
                if route_block:
                    dve.sem_inc(seen, 1)
                chain(lambda: [dve.max(best[:, t], prob[:, t]) for t in range(TPK)])
                if route_block:
                    dve.sem_inc(seen, 1)
                chain(lambda: [dve.max_index(besti[:, t], best[:, t], prob[:, t]) for t in range(TPK)])
                chain(lambda: [dve.tensor_copy(expert[:], besti[:, :, 0:TOP_K])])
                flat = [P, TPK * TOP_K, E]
                chain(lambda: [dve.tensor_tensor(onehot[:].rearrange("p t k e -> p (t k) e"),
                                                 iota.unsqueeze(1).to_broadcast(flat),
                                                 expert[:].rearrange("p t k -> p (t k)").unsqueeze(2).to_broadcast(flat),
                                                 ALU.is_equal),
                               dve.tensor_scalar(copies[:], expert[:], float(E_COPY), None, ALU.is_equal),
                               dve.tensor_scalar(mlps[:], expert[:], float(E_MLP), None, ALU.is_ge)])
                chain(lambda: [dve.tensor_tensor(chosen[:], onehot[:, :, 0], onehot[:, :, 1], ALU.add),
                               dve.tensor_tensor(holds[:], copies[:], mlps[:], ALU.add)])
                for t in range(TPK):
                    chain(lambda: [dve.tensor_tensor(count[:, i, t + 1], count[:, i, t], chosen[:, t], ALU.add)],
                          lambda: residual(t))
                if route_block:
                    dve.tensor_copy(count[:, 1 - i, 0], count[:, i, TPK]).then_inc(S["counted"], 1)
                for t in range(TPK):
                    statistics(t)
                if sum_block:
                    n, i, used = sum_block
                    dve.wait_ge(S["stat"], (n + 1) * TPK)
                    dve.sem_inc(seen, 1)
                    for t in range(TPK):
                        dve.bn_aggr(moments[:, i, t], stats[:, t]).then_inc(S["aggr"], 1)
                if route_block:
                    n, i, used = route_block
                    dve.wait_ge(S["ranks_ready"], n + 1)
                chain(lambda: [dve.tensor_tensor(ranked[:, :, k], onehot[:, :, k], PR[:], ALU.mult) for k in range(TOP_K)],
                      lambda: head_sums(2))
                chain(lambda: [dve.tensor_reduce(rank[:], ranked[:], AX.X, ALU.add)], lambda: weigh_heads(2))
                chain(lambda: [dve.tensor_scalar(kept[:], rank[:], float(CAP), None, ALU.is_lt),
                               dve.tensor_scalar(place[:], rank[:], float(CAP - 1), None, ALU.min)], lambda: head_sums(3))
                chain(lambda: [dve.scalar_tensor_tensor(out=slot[:], in0=expert[:], scalar=float(CAP), in1=place[:],
                                                        op0=ALU.mult, op1=ALU.add),
                               dve.tensor_tensor(moves[:], holds[:], kept[:], ALU.mult),
                               dve.tensor_tensor(weight[:], best[:, :, 0:TOP_K], kept[:], ALU.mult)],
                      lambda: weigh_heads(3))
                if route_block:
                    dve.wait_ge(route_out[i], used * 32 + 32)
                    dve.wait_ge(S["xn_free"], n + 1)
                chain(lambda: [dve.tensor_scalar(target[:], moves[:], -NOWHERE, NOWHERE, ALU.mult, ALU.add),
                               dve.tensor_copy(from_slot[:, i], slot[:]),
                               dve.tensor_tensor(wsum[:], weight[:, :, 0], weight[:, :, 1], ALU.add)])
                chain(lambda: [dve.tensor_tensor(to_slot[:, i], target[:], slot[:], ALU.add),
                               dve.tensor_scalar(wzero[:], wsum[:], 0.0, None, ALU.is_le)])
                chain(lambda: [dve.tensor_tensor(divisor[:], wsum[:], wzero[:], ALU.add)])
                chain(lambda: [dve.reciprocal(rwsum[:], divisor[:])])
                if route_block:
                    dve.tensor_tensor(coef[:, i], weight[:], rwsum[:].unsqueeze(2).to_broadcast([P, TPK, TOP_K]), ALU.mult)\
                       .then_inc(S["routed"], 1)
                assert done == ROUTE_STEPS, done

            steps(dve, step, ROUTE)

        @block.gpsimd
        def _(pool):
            pool.sem_inc(S["xn_free"], 2)
            pool.sem_inc(S["xn_done"], 1)

            def step(p, h):
                if now := at(p, h, ROUTE):
                    n, i, used = now
                    pool.wait_ge(S["scaled3_done"], (n + 1) * TPK)
                    pool.sem_inc(pool_seen, 1)
                    pool.tensor_tensor(xn[:, i], scaled3[:], nw[:].unsqueeze(1).to_broadcast([P, TPK, DIM]), ALU.mult)\
                        .then_inc(S["xn_done"], 1)
                    if not isinstance(n, int) or n > 0:
                        pool.wait_ge(scattered, n * 16 * TPK * TOP_K)
                        pool.sem_inc(S["xn_free"], 1)
                    pool.wait_ge(S["xn_done"], n + 2)
                    pool.wait_ge(S["routed"], n + 1)
                    pool.sem_inc(pool_seen, 1)
                    for t in range(TPK):
                        for k in range(TOP_K):
                            pool.indirect_dma_start(out=d["slots"], out_offset=bass.IndirectOffsetOnAxis(
                                ap=to_slot[:, i, t, k:k + 1].bitcast(U32), axis=0), in_=xn[:, i, t], in_offset=None,
                                bounds_check=SLOTS - 1, oob_is_err=False).then_inc(scattered, 16)

            steps(pool, step, ROUTE)
            pool.wait_ge(scattered, BLOCKS * 16 * TPK * TOP_K)


ROUTE_STEPS = 24
FFN = 1024
FC = FFN // P


class ExpertWeights:

    def __init__(self, nc, ctx):
        a = Alloc(nc, ctx, "w")
        self.w1 = a.sb("w1", [P, 2, CD, FFN])
        self.w2 = a.sb("w2", [P, 2, FC, DIM])
        self.b1 = a.sb("b1", [P, 2, FC])
        self.b2 = a.sb("b2", [P, 2, DIM])
        self.w1_in = [a.sem(f"w1_in{i}") for i in range(2)]
        self.w2_in = [a.sem(f"w2_in{i}") for i in range(2)]

    def load_up(self, eng, d, one, i):
        eng.dma_start(self.w1[:, i], d["L1_ffn_fc1T"][one].rearrange("o (c p) f -> p (o c) f", p=P))\
           .then_inc(self.w1_in[i], 16)
        eng.dma_start(self.b1[:, i], d["L1_ffn_fc1_biasT"][one].rearrange("o p c -> p (o c)")).then_inc(self.w1_in[i], 16)

    def load_first(self, eng, d):
        for e in range(2):
            self.load_up(eng, d, bass.ds(e, 1), e)
            self.load_down(eng, d, bass.ds(e, 1), e)

    def load_down(self, eng, d, one, i):
        eng.dma_start(self.w2[:, i], d["L1_ffn_fc2T"][one].rearrange("o (c p) n -> p (o c) n", p=P))\
           .then_inc(self.w2_in[i], 16)
        eng.dma_start(self.b2[:, i], d["L1_ffn_fc2_bias"][one].to_broadcast([P, DIM])).then_inc(self.w2_in[i], 16)


def phase_experts(nc, d, keep, weights):
    ST = CAP // P
    with ExitStack() as ctx:
        a = Alloc(nc, ctx, "f")
        ident = keep["const"][:, C_IDENT:C_IDENT + P]
        w1, w2, b1, b2 = weights.w1, weights.w2, weights.b1, weights.b2
        w1_high, w1_low = (a.sb(f"w1_{half}", [P, CD, FFN], F32R) for half in ("high", "low"))
        w2_high, w2_low = (a.sb(f"w2_{half}", [P, 2, FC, DIM], F32R) for half in ("high", "low"))
        x = a.sb("x", [P, 2, ST, DIM])
        xT = a.sb("xT", [P, HALVES1, CD, CAP], F32R)
        h_high, h_low = (a.sb(f"h_{half}", [P, FC, CAP], F32R) for half in ("high", "low"))
        h = a.sb("h", [P, 4, CAP])
        y = a.sb("y", [P, 2, ST, DIM])
        TR = [a.ps(f"TR{i}", [P, CAP]) for i in range(CD)]
        PH = [a.ps(f"PH{i}", [P, CAP]) for i in range(4)]
        PY = [a.ps(f"PY{i}", [P, DIM]) for i in range(2)]
        x_in = [a.sem(f"x_in{i}") for i in range(2)]
        turned, x_high, x_low, w1_cut, w1_done, w2_cut, w2_done, h_ready, h_done, h_cut, h_left, y_ready, y_done = (
            a.sem(n) for n in ("turned", "x_high", "x_low", "w1_cut", "w1_done", "w2_cut", "w2_done", "h_ready", "h_done",
                               "h_cut", "h_left", "y_ready", "y_done"))
        y_out = [a.sem(f"y_out{i}") for i in range(2)]
        block = ctx.enter_context(nc.Block())

        def over_experts(eng, body):
            for i in range(2):
                body(0, i)
            with eng.Fori(1, MLPS // 2) as e:
                for i in range(2):
                    body(e, i)

        def is_first(s, i):
            return first(s) and i == 0

        @block.sync
        def _(sp):
            def load(s, i):
                n = s * 2 + i
                e = n if isinstance(s, int) else sp.snap(n)
                at = bass.ds(e * CAP + E_MLP * CAP if isinstance(s, int) else sp.snap(n * CAP + E_MLP * CAP), CAP)
                one = bass.ds(e, 1)
                if not first(s):
                    sp.wait_ge(turned, (n - 1) * CD)
                sp.dma_start(x[:, i], d["slots"][at, :].rearrange("(t p) c -> p t c", p=P)).then_inc(x_in[i], 16)
                if not first(s):
                    sp.wait_ge(h_cut, (n - 1) * FC)
                    weights.load_up(sp, d, one, i)
                    sp.wait_ge(y_done, (n - 1) * ST)
                    weights.load_down(sp, d, one, i)

            over_experts(sp, load)

        @block.tensor
        def _(pe):
            def turn(s, i):
                n = s * 2 + i
                pe.wait_ge(x_in[i], (s + 1) * 16)
                for c in range(CD):
                    if not is_first(s, i):
                        pe.wait_ge(x_low, (n - 1) * CD + c + 1)
                    for t in range(ST):
                        mm = pe.transpose(TR[c][:, t * P:(t + 1) * P], x[:, i, t, c * P:(c + 1) * P], ident)
                    mm.then_inc(turned, 1)

            def up(s, i):
                n = s * 2 + i
                pe.wait_ge(x_low, (n + 1) * CD)
                pe.wait_ge(w1_done, n + 1)
                for f in range(FC):
                    if not (is_first(s, i) and f < 4):
                        pe.wait_ge(h_cut, n * FC + f - 3)
                    at = slice(f * P, (f + 1) * P)
                    for k, (w, half) in enumerate(((w1_high, 0), (w1_high, 1), (w1_low, 0))):
                        for c in range(CD):
                            mm = pe.matmul(PH[f % 4][:], w[:, c, at], xT[:, half, c, :], start=(k == 0 and c == 0),
                                           stop=(k == 2 and c == CD - 1))
                    mm.then_inc(h_ready, 1)

            def down(n, i, new):
                pe.wait_ge(w2_done, n + 1)
                for t in range(ST):
                    if not (new and t < 2):
                        pe.wait_ge(y_done, n * ST + t - 1)
                    at = slice(t * P, (t + 1) * P)
                    for f in range(FC):
                        if t == 0:
                            pe.wait_ge(h_left, n * FC + f + 1)
                        for k, (hidden, w) in enumerate(((h_high, w2_high), (h_low, w2_high), (h_high, w2_low))):
                            mm = pe.matmul(PY[t % 2][:], hidden[:, f, at], w[:, i, f, :], start=(f == 0 and k == 0),
                                           stop=(f == FC - 1 and k == 2))
                    mm.then_inc(y_ready, 1)

            def body(s, i):
                turn(s, i)
                if not is_first(s, i):
                    down(s * 2 + i - 1, 1 - i, first(s) and i == 1)
                up(s, i)

            over_experts(pe, body)
            down(MLPS - 1, (MLPS - 1) % 2, False)

        @block.scalar
        def _(act):
            for i in range(2):
                act.sem_inc(y_out[i], 16)

            def store(n, i):
                at = bass.ds(n * CAP + E_MLP * CAP if isinstance(n, int) else act.snap(n * CAP + E_MLP * CAP), CAP)
                act.wait_ge(y_done, (n + 1) * ST)
                act.dma_start(d["slots"][at, :].rearrange("(t p) c -> p t c", p=P), y[:, i]).then_inc(y_out[i], 16)

            def body(s, i):
                n = s * 2 + i
                for c in range(CD):
                    act.wait_ge(turned, n * CD + c + 1)
                    act.activation(xT[:, 0, c], TR[c][:], ACT.Copy).then_inc(x_high, 1)
                for f in range(FC):
                    act.wait_ge(h_ready, n * FC + f + 1)
                    if not (is_first(s, i) and f < 4):
                        act.wait_ge(h_left, n * FC + f - 3)
                    act.activation(h[:, f % 4], PH[f % 4][:], ACT.Gelu, bias=b1[:, i, f:f + 1]).then_inc(h_done, 1)
                    act.activation(h_high[:, f], PH[f % 4][:], ACT.Gelu, bias=b1[:, i, f:f + 1]).then_inc(h_cut, 1)
                if not is_first(s, i):
                    store(n - 1, 1 - i)

            over_experts(act, body)
            store(MLPS - 1, (MLPS - 1) % 2)
            for i in range(2):
                act.wait_ge(y_out[i], 16 * (MLPS // 2 + 1))

        @block.vector
        def _(dve):
            def cut_weights(w, high, low, arrived, times, cut, done, n):
                def take_high():
                    dve.wait_ge(arrived, times)
                    dve.tensor_copy(high, w).then_inc(cut, 1)

                def leave_low():
                    dve.wait_ge(cut, n + 1)
                    dve.tensor_tensor(low, w, high.bitcast(F32), ALU.subtract).then_inc(done, 1)
                return [take_high, leave_low]

            def sums(n, i, t, stored_before):
                if t == 0:
                    dve.wait_ge(y_out[i], stored_before)
                dve.wait_ge(y_ready, n * ST + t + 1)
                dve.tensor_tensor(y[:, i, t], b2[:, i], PY[t % 2][:], ALU.add).then_inc(y_done, 1)

            def body(s, i):
                n = s * 2 + i
                for c in range(CD):
                    dve.wait_ge(x_high, n * CD + c + 1)
                    dve.tensor_tensor(xT[:, 1, c], TR[c][:], xT[:, 0, c].bitcast(F32), ALU.subtract).then_inc(x_low, 1)
                cuts = (cut_weights(w1[:, i], w1_high[:], w1_low[:], weights.w1_in[i], (s + 1) * 32, w1_cut, w1_done, n)
                        + cut_weights(w2[:, i], w2_high[:, i], w2_low[:, i], weights.w2_in[i], (s + 1) * 32, w2_cut, w2_done, n))
                for t in range(ST):
                    cuts[t]()
                    if not is_first(s, i):
                        sums(n - 1, 1 - i, t, s * 16 + 16 * i)
                for f in range(FC):
                    dve.wait_ge(h_cut, n * FC + f + 1)
                    dve.tensor_tensor(h_low[:, f], h[:, f % 4], h_high[:, f].bitcast(F32), ALU.subtract)\
                       .then_inc(h_left, 1)

            over_experts(dve, body)
            for t in range(ST):
                sums(MLPS - 1, (MLPS - 1) % 2, t, 16 * MLPS // 2)


def phase_combine(nc, d, keep):
    with ExitStack() as ctx:
        a = Alloc(nc, ctx, "g")
        NBUF = 4
        from_slot = a.sb("from_slot", [P, TILES * TOP_K], I32)
        coef = a.sb("coef", [P, TILES * TOP_K])
        x3 = a.sb("x3", [P, TILES, DIM])
        got = a.sb("got", [P, TILES, TOP_K, DIM])
        s4 = a.sb("s4", [P, NBUF, DIM])
        s5 = a.sb("s5", [P, NBUF, DIM])
        y = a.sb("y", [P, TILES, DIM])
        eps = a.sb("eps", [P, 1])
        stats = a.sb("stats", [P, TILES, 6])
        moments = a.sb("moments", [P, TILES, 2])
        std = a.sb("std", [P, TILES])
        rstd = a.sb("rstd", [P, TILES])
        idx_in, x3_in, prep, out_done = (a.sem(n) for n in ("idx_in", "x3_in", "prep", "out_done"))
        gathered = [a.sem(f"gathered{i}") for i in range(BLOCKS)]
        added, summed, stat, aggr, std_done, rstd_done, y_done = (
            a.sem(n) for n in ("added", "summed", "stat", "aggr", "std_done", "rstd_done", "y_done"))
        block = ctx.enter_context(nc.Block())

        @block.sync
        def _(sp):
            sp.dma_start(from_slot[:], d["from_slot"]).then_inc(idx_in, 16)
            sp.dma_start(coef[:], d["coef"]).then_inc(x3_in, 16)
            sp.dma_start(x3[:], d["x3"].rearrange("(t p) c -> p t c", p=P)).then_inc(x3_in, 16)
            for n in range(BLOCKS):
                sp.wait_ge(y_done, (n + 1) * TPK)
                sp.dma_start(d["out"][n * BLK:(n + 1) * BLK, :].rearrange("(t p) c -> p t c", p=P),
                             y[:, n * TPK:(n + 1) * TPK]).then_inc(out_done, 16)
            sp.wait_ge(out_done, 16 * BLOCKS)

        @block.gpsimd
        def _(pool):
            pool.wait_ge(idx_in, 16)
            for t in range(TILES):
                for k in range(TOP_K):
                    pool.indirect_dma_start(out=got[:, t, k], out_offset=None, in_=d["slots"],
                                            in_offset=bass.IndirectOffsetOnAxis(
                                                ap=from_slot[:, t * TOP_K + k:t * TOP_K + k + 1].bitcast(U32), axis=0),
                                            bounds_check=SLOTS - 1, oob_is_err=False).then_inc(gathered[t // TPK], 16)

        @block.scalar
        def _(act):
            act.wait_ge(prep, 1)
            for n in range(BLOCKS):
                act.wait_ge(aggr, (n + 1) * TPK)
                act.activation(std[:, n * TPK:(n + 1) * TPK], moments[:, n * TPK:(n + 1) * TPK, 1], ACT.Sqrt,
                               bias=eps[:, 0:1]).then_inc(std_done, 1)

        @block.vector
        def _(dve):
            dve.memset(eps[:], LN_EPS).then_inc(prep, 1)
            dve.wait_ge(x3_in, 32)
            for n in range(BLOCKS):
                tiles = range(n * TPK, (n + 1) * TPK)
                dve.wait_ge(gathered[n], 16 * TPK * TOP_K)
                for t in tiles:
                    dve.scalar_tensor_tensor(out=s4[:, t % NBUF], in0=got[:, t, 0], scalar=coef[:, 2 * t:2 * t + 1],
                                             in1=x3[:, t], op0=ALU.mult, op1=ALU.add).then_inc(added, 1)
                for t in tiles:
                    dve.wait_ge(added, t + 1)
                    dve.scalar_tensor_tensor(out=s5[:, t % NBUF], in0=got[:, t, 1], scalar=coef[:, 2 * t + 1:2 * t + 2],
                                             in1=s4[:, t % NBUF], op0=ALU.mult, op1=ALU.add).then_inc(summed, 1)
                for t in tiles:
                    dve.wait_ge(summed, t + 1)
                    dve.bn_stats(stats[:, t], s5[:, t % NBUF]).then_inc(stat, 1)
                for t in tiles:
                    dve.wait_ge(stat, t + 1)
                    dve.bn_aggr(moments[:, t], stats[:, t]).then_inc(aggr, 1)
                dve.wait_ge(std_done, n + 1)
                dve.reciprocal(rstd[:, n * TPK:(n + 1) * TPK], std[:, n * TPK:(n + 1) * TPK]).then_inc(rstd_done, 1)
                dve.wait_ge(rstd_done, n + 1)
                for t in tiles:
                    dve.tensor_scalar(y[:, t], s5[:, t % NBUF], moments[:, t, 0:1], rstd[:, t:t + 1], ALU.subtract,
                                      ALU.mult).then_inc(y_done, 1)


def program(nc, d):
    with ExitStack() as ctx:
        keep = {"const": ctx.enter_context(nc.sbuf_tensor("const", [P, C_COLS], F32))}
        phase_qkv0(nc, d, keep)
        with ExitStack() as layer0:
            weights = Layer0Weights(nc, layer0)
            phase_attention0(nc, d, keep, weights)
            phase_ffn0(nc, d, keep, weights)
        with ExitStack() as experts:
            weights = ExpertWeights(nc, experts)
            phase_attention1(nc, d, keep, weights)
            phase_route(nc, d, keep, weights)
            phase_experts(nc, d, keep, weights)
        phase_combine(nc, d, keep)


def layout(inputs):
    a = {name: np.ascontiguousarray(inputs[name]) for name in inputs}
    out = {"constants": constants()}
    x = a["L0_attn_x"].reshape(TOKENS, DIM)
    out["x"] = x
    out["xT"] = x.T
    out["L0_wqkvT"] = a["L0_attn_w_qkv"].T
    out["L0_wprojT"] = a["L0_attn_w_proj"].T
    for name in ("b_proj", "q_gamma", "q_beta", "k_gamma", "k_beta"):
        out["L0_attn_" + name] = a["L0_attn_" + name]
    for name in ("w_gate", "w_up", "w_down"):
        out["L0_ffn_" + name + "T"] = a["L0_ffn_" + name].T
    for name in ("L1_attn_w_qkv", "L1_attn_w_out", "L1_attn_head_scales", "L1_ffn_norm_weight", "L1_ffn_router_bias",
                 "L1_ffn_fc2_bias", "L1_ffn_constant_vectors"):
        out[name] = a[name]
    out["L1_ffn_router_weightT"] = a["L1_ffn_router_weight"].T
    out["L1_ffn_fc1_biasT"] = a["L1_ffn_fc1_bias"].reshape(MLPS, FC, P).transpose(0, 2, 1)
    out["L1_ffn_fc1T"] = a["L1_ffn_fc1_weight"].transpose(0, 2, 1)
    out["L1_ffn_fc2T"] = a["L1_ffn_fc2_weight"].transpose(0, 2, 1)
    return {name: np.ascontiguousarray(v) for name, v in out.items()}


SCRATCH = {
    "qk0": ([PARTS * QK_BLK, P, TOKENS], BF16),
    "v0": ([TOKENS, H0 * VS0], F32),
    "att0": ([HG0, P, TOKENS], F32),
    "x2": ([TOKENS, DIM], F32),
    "qk1": ([HALVES1 * 4, P, TOKENS], F32),
    "v1": ([TOKENS, H1 * VS1], F32),
    "att1": ([HG1, P, TOKENS], F32),
    "x3": ([TOKENS, DIM], F32),
    "from_slot": ([P, TILES * TOP_K], I32),
    "coef": ([P, TILES * TOP_K], F32),
    "slots": ([E * CAP, DIM], F32),
}


def kernel(**inputs):
    import concourse.bacc as bacc
    from concourse.bass_utils import run_bass_kernel_spmd

    nc = bacc.Bacc("TRN2", target_bir_lowering=False, num_devices=1)
    arrays = layout(inputs)
    d = {name: nc.dram_tensor(name, v.shape, mybir.dt.from_np(v.dtype), kind="ExternalInput").ap()
         for name, v in arrays.items()}
    for name, (shape, dt) in SCRATCH.items():
        d[name] = nc.dram_tensor(name, shape, dt).ap()
    d["out"] = nc.dram_tensor("out", [TOKENS, DIM], F32, kind="ExternalOutput").ap()
    program(nc, d)
    result = run_bass_kernel_spmd(nc, [arrays], core_ids=[0])
    return result.results[0]["out"].reshape(BATCH, SEQ, DIM)
```

```python
from contextlib import ExitStack

import numpy as np
import concourse.bass as bass
from concourse import mybir

F32 = mybir.dt.float32
BF16 = mybir.dt.bfloat16
I32 = mybir.dt.int32
U32 = mybir.dt.uint32
ALU = mybir.AluOpType
ACT = mybir.ActivationFunctionType
AX = mybir.AxisListType

P = 128
BATCH, SEQ, DIM = 4, 1024, 256
TOKENS = BATCH * SEQ
TILES = TOKENS // P
TPB = SEQ // P
CD = DIM // P
BLK = 512
TPK = BLK // P
BLOCKS = TOKENS // BLK
PARTS = 3
COMBOS = [(0, 0), (0, 1), (0, 2), (1, 0), (1, 1), (2, 0)]
MASKED = -1.0e30
LN_EPS = 1e-5

E, CAP = 16, 512
SLOT_COLS = 256 + 2
H0, D0 = 16, 16
G0 = 4
HG0 = H0 // G0
QK0_EPS = 1e-6
VS0 = 32
QK_COLS = 2 * H0 * D0
QK_BLK = QK_COLS // P

C_IDENT, C_MASK_Q, C_MASK_K, C_BEFORE, C_COS, C_SIN, C_IOTA, C_DIRS, C_NAMES = np.cumsum(
    [0, P, P, P, P, TPB * D0, TPB * D0, 16, 24]).tolist()
C_COLS = C_NAMES + 16


def constants():
    c = np.zeros((P, C_COLS), np.float32)
    i = np.arange(P)
    c[:, C_IDENT:C_IDENT + P] = np.eye(P)
    c[:, C_MASK_Q:C_MASK_Q + P] = np.where(i[None, :] > i[:, None], MASKED, 0.0)
    c[:, C_MASK_K:C_MASK_K + P] = np.where(i[None, :] < i[:, None], MASKED, 0.0)
    c[:, C_BEFORE:C_BEFORE + P] = i[:, None] < i[None, :]
    half = D0 // 2
    inv_freq = np.float32(1.0) / np.float32(10000.0) ** (np.arange(half, dtype=np.float32) / np.float32(half))
    freqs = np.outer(np.arange(SEQ, dtype=np.float32), inv_freq.astype(np.float32)).astype(np.float32)
    cos = np.cos(np.concatenate([freqs, freqs], -1)).astype(np.float32)
    sin = np.sin(np.concatenate([-freqs, freqs], -1)).astype(np.float32)
    for at, table in ((C_COS, cos), (C_SIN, sin)):
        c[:, at:at + TPB * D0] = table.reshape(TPB, P, D0).transpose(1, 0, 2).reshape(P, TPB * D0)
    c[:, C_IOTA:C_IOTA + 16] = np.arange(16)
    dirs = np.array([[(n >> 2 & 1) * 2 - 1, (n >> 1 & 1) * 2 - 1, (n & 1) * 2 - 1] for n in range(8)], np.float32)
    c[:, C_DIRS:C_DIRS + 24] = (dirs / np.sqrt(3.0, dtype=np.float32)).reshape(1, 24)
    block, tile = np.meshgrid(np.arange(-2, 0), np.arange(TPK), indexing="ij")
    c[:, C_NAMES:C_NAMES + 2 * TPK] = ((block * BLK + tile * P).ravel()[None, :] + i[:, None]) * 2 + 1
    return c


class Alloc:

    def __init__(self, nc, ctx, phase):
        self.nc, self.ctx, self.phase = nc, ctx, phase
        self.sems = []
        ctx.callback(self.clear)

    def sb(self, name, shape, dt=F32):
        return self.ctx.enter_context(self.nc.sbuf_tensor(f"{self.phase}_{name}", shape, dt))

    def ps(self, name, shape, dt=F32):
        return self.ctx.enter_context(self.nc.psum_tensor(f"{self.phase}_{name}", shape, dt))

    def sem(self, name):
        self.sems.append(self.nc.alloc_semaphore(f"{self.phase}_{name}"))
        return self.sems[-1]

    def clear(self):
        self.nc.clear_and_free_semaphores(self.sems)
        self.nc.all_engine_barrier()


def phase_qkv0(nc, d, keep, stacks):
    with ExitStack() as ctx:
        a = Alloc(nc, ctx, "a")
        const = keep["const"]
        ident = const[:, C_IDENT:C_IDENT + P]
        wT = a.sb("wT", [P, CD, 3 * DIM])
        wmean = a.sb("wmean", [P, CD, 2 * H0])
        gb = a.sb("gb", [P, 4, D0])
        gbs = a.sb("gbs", [P, 4, D0])
        ropeA = a.sb("ropeA", [P, TPB, 2, D0])
        ropeB = a.sb("ropeB", [P, TPB, 2, D0])
        ropeC = a.sb("ropeC", [P, TPB, 2, D0])
        ropeD = a.sb("ropeD", [P, TPB, 2, D0])
        eps = a.sb("eps", [P, 1])
        xT = a.sb("xT", [P, 2, CD, BLK])
        sq = a.sb("sq", [P, 2, QK_COLS])
        ss = a.sb("ss", [P, 2, 2 * H0])
        std = a.sb("std", [P, 2, 2 * H0])
        rstd = a.sb("rstd", [P, 2, 2 * H0])
        z = a.sb("z", [P, 4, 2, H0, D0])
        za = a.sb("za", [P, 2, 2, H0, D0])
        zb = a.sb("zb", [P, 2, 2, H0, D0])
        zs = a.sb("zs", [P, 2, 2, H0, D0])
        y = a.sb("y", [P, 4, QK_COLS])
        rest = a.sb("rest", [P, 2, QK_BLK, P])
        parts = a.sb("parts", [P, 2, PARTS, QK_BLK, BLK], BF16)
        vaug = a.sb("vaug", [P, 4, H0, VS0])
        QK = [a.ps(f"QK{i}", [P, QK_COLS]) for i in range(2)]
        V = [a.ps(f"V{i}", [P, DIM]) for i in range(2)]
        YT = [a.ps(f"YT{i}", [P, QK_BLK, P]) for i in range(2)]

        w_in = a.sem("w_in")
        x_in = [a.sem(f"x_in{i}") for i in range(2)]
        prep = a.sem("prep")
        ones_set = a.sem("ones_set")
        qk_ready, v_ready, v_free = a.sem("qk_ready"), a.sem("v_ready"), a.sem("v_free")
        sq_done, red_done, std_done, rstd_done = (a.sem(n) for n in ("sq_done", "red_done", "std_done", "rstd_done"))
        z_done, za_done, zb_done, zs_done, y_done = (a.sem(n) for n in ("z_done", "za_done", "zb_done", "zs_done", "y_done"))
        yt_ready, hi_done, rest_done, mid_done, lo_done = (
            a.sem(n) for n in ("yt_ready", "hi_done", "rest_done", "mid_done", "lo_done"))
        v_done = a.sem("v_done")
        parts_out = [a.sem(f"parts_out{i}") for i in range(2)]
        v_out = [a.sem(f"v_out{i}") for i in range(4)]
        LAG = 3
        block = ctx.enter_context(nc.Block())

        @block.sync
        def _(sp):
            sp.dma_start(wT[:], d["L0_wqkvT"].rearrange("(c p) n -> p c n", p=P)).then_inc(w_in, 16)
            sp.dma_start(const[:], d["constants"]).then_inc(w_in, 16)
            for i, name in enumerate(("q_gamma", "q_beta", "k_gamma", "k_beta")):
                row = d["L0_attn_" + name].rearrange("(o n) -> o n", o=1)
                sp.dma_start(gb[:, i, :], row.to_broadcast([P, D0])).then_inc(w_in, 16)

            def load(b, h):
                if b > 0:
                    sp.wait_ge(v_ready, (b - 1) * TPB + (h + 1) * TPK)
                src = d["xT"][:, bass.ds(b * SEQ + h * BLK, BLK)].rearrange("(c p) n -> p c n", p=P)
                sp.dma_start(xT[:, h], src).then_inc(x_in[h], 16)

            def store(b, h, pieces=1):
                for k in range(pieces):
                    sp.wait_ge(lo_done, b * TPB + h * TPK + (k + 1) * TPK // pieces)
                    at = slice(k * BLK // pieces, (k + 1) * BLK // pieces)
                    first_tok = b * SEQ + h * BLK
                    dst = d["qk0"][:, :, first_tok + at.start:first_tok + at.stop].rearrange("a p n -> p a n")
                    sp.dma_start(dst, parts[:, h].rearrange("p s k n -> p (s k) n")[:, :, at]).then_inc(parts_out[h], 16)

            def load_attention():
                for i in range(4):
                    sp.wait_ge(v_out[i], 16 * TPB // 4)
                for h in range(2):
                    sp.wait_ge(parts_out[h], 16 + 16)
                for hg in range(stacks.EARLY):
                    stacks.load(sp, d, 0, hg)

            for h in range(2):
                load(0, h)
            for b in range(BATCH):
                for h in range(2):
                    if b + 1 < BATCH:
                        load(b + 1, h)
                    if (b, h) == (1, 0):
                        load_attention()
                    store(b, h, 2 if (b, h) == (BATCH - 1, 1) else 1)
            for h in range(2):
                sp.wait_ge(parts_out[h], 16 * (BATCH + 1 + h))

        @block.gpsimd
        def _(pool):
            pool.wait_ge(prep, 14)

            def steps(b, lo, hi):
                for k in range(lo, hi):
                    n = b * TPB + k
                    if k < TPB:
                        pool.wait_ge(z_done, n + 1)
                        tab = ropeA[:, k % TPB].unsqueeze(2).to_broadcast([P, 2, H0, D0])
                        pool.tensor_tensor(za[:, k % 2], z[:, k % 4], tab, ALU.mult).then_inc(za_done, 1)
                    m = k - 1
                    if (not first(b) or m >= 0) and m < TPB:
                        pool.wait_ge(zs_done, n)
                        if not (first(b) and m < 4):
                            pool.wait_ge(yt_ready, n - 4)
                        tab = ropeC[:, m % TPB].unsqueeze(2).to_broadcast([P, 2, H0, D0])
                        out = y[:, m % 4].rearrange("p (x h c) -> p x h c", x=2, h=H0)
                        pool.tensor_tensor(out, zs[:, m % 2], tab, ALU.add).then_inc(y_done, 1)
                    m = k - 3
                    if (not first(b) or m >= 0) and m < TPB:
                        pool.wait_ge(mid_done, n - 2)
                        t = m % TPB
                        at = parts[:, t // TPK, :, :, (t % TPK) * P:(t % TPK + 1) * P]
                        pool.tensor_tensor(at[:, 2], rest[:, m % 2], at[:, 1], ALU.subtract).then_inc(lo_done, 1)

            pipeline(pool, steps, LAG)

        @block.tensor
        def _(pe):
            pe.wait_ge(prep, 6)

            def qk(b, t):
                n = b * TPB + t
                h, at = t // TPK, (t % TPK) * P
                if t % TPK == 0:
                    pe.wait_ge(x_in[h], b * 16 + 16)
                if not (first(b) and t < 2):
                    pe.wait_ge(z_done, n - 1)
                for c in range(CD):
                    mm = pe.matmul(QK[t % 2][:], xT[:, h, c, at:at + P], wT[:, c, 0:QK_COLS],
                                   start=(c == 0), stop=(c == CD - 1))
                mm.then_inc(qk_ready, 1)

            def values(b, t):
                n = b * TPB + t
                h, at = t // TPK, (t % TPK) * P
                if not (first(b) and t < 2):
                    pe.wait_ge(v_done, n - 1)
                for c in range(CD):
                    mm = pe.matmul(V[t % 2][:], xT[:, h, c, at:at + P], wT[:, c, QK_COLS:3 * DIM],
                                   start=(c == 0), stop=(c == CD - 1))
                mm.then_inc(v_ready, 1)

            def turn(b, t):
                n = b * TPB + t
                pe.wait_ge(y_done, n + 1)
                if not (first(b) and t < 2):
                    pe.wait_ge(rest_done, n - 1)
                for i in range(QK_BLK):
                    mm = pe.transpose(YT[t % 2][:, i], y[:, t % 4, i * P:(i + 1) * P], ident)
                mm.then_inc(yt_ready, 1)

            def steps(b, lo, hi):
                for k in range(lo, hi):
                    if k < TPB:
                        qk(b, k)
                    m = k - 3
                    if (not first(b) or m >= 0) and m < TPB:
                        if m >= 0:
                            turn(b, m)
                        else:
                            turn(b - 1, m + TPB)
                    if k < TPB:
                        values(b, k)

            pipeline(pe, steps, LAG)

        @block.scalar
        def _(act):
            for h in range(2):
                act.sem_inc(parts_out[h], 16)
            act.wait_ge(prep, 14)

            def steps(b, lo, hi):
                for k in range(lo, hi):
                    n = b * TPB + k
                    old = not (first(b) and k < 3) and k - 3 < TPB
                    t = (k - 3) % TPB
                    at = parts[:, t // TPK, :, :, (t % TPK) * P:(t % TPK + 1) * P]
                    if k < TPB:
                        act.wait_ge(qk_ready, n + 1)
                        if not (first(b) and k < 2):
                            act.wait_ge(red_done, n - 1)
                        act.activation(sq[:, k % 2], QK[k % 2][:], ACT.Square).then_inc(sq_done, 1)
                    if old:
                        act.wait_ge(yt_ready, n - 2)
                        if t % TPK == 0:
                            act.wait_ge(parts_out[t // TPK], b * 16 + 16 if k >= 3 else b * 16)
                        act.activation(at[:, 0], YT[t % 2][:], ACT.Copy).then_inc(hi_done, 1)
                    if k < TPB:
                        act.wait_ge(red_done, n + 1)
                        act.activation(std[:, k % 2], ss[:, k % 2], ACT.Sqrt, bias=eps[:, 0:1],
                                       scale=1.0 / D0).then_inc(std_done, 1)
                        act.wait_ge(v_ready, n + 1)
                        if not (first(b) and k < 4):
                            act.wait_ge(v_out[k % 4], (b * 2 + k // 4) * 16)
                        act.activation(vaug[:, k % 4, :, 0:D0], V[k % 2][:].rearrange("p (h c) -> p h c", h=H0),
                                       ACT.Copy).then_inc(v_done, 1)
                        act.wait_ge(v_done, n + 1)
                        act.dma_start(d["v0"][bass.ds(b * SEQ + k * P, P), :],
                                      vaug[:, k % 4].rearrange("p h c -> p (h c)")).then_inc(v_out[k % 4], 16)
                    if old:
                        act.wait_ge(rest_done, n - 2)
                        act.activation(at[:, 1], rest[:, t % 2], ACT.Copy).then_inc(mid_done, 1)

            pipeline(act, steps, LAG)
            for i in range(4):
                act.wait_ge(v_out[i], 16 * TILES // 4)

        @block.vector
        def _(dve):
            dve.memset(eps[:], QK0_EPS).then_inc(prep, 1)
            for i in range(4):
                last = dve.memset(vaug[:, i], 0.0)
            last.then_inc(ones_set, 1)
            dve.wait_ge(ones_set, 1)
            dve.memset(vaug[:, :, :, D0:D0 + 1], 1.0).then_inc(prep, 1)
            dve.wait_ge(w_in, 16 * 6)
            half = D0 // 2
            dve.tensor_copy(gbs[:, :, 0:half], gb[:, :, half:D0])
            dve.tensor_copy(gbs[:, :, half:D0], gb[:, :, 0:half]).then_inc(ones_set, 1)
            dve.wait_ge(ones_set, 2)
            for c in range(CD):
                last = dve.tensor_reduce(wmean[:, c], wT[:, c, 0:QK_COLS].rearrange("p (h c) -> p h c", c=D0),
                                         AX.X, ALU.add)
            last.then_inc(prep, 1)
            for x in range(2):
                if x == 0:
                    for g in (gb, gbs):
                        last = dve.tensor_scalar(g[:, 0:2], g[:, 0:2], float(D0) ** -0.5, None, ALU.mult)
                    last.then_inc(prep, 1)
            dve.wait_ge(prep, 4)
            dve.tensor_scalar(wmean[:], wmean[:], 1.0 / D0, None, ALU.mult).then_inc(prep, 1)
            dve.wait_ge(prep, 5)
            for c in range(CD):
                w = wT[:, c, 0:QK_COLS].rearrange("p (h c) -> p h c", c=D0)
                last = dve.tensor_tensor(w, w, wmean[:, c].unsqueeze(2).to_broadcast([P, 2 * H0, D0]), ALU.subtract)
            last.then_inc(prep, 1)
            cos = const[:, C_COS:C_COS + TPB * D0].rearrange("p (t c) -> p t c", t=TPB)
            sin = const[:, C_SIN:C_SIN + TPB * D0].rearrange("p (t c) -> p t c", t=TPB)
            for x in range(2):
                def row(g, i):
                    return g[:, 2 * x + i].unsqueeze(1).to_broadcast([P, TPB, D0])
                dve.tensor_tensor(ropeA[:, :, x], cos, row(gb, 0), ALU.mult).then_inc(prep, 1)
                dve.tensor_tensor(ropeB[:, :, x], sin, row(gbs, 0), ALU.mult).then_inc(prep, 1)
                dve.tensor_tensor(ropeC[:, :, x], cos, row(gb, 1), ALU.mult).then_inc(prep, 1)
                dve.tensor_tensor(ropeD[:, :, x], sin, row(gbs, 1), ALU.mult).then_inc(ones_set, 1)
                dve.wait_ge(prep, 9 + 4 * x)
                dve.wait_ge(ones_set, 3 + x)
                dve.tensor_tensor(ropeC[:, :, x], ropeC[:, :, x], ropeD[:, :, x], ALU.add).then_inc(prep, 1)
            dve.wait_ge(prep, 14)
            half = D0 // 2

            def steps(b, lo, hi):
                for k in range(lo, hi):
                    n = b * TPB + k
                    if k < TPB:
                        dve.wait_ge(sq_done, n + 1)
                        if not (first(b) and k < 2):
                            dve.wait_ge(std_done, n - 1)
                        dve.tensor_reduce(ss[:, k % 2], sq[:, k % 2].rearrange("p (h c) -> p h c", c=D0), AX.X,
                                          ALU.add).then_inc(red_done, 1)
                    if not (first(b) and k < 3) and k - 3 < TPB:
                        t = (k - 3) % TPB
                        at = parts[:, t // TPK, :, :, (t % TPK) * P:(t % TPK + 1) * P]
                        dve.wait_ge(hi_done, n - 2)
                        if not (first(b) and k < 5):
                            dve.wait_ge(lo_done, n - 4)
                        dve.tensor_tensor(rest[:, t % 2], YT[t % 2][:], at[:, 0], ALU.subtract).then_inc(rest_done, 1)
                    if k < TPB:
                        dve.wait_ge(std_done, n + 1)
                        dve.reciprocal(rstd[:, k % 2], std[:, k % 2]).then_inc(rstd_done, 1)
                        dve.wait_ge(rstd_done, n + 1)
                        dve.tensor_tensor(z[:, k % 4].rearrange("p x h c -> p (x h) c"),
                                          QK[k % 2][:].rearrange("p (h c) -> p h c", c=D0),
                                          rstd[:, k % 2].unsqueeze(2).to_broadcast([P, 2 * H0, D0]),
                                          ALU.mult).then_inc(z_done, 1)
                        dve.wait_ge(z_done, n + 1)
                        tab = ropeB[:, k].unsqueeze(2).to_broadcast([P, 2, H0, D0])
                        zk, zbk = z[:, k % 4], zb[:, k % 2]
                        dve.tensor_tensor(zbk[:, :, :, 0:half], zk[:, :, :, half:D0], tab[:, :, :, 0:half], ALU.mult)
                        dve.tensor_tensor(zbk[:, :, :, half:D0], zk[:, :, :, 0:half], tab[:, :, :, half:D0],
                                          ALU.mult).then_inc(zb_done, 1)
                    m = k - 1
                    if (not first(b) or m >= 0) and m < TPB:
                        dve.wait_ge(za_done, n)
                        dve.wait_ge(zb_done, n)
                        if not (first(b) and m < 2):
                            dve.wait_ge(y_done, n - 2)
                        dve.tensor_tensor(zs[:, m % 2], za[:, m % 2], zb[:, m % 2], ALU.add).then_inc(zs_done, 1)

            pipeline(dve, steps, LAG)


def first(b):
    return isinstance(b, int) and b == 0


def pipeline(eng, steps, lag):
    steps(0, 0, TPB)
    with eng.Fori(1, BATCH) as b:
        steps(b, 0, TPB)
    steps(BATCH, 0, 0) if lag == 0 else tail(steps, lag)


def tail(steps, lag):
    steps(BATCH - 1, TPB, TPB + lag)


class Stacks0:
    EARLY = 1

    def __init__(self, nc, ctx):
        a = Alloc(nc, ctx, "s")
        self.q, self.k, self.v, self.qk_in, self.v_in = [], [], [], [], []
        self.add(a, range(self.EARLY))

    def add(self, a, buffers):
        for i in buffers:
            self.q.append(a.sb(f"qst{i}", [P, G0, SEQ], BF16))
            self.k.append(a.sb(f"kst{i}", [P, G0, SEQ], BF16))
            self.v.append(a.sb(f"vst{i}", [P, TPB, G0, VS0]))
            self.qk_in.append(a.sem(f"q_in{i}"))
            self.v_in.append(a.sem(f"v_in{i}"))

    def load(self, sp, d, b, hg):
        tok = bass.ds(b * SEQ, SEQ)
        for stack, side, first_blk in ((self.q, 0, 0), (self.k, 1, QK_BLK // 2)):
            for s, combo in enumerate(COMBOS):
                rows = d["qk0"][combo[side] * QK_BLK + first_blk + hg // 2, (hg % 2) * 64:(hg % 2) * 64 + 64, tok]
                sp.dma_start(stack[hg][s * D0:(s + 1) * D0], rows.rearrange("(j p) n -> p j n", p=D0))\
                  .then_inc(self.qk_in[hg], 16)
        src = d["v0"][tok, hg * G0 * VS0:(hg + 1) * G0 * VS0].rearrange("(t p) c -> p t c", p=P)
        sp.dma_start(self.v[hg][:].rearrange("p t j c -> p t (j c)"), src).then_inc(self.v_in[hg], 16)


def phase_attention0(nc, d, keep, weights, stacks):
    HALVES = SEQ // BLK
    ROUNDS = HALVES * TPB
    UNITS = ROUNDS * G0
    MAXES = G0 * TPB * HALVES
    AHEAD = 5 * G0
    TURN = (MAXES - AHEAD) // G0 + 1
    RING = 16
    SBANKS, MBANKS = 3, 4
    K = len(COMBOS) * D0
    TURNS = MAXES // MBANKS
    KM = K + PARTS
    BUFS = HG0
    ROW_DMAS = 16 * G0
    ZERO_ROWS = 4
    with ExitStack() as ctx:
        a = Alloc(nc, ctx, "b")
        stacks.add(a, range(stacks.EARLY, BUFS))
        qst, kst, vst, q_in, v_in = stacks.q, stacks.k, stacks.v, stacks.qk_in, stacks.v_in
        probs = a.sb("probs", [P, RING, BLK])
        outT = a.sb("outT", [P, HALVES, BLK])
        mx = a.sb("mx", [P, G0, TPB, HALVES])
        m = a.sb("m", [P, G0, TPB])
        mrest = a.sb("mrest", [P, G0, TPB])
        mparts = a.sb("mparts", [P, TPB, G0, 32], BF16)
        mrows = a.sb("mrows", [P, SEQ], BF16)
        identb = a.sb("identb", [P, P], BF16)
        zero = a.sb("zero", [P, ZERO_ROWS * SLOT_COLS])
        PM = [a.ps(f"PM{i}", [P, BLK]) for i in range(MBANKS)]
        PS = [a.ps(f"PS{i}", [P, BLK]) for i in range(SBANKS)]
        PO = a.ps("PO", [P, BLK])
        PT = PM[MBANKS - 1][:].bitcast(BF16)

        setup, ones_set = a.sem("setup"), a.sem("ones_set")
        max_scores = a.sem("max_scores")
        max_taken = [a.sem(f"max_taken{i}") for i in range(MBANKS)]
        m_step, m_parts, m_turned, m_copied, rows_in = (
            a.sem(n) for n in ("m_step", "m_parts", "m_turned", "m_copied", "rows_in"))
        scores, exped, pv_done, out_copied = (a.sem(n) for n in ("scores", "exped", "pv_done", "out_copied"))
        out_stored = [a.sem(f"out_stored{i}") for i in range(HALVES)]
        zeroed, zero_out = a.sem("zeroed"), a.sem("zero_out")
        block = ctx.enter_context(nc.Block())

        def over_groups(eng, body):
            with eng.Fori(0, BATCH - 1) as b:
                for hg in range(HG0):
                    body(b, hg, 2)
            for hg in range(HG0):
                body(BATCH - 1, hg, min(2, HG0 - 1 - hg))

        @block.sync
        def _(sp):
            def rows(g, nxt):
                sp.wait_ge(m_copied, g + 1)
                for j in range(G0):
                    sp.dma_start(qst[nxt][K:KM, j, :], mrows[32 * j:32 * j + PARTS, :]).then_inc(rows_in, 16)

            def store(b, g, hg, half):
                sp.wait_ge(out_copied, g * HALVES + half + 2)
                sp.dma_start(d["att0"][hg, :, bass.ds(b * SEQ + half * BLK, BLK)], outT[:, half])\
                  .then_inc(out_stored[half], 16)

            def group(b, hg, left):
                g = b * HG0 + hg
                store(b, g, hg, 0)
                if left:
                    rows(g + 1, (hg + 1) % BUFS)
                store(b, g, hg, 1)
                if not isinstance(b, int):
                    sp.wait_ge(pv_done, (g + 1) * ROUNDS + RING // G0)
                    stacks.load(sp, d, b + 1, hg)

            for hg in range(stacks.EARLY, HG0):
                stacks.load(sp, d, 0, hg)
            rows(0, 0)
            over_groups(sp, group)
            for half in range(HALVES):
                sp.wait_ge(out_stored[half], 16 * (BATCH * HG0 + 1))

        @block.gpsimd
        def _(pool):
            for i in range(BUFS):
                pool.memset(kst[i][K:KM], 1.0).then_inc(ones_set, 1)
            pool.wait_ge(ones_set, BUFS)
            pool.wait_ge(v_in[HG0 - 1], 16)
            weights.prepare(a, pool, d, keep["const"])
            pool.memset(zero[:], 0.0).then_inc(zeroed, 1)
            pool.wait_ge(zeroed, 1)
            sent = 0
            for rows, count in ((d["slots"], E * CAP), (d["answers"], TOKENS * TOP_K)):
                blocks = rows.rearrange("(n p r) c -> n p (r c)", p=P, r=ZERO_ROWS)
                for n in range(count // (P * ZERO_ROWS)):
                    if sent:
                        pool.wait_ge(zero_out, 16 * sent)
                    pool.dma_start(blocks[n], zero[:, 0:blocks.shape[2]]).then_inc(zero_out, 16)
                    sent += 1
            pool.wait_ge(zero_out, 16 * sent)

        @block.tensor
        def _(pe):
            pe.sem_inc(pv_done, RING // G0)
            pe.wait_ge(setup, 1)
            turns = 16 * 2 * len(COMBOS)

            def max_product(g, buf, u):
                j, qt, kh = u // (HALVES * TPB), u // HALVES % TPB, u % HALVES
                pe.wait_ge(max_taken[u % MBANKS], g * TURNS + u // MBANKS + 1)
                pe.matmul(PM[u % MBANKS][:], qst[buf][0:K, j, qt * P:(qt + 1) * P],
                          kst[buf][0:K, j, kh * BLK:(kh + 1) * BLK], start=True, stop=True).then_inc(max_scores, 1)

            def turn_max(g, behind):
                pe.wait_ge(m_parts, g + 1)
                pe.wait_ge(max_taken[MBANKS - 1], (g + 1) * TURNS + behind // MBANKS + 1)
                for qt in range(TPB):
                    mm = pe.transpose(PT[:, qt * P:(qt + 1) * P], mparts[:, qt].rearrange("p j c -> p (j c)"), identb[:])
                mm.then_inc(m_turned, 1)

            def values(g, hg, r):
                kt = r % TPB
                pe.wait_ge(exped, g * UNITS + (r + 1) * G0 + SBANKS)
                if kt == 0:
                    pe.wait_ge(out_copied, g * HALVES + r // TPB + 1)
                for j in range(G0):
                    mm = pe.matmul(PO[j * VS0:(j + 1) * VS0, :], vst[hg][:, kt, j, :], probs[:, (r * G0 + j) % RING],
                                   start=(kt == 0), stop=(kt == TPB - 1), tile_position=(0, j * VS0))
                mm.then_inc(pv_done, 1)

            def stream(s):
                pause = TURN * G0 + G0 - 1
                late = {pause + 1: 1, pause + 2: 2, pause + 3: 1}
                return AHEAD + s - late.get(s, 0)

            def group(b, hg, left):
                g = b * HG0 + hg

                def ahead(t):
                    n = 1 + t // MAXES
                    if n > left:
                        return
                    if t == MAXES:
                        pe.wait_ge(q_in[(hg + 2) % BUFS], (b + (hg + 2) // BUFS) * turns + turns)
                    if t == MAXES + 2 * MBANKS - 1:
                        pe.wait_ge(m_copied, g + 2)
                    max_product(g + n, (hg + n) % BUFS, t % MAXES)

                pe.wait_ge(v_in[hg], b * 16 + 16)
                pe.wait_ge(rows_in, (g + 1) * ROW_DMAS)
                for r in range(ROUNDS):
                    half, kt = r // TPB, r % TPB
                    for j in range(G0):
                        s = r * G0 + j
                        pe.wait_ge(exped, g * UNITS + s + 1)
                        pe.matmul(PS[s % SBANKS][:], kst[hg][0:KM, j, kt * P:(kt + 1) * P],
                                  qst[hg][0:KM, j, half * BLK:(half + 1) * BLK], start=True, stop=True).then_inc(scores, 1)
                        if r == TURN and j == G0 - 1 and left:
                            turn_max(g + 1, MBANKS if left > 1 else 0)
                        if r < ROUNDS - 1:
                            for t in range(stream(s), stream(s + 1)):
                                ahead(t)
                    if r > 0:
                        values(g, hg, r - 1)
                for j in range(G0):
                    ahead(AHEAD + UNITS - G0 + j)
                values(g, hg, ROUNDS - 1)

            pe.wait_ge(q_in[0], turns)
            for u in range(MAXES):
                max_product(0, 0, u)
            turn_max(0, 0)
            pe.wait_ge(q_in[1], turns)
            for u in range(AHEAD):
                if u == MBANKS - 1:
                    pe.wait_ge(m_copied, 1)
                max_product(1, 1, u)
            pe.wait_ge(ones_set, BUFS)
            over_groups(pe, group)

        @block.scalar
        def _(act):
            act.sem_inc(exped, SBANKS)

            def group(b, hg, left):
                g = b * HG0 + hg
                for r in range(ROUNDS):
                    for j in range(G0):
                        s = r * G0 + j
                        act.wait_ge(scores, g * UNITS + s + 1)
                        if j == 0:
                            act.wait_ge(pv_done, g * ROUNDS + r + 1)
                        act.activation(probs[:, s % RING], PS[s % SBANKS][:], ACT.Exp).then_inc(exped, 1)
                        if r == TURN and j == G0 - 1 and left:
                            act.wait_ge(rows_in, (g + 1) * ROW_DMAS)
                            act.wait_ge(m_turned, g + 2)
                            act.activation(mrows[:], PT, ACT.Copy).then_inc(m_copied, 1)

            act.wait_ge(m_turned, 1)
            act.activation(mrows[:], PT, ACT.Copy).then_inc(m_copied, 1)
            over_groups(act, group)

        @block.vector
        def _(dve):
            for i in range(MBANKS):
                dve.sem_inc(max_taken[i], 1)
            dve.sem_inc(out_copied, 1)
            for half in range(HALVES):
                dve.sem_inc(out_stored[half], 16)
            dve.tensor_copy(identb[:], keep["const"][:, C_IDENT:C_IDENT + P])
            dve.memset(mparts[:], 0.0).then_inc(setup, 1)
            dve.wait_ge(setup, 1)

            def take(g, u):
                dve.wait_ge(max_scores, g * MAXES + u + 1)
                j, qt, kh = u // (HALVES * TPB), u // HALVES % TPB, u % HALVES
                dve.tensor_reduce(mx[:, j, qt, kh:kh + 1], PM[u % MBANKS][:], AX.X, ALU.max)\
                   .then_inc(max_taken[u % MBANKS], 1)

            def minus_max(g):
                dve.wait_ge(max_taken[MBANKS - 1], (g + 1) * TURNS + 1)
                dve.tensor_tensor(m[:], mx[:, :, :, 0], mx[:, :, :, 1], ALU.max).then_inc(m_step, 1)
                part = [mparts[:, :, :, i].rearrange("p t j -> p j t") for i in range(PARTS)]
                dve.wait_ge(m_step, g * 4 + 1)
                if not (isinstance(g, int) and g == 0):
                    dve.wait_ge(m_turned, g)
                dve.tensor_scalar(part[0], m[:], -1.0, None, ALU.mult).then_inc(m_step, 1)
                dve.wait_ge(m_step, g * 4 + 2)
                dve.scalar_tensor_tensor(out=mrest[:], in0=m[:], scalar=-1.0, in1=part[0], op0=ALU.mult,
                                         op1=ALU.subtract).then_inc(m_step, 1)
                dve.wait_ge(m_step, g * 4 + 3)
                dve.tensor_copy(part[1], mrest[:]).then_inc(m_step, 1)
                dve.wait_ge(m_step, g * 4 + 4)
                dve.tensor_tensor(part[2], mrest[:], part[1], ALU.subtract).then_inc(m_parts, 1)

            def copy_out(g, half):
                dve.wait_ge(pv_done, g * ROUNDS + (half + 1) * TPB + RING // G0)
                dve.wait_ge(out_stored[half], g * 16 + 16)
                dve.tensor_copy(outT[:, half], PO[:]).then_inc(out_copied, 1)

            def group(b, hg, left):
                g = b * HG0 + hg
                for t in range(AHEAD, AHEAD + MAXES):
                    if t - AHEAD == (TPB + 1) * G0 + 1:
                        copy_out(g, 0)
                    if 1 + t // MAXES <= left:
                        take(g + 1 + t // MAXES, t % MAXES)
                    if t == MAXES - 1 and left:
                        minus_max(g + 1)
                copy_out(g, 1)

            for u in range(MAXES):
                take(0, u)
            minus_max(0)
            for u in range(AHEAD):
                take(1, u)
            over_groups(dve, group)

HID = 768
HC = HID // P
INT8_SCALE = float(np.float32(1.0 / 127.0))
H1, D1 = 8, 32
G1 = 2
HG1 = H1 // G1
VS1 = 64
HPS = SEQ // BLK
F32R = mybir.dt.float32r
HALVES1 = 2
HIGH_BITS = -(1 << 12)
PAIRS1 = [(0, 0), (0, 1), (1, 0)]


def high_half(eng, out, x):
    return eng.tensor_scalar(out.bitcast(I32), x.bitcast(I32), HIGH_BITS, None, ALU.bitwise_and)


def lagged(b, h, lag):
    m = h - lag
    if m >= HPS or (first(b) and m < 0):
        return None
    return b * HPS + m, m % 2, first(b)


def block_pipeline(eng, step, lag):
    for h in range(HPS):
        step(0, h)
    with eng.Fori(1, BATCH) as b:
        for h in range(HPS):
            step(b, h)
    for h in range(HPS, HPS + lag):
        step(BATCH - 1, h)


class Layer0Weights:

    def __init__(self, nc, ctx):
        a = Alloc(nc, ctx, "u")
        shapes = {"proj": (CD, DIM), "gate": (CD, HID), "up": (CD, HID), "qkv": (CD, 3 * DIM), "down": (HC, DIM)}
        self.shapes = shapes
        self.halves = {n: a.sb("w_" + n, [P, HALVES1, *shape], F32R) for n, shape in shapes.items()}

    def prepare(self, a, pool, d, const):
        raw = {n: a.sb("raw_" + n, [P, *shape]) for n, shape in self.shapes.items()}
        hscale = a.sb("hscale", [P, H1])
        geo = a.sb("geo", [P, CD, H1, 3])
        dot = a.sb("dot", [P, CD, H1])
        dot2 = a.sb("dot2", [P, CD, H1])
        w_in, scaled, geo_step, cut, low = (a.sem("w_" + n) for n in ("in", "scaled", "geo_step", "cut", "low"))
        sources = {"proj": "L0_wprojT", "gate": "L0_ffn_w_gateT", "up": "L0_ffn_w_upT", "qkv": "L1_attn_w_qkv",
                   "down": "L0_ffn_w_downT"}
        whole = ("gate", "up", "down")
        for n, source in sources.items():
            out = raw[n][:].bitcast(I32) if n in whole else raw[n][:]
            pool.dma_start(out, d[source].rearrange("(c p) n -> p c n", p=P)).then_inc(w_in, 16)
        pool.dma_start(hscale[:], d["L1_attn_head_scales"].rearrange("(o n) -> o n", o=1).to_broadcast([P, H1])).then_inc(w_in, 16)
        pool.wait_ge(w_in, 16 * 6)
        for n in whole:
            pool.tensor_scalar(raw[n][:], raw[n][:].bitcast(I32), INT8_SCALE, None, ALU.mult).then_inc(scaled, 1)
        dirs = const[:, C_DIRS:C_DIRS + 24].rearrange("p (h c) -> p h c", c=3)
        wq = [raw["qkv"][:, c, 0:DIM].rearrange("p (h c) -> p h c", c=D1) for c in range(CD)]
        done = 0

        def steps(*instructions):
            nonlocal done
            done += 1
            instructions[-1].then_inc(geo_step, 1)
            pool.wait_ge(geo_step, done)
        steps(*[pool.tensor_tensor(geo[:, c], wq[c][:, :, 0:3], dirs, ALU.mult) for c in range(CD)])
        steps(pool.tensor_tensor(dot[:], geo[:, :, :, 0], geo[:, :, :, 1], ALU.add),
              *[pool.tensor_scalar(raw["qkv"][:, c, 0:DIM], raw["qkv"][:, c, 0:DIM], float(1.0 / np.sqrt(D1)), None, ALU.mult)
                for c in range(CD)])
        steps(pool.tensor_tensor(dot2[:], dot[:], geo[:, :, :, 2], ALU.add))
        steps(pool.tensor_tensor(dot[:], dot2[:], hscale[:].unsqueeze(1).to_broadcast([P, CD, H1]), ALU.mult))
        steps(*[pool.tensor_tensor(geo[:, c], dirs, dot[:, c].unsqueeze(2).to_broadcast([P, H1, 3]), ALU.mult)
                for c in range(CD)])
        steps(*[pool.tensor_tensor(wq[c][:, :, 0:3], wq[c][:, :, 0:3], geo[:, c], ALU.add) for c in range(CD)])
        pool.wait_ge(scaled, len(whole))
        for k, n in enumerate(self.shapes):
            pool.tensor_copy(self.halves[n][:, 0], raw[n][:]).then_inc(cut, 1)
        for k, n in enumerate(self.shapes):
            pool.wait_ge(cut, k + 1)
            pool.tensor_tensor(self.halves[n][:, 1], raw[n][:], self.halves[n][:, 0].bitcast(F32), ALU.subtract).then_inc(low, 1)
        pool.wait_ge(low, len(self.shapes))


def phase_ffn0(nc, d, keep, weights):
    with ExitStack() as ctx:
        a = Alloc(nc, ctx, "c")
        const = keep["const"]
        ident = const[:, C_IDENT:C_IDENT + P]
        bproj = a.sb("bproj", [P, DIM])
        wproj, wgate, wup, wdown, wqkv = (weights.halves[name] for name in ("proj", "gate", "up", "down", "qkv"))
        eps = a.sb("eps", [P, 1])
        attT = a.sb("attT", [P, 2, HG0, BLK])
        xin = a.sb("xin", [P, 2, TPK, DIM])
        rec = a.sb("rec", [P, 2, H0])
        att = a.sb("att", [P, TPK, DIM])
        att2T = a.sb("att2T", [P, HALVES1, CD, BLK], F32R)
        s1 = a.sb("s1", [P, TPK, DIM])
        x1 = a.sb("x1", [P, 2, TPK, DIM])
        x1T = a.sb("x1T", [P, HALVES1, CD, BLK], F32R)
        gate = a.sb("gate", [P, 2, BLK])
        hidden = a.sb("hidden", [P, 2, BLK])
        hT = a.sb("hT", [P, HALVES1, HC, BLK], F32R)
        s2 = a.sb("s2", [P, TPK, DIM])
        x2 = a.sb("x2", [P, 2, TPK, DIM])
        x2T = a.sb("x2T", [P, HALVES1, CD, BLK], F32R)
        stats = a.sb("stats", [P, 2, TPK, 6])
        moments = a.sb("moments", [P, 2, TPK, 2])
        std = a.sb("std", [P, 2, TPK])
        rstd = a.sb("rstd", [P, 2, TPK])
        halves = a.sb("halves", [P, HALVES1, 4, BLK])
        vaug = a.sb("vaug", [P, 2, TPK, H1, VS1])
        TR = [a.ps(f"TR{i}", [P, BLK]) for i in range(2)]
        PG = [a.ps(f"PG{i}", [P, BLK]) for i in range(2)]
        PU = [a.ps(f"PU{i}", [P, BLK]) for i in range(2)]
        PO = [a.ps(f"PO{i}", [P, BLK]) for i in range(2)]
        QK = [PG[0], PG[1], PU[0], PU[1]]

        w_in, prep, vset = a.sem("w_in"), a.sem("prep"), a.sem("vset")
        seen = a.sem("seen")
        att_in = [a.sem(f"att_in{i}") for i in range(2)]
        xin_in = [a.sem(f"xin_in{i}") for i in range(2)]
        names = ("att_turned", "rec_done", "normed", "att2_turned", "att2_high", "att2_low", "projected", "biased", "summed1",
                 "stat1", "aggr1", "std1", "rstd1", "x1_done", "x1_turned", "x1_high", "x1_low", "gated", "upped", "silu", "hidden", "h_high", "h_low",
                 "downed", "summed2", "stat2", "aggr2", "std2", "rstd2", "x2_done", "x2_turned", "x2_high", "x2_low",
                 "qk_ready", "hi_done", "lo_done", "v_ready", "v_copied")
        S = {n: a.sem(n) for n in names}
        x2_out = [a.sem(f"x2_out{i}") for i in range(2)]
        halves_out, last_out = a.sem("halves_out"), a.sem("last_out")
        v_out = [a.sem(f"v_out{i}") for i in range(2)]
        PREP = 2
        LAG = 2
        block = ctx.enter_context(nc.Block())

        @block.sync
        def _(sp):
            def step(b, h):
                if now := lagged(b, h, 0):
                    n, i, new = now
                    tok = bass.ds(n * BLK if isinstance(b, int) else sp.snap(n * BLK), BLK)
                    if not new:
                        sp.wait_ge(S["att_turned"], (n - 1) * TPK)
                        sp.wait_ge(S["summed1"], (n - 1) * TPK)
                    sp.dma_start(attT[:, i], d["att0"][:, :, tok].rearrange("g p n -> p g n")).then_inc(att_in[i], 16)
                    sp.dma_start(xin[:, i], d["x"][tok, :].rearrange("(t p) c -> p t c", p=P)).then_inc(xin_in[i], 16)
                if now := lagged(b, h, 2):
                    n, i, new = now
                    tok = bass.ds(n * BLK if isinstance(b, int) else sp.snap(n * BLK), BLK)
                    sp.wait_ge(S["x2_done"], (n + 1) * TPK)
                    sp.dma_start(d["x2"][tok, :].rearrange("(t p) c -> p t c", p=P), x2[:, i]).then_inc(x2_out[i], 16)
            block_pipeline(sp, step, LAG)
            for k in range(4):
                sp.wait_ge(S["lo_done"], BLOCKS * 4 + k + 1)
                sp.dma_start(d["qk1"].rearrange("(s k) p n -> k p s n", k=4)[k][:, :, TOKENS - BLK:TOKENS], halves[:, :, k])\
                  .then_inc(last_out, 16)
            for i in range(2):
                for s in (x2_out, v_out):
                    sp.wait_ge(s[i], 16 * BATCH + 16)
            sp.wait_ge(halves_out, 16 * BLOCKS)
            sp.wait_ge(last_out, 16 * 4)

        @block.gpsimd
        def _(pool):
            pool.wait_ge(w_in, 16)

            def step(b, h):
                if now := lagged(b, h, 0):
                    n, i, new = now
                    pool.wait_ge(xin_in[i], b * 16 + 16)
                    pool.tensor_tensor(xin[:, i], xin[:, i], bproj[:].unsqueeze(1).to_broadcast([P, TPK, DIM]),
                                       ALU.add).then_inc(S["biased"], 1)
                if now := lagged(b, h, 1):
                    n, i, new = now
                    for k in range(HC):
                        pool.wait_ge(S["h_high"], n * HC + k + 1)
                        pool.tensor_tensor(hT[:, 1, k], hidden[:, k % 2], hT[:, 0, k].bitcast(F32), ALU.subtract)\
                            .then_inc(S["h_low"], 1)

            block_pipeline(pool, step, LAG)

        @block.tensor
        def _(pe):

            def turn(out, src, count):
                for c in range(CD):
                    for t in range(TPK):
                        mm = pe.transpose(out[c][:, t * P:(t + 1) * P], src[:, t, c * P:(c + 1) * P], ident)
                    mm.then_inc(count, 1)

            def product(out, lhs, rhs, chunks):
                for k, (left, right) in enumerate(PAIRS1):
                    for c in range(chunks):
                        mm = pe.matmul(out, lhs(left, c), rhs(right, c), start=(k == 0 and c == 0),
                                       stop=(k == len(PAIRS1) - 1 and c == chunks - 1))
                return mm

            def turn_sums(b, h, tiles):
                if now := lagged(b, h, 0):
                    n, i, new = now
                    if 0 in tiles:
                        pe.wait_ge(att_in[i], b * 16 + 16)
                    for t in tiles:
                        if t >= 2:
                            pe.wait_ge(S["normed"], n * TPK + t - 1)
                        elif not (new and i == 0):
                            pe.wait_ge(S["att2_low"], n * CD)
                        for g in range(HG0):
                            mm = pe.transpose(TR[t % 2][:, g * P:(g + 1) * P], attT[:, i, g, t * P:(t + 1) * P], ident)
                        mm.then_inc(S["att_turned"], 1)

            def turn_x2(b, h):
                if now := lagged(b, h, 2):
                    n, i, new = now
                    pe.wait_ge(S["x2_done"], (n + 1) * TPK)
                    if lagged(b, h, 0):
                        pe.wait_ge(S["normed"], (n + 3) * TPK)
                    else:
                        pe.wait_ge(S["att2_low"], BLOCKS * CD)
                        if h == HPS + 1:
                            pe.wait_ge(S["x2_low"], n * CD)
                    turn(TR, x2[:, i], S["x2_turned"])

            def turn_att(b, h):
                if now := lagged(b, h, 0):
                    n, i, new = now
                    pe.wait_ge(S["normed"], (n + 1) * TPK)
                    if lagged(b, h, 2):
                        pe.wait_ge(S["x2_low"], (n - 1) * CD)
                    turn(TR, att[:], S["att2_turned"])

            def turn_x1(b, h):
                if now := lagged(b, h, 0):
                    n, i, new = now
                    pe.wait_ge(S["x1_done"], (n + 1) * TPK)
                    if lagged(b, h, 2):
                        pe.wait_ge(S["lo_done"], n * 4)
                    turn(PG, x1[:, i], S["x1_turned"])

            def step(b, h):
                turn_sums(b, h, (0, 1))
                now = lagged(b, h, 1)
                if now:
                    n, i, new = now
                    pe.wait_ge(S["x1_low"], (n + 1) * CD)
                    if not (new and i == 0):
                        pe.wait_ge(S["lo_done"], n * 4)
                for k in range(HC):
                    if k == 2:
                        turn_sums(b, h, (2, 3))
                    elif k == 3:
                        turn_x2(b, h)
                    elif k == 5:
                        turn_att(b, h)
                    if now:
                        if not (new and i == 0 and k < 2):
                            pe.wait_ge(S["hidden"], n * HC + k - 1)
                        for w, out, done in ((wgate, PG, "gated"), (wup, PU, "upped")):
                            product(out[k % 2][:], lambda s, c: w[:, s, c, k * P:(k + 1) * P], lambda s, c: x1T[:, s, c, :],
                                    CD).then_inc(S[done], 1)
                if now := lagged(b, h, 0):
                    n, i, new = now
                    pe.wait_ge(S["att2_low"], (n + 1) * CD)
                    for t in range(TPK):
                        if t < 2 and not (first(b) and h < 2):
                            pe.wait_ge(S["summed2"], (n - 1) * TPK)
                        if t >= 2:
                            pe.wait_ge(S["summed1"], n * TPK + t - 1)
                        product(PO[t % 2][:, 0:DIM], lambda s, c: att2T[:, s, c, t * P:(t + 1) * P],
                                lambda s, c: wproj[:, s, c, :], CD).then_inc(S["projected"], 1)
                if now := lagged(b, h, 2):
                    n, i, new = now
                    pe.wait_ge(S["x2_low"], (n + 1) * CD)
                    pe.wait_ge(S["hidden"], (n + 2) * HC if lagged(b, h, 1) else BLOCKS * HC)
                    for k in range(4):
                        product(QK[k][:], lambda s, c: wqkv[:, s, c, k * P:(k + 1) * P], lambda s, c: x2T[:, s, c, :],
                                CD).then_inc(S["qk_ready"], 1)
                    for t in range(TPK):
                        if t < 2:
                            if lagged(b, h, 0):
                                pe.wait_ge(S["summed1"], (n + 3) * TPK)
                            else:
                                pe.wait_ge(S["summed2"], (n + 1) * TPK)
                        else:
                            pe.wait_ge(S["v_copied"], n * TPK + t - 1)
                        product(PO[t % 2][:, 0:DIM], lambda s, c: x2T[:, s, c, t * P:(t + 1) * P],
                                lambda s, c: wqkv[:, s, c, 2 * DIM:3 * DIM], CD).then_inc(S["v_ready"], 1)
                if now := lagged(b, h, 1):
                    pe.wait_ge(S["h_low"], (now[0] + 1) * HC)
                for t in range(TPK):
                    if t == TPK // 2:
                        turn_x1(b, h)
                    if now:
                        n, i, new = now
                        if t < 2:
                            if lagged(b, h, 2):
                                pe.wait_ge(S["v_copied"], (n - 1) * TPK + t + 3)
                            elif lagged(b, h, 0):
                                pe.wait_ge(S["summed1"], (n + 2) * TPK)
                        else:
                            pe.wait_ge(S["summed2"], n * TPK + t - 1)
                        product(PO[t % 2][:, 0:DIM], lambda s, k: hT[:, s, k, t * P:(t + 1) * P],
                                lambda s, k: wdown[:, s, k, :], HC).then_inc(S["downed"], 1)

            block_pipeline(pe, step, LAG)

        @block.scalar
        def _(act):
            for i in range(2):
                act.sem_inc(v_out[i], 16)
            act.sem_inc(halves_out, 16)
            act.dma_start(bproj[:], d["L0_attn_b_proj"].rearrange("(o n) -> o n", o=1).to_broadcast([P, DIM])).then_inc(w_in, 16)
            act.wait_ge(prep, PREP)

            def deviation(which, i, n, count, done):
                act.wait_ge(S[count], (n + 1) * TPK)
                act.activation(std[:, which], moments[:, which, :, 1], ACT.Sqrt, bias=eps[:, 0:1]).then_inc(S[done], 1)

            def high_halves(n, xT, banks, name):
                for c in range(CD):
                    act.wait_ge(S[name + "_turned"], n * CD + c + 1)
                    act.activation(xT[:, 0, c], banks[c][:], ACT.Copy).then_inc(S[name + "_high"], 1)

            def step(b, h):
                gated = lagged(b, h, 1)
                for k in range(HC):
                    if k == 3 and (now := lagged(b, h, 2)):
                        high_halves(now[0], x2T, TR, "x2")
                    if k == 5 and (now := lagged(b, h, 0)):
                        high_halves(now[0], att2T, TR, "att2")
                    if gated:
                        n, i, new = gated
                        act.wait_ge(S["gated"], n * HC + k + 1)
                        if not (new and i == 0 and k < 2):
                            act.wait_ge(S["hidden"], n * HC + k - 1)
                        act.activation(gate[:, k % 2], PG[k % 2][:], ACT.Silu).then_inc(S["silu"], 1)
                if now := lagged(b, h, 2):
                    n, i, new = now
                    act.wait_ge(v_out[i], stored(b, h, 2))
                    for t in range(TPK):
                        act.wait_ge(S["v_ready"], n * TPK + t + 1)
                        act.activation(vaug[:, i, t, :, 0:D1], PO[t % 2][:, 0:DIM].rearrange("p (h c) -> p h c", h=H1),
                                       ACT.Copy).then_inc(S["v_copied"], 1)
                if now := lagged(b, h, 0):
                    n, i, new = now
                    deviation(0, i, n, "aggr1", "std1")
                    high_halves(n, x1T, PG, "x1")
                if now := lagged(b, h, 1):
                    n, i, new = now
                    deviation(1, i, n, "aggr2", "std2")
                if now := lagged(b, h, 2):
                    n, i, new = now
                    tok = bass.ds(n * BLK if isinstance(b, int) else act.snap(n * BLK), BLK)
                    act.wait_ge(S["v_copied"], (n + 1) * TPK)
                    act.dma_start(d["v1"][tok, :].rearrange("(t p) c -> p t c", p=P),
                                  vaug[:, i].rearrange("p t h c -> p t (h c)")).then_inc(v_out[i], 16)
                    if not (isinstance(n, int) and n == BLOCKS - 1):
                        act.wait_ge(S["lo_done"], (n + 1) * 4 + 4)
                        act.dma_start(d["qk1"][:, :, tok].rearrange("a p n -> p a n"),
                                      halves[:].rearrange("p s k n -> p (s k) n")).then_inc(halves_out, 16)

            block_pipeline(act, step, LAG)

        @block.vector
        def _(dve):
            for i in range(2):
                dve.sem_inc(x2_out[i], 16)
            dve.sem_inc(S["lo_done"], 4)
            dve.memset(eps[:], LN_EPS).then_inc(prep, 1)
            for i in range(2):
                last = dve.memset(vaug[:, i], 0.0)
            last.then_inc(vset, 1)
            dve.wait_ge(vset, 1)
            for i in range(2):
                last = dve.memset(vaug[:, i, :, :, D1:D1 + 1], 1.0)
            last.then_inc(prep, 1)
            dve.wait_ge(prep, PREP)

            def moments_of(which, src, n, count, done):
                for t in range(TPK):
                    dve.wait_ge(S[count], n * TPK + t + 1)
                    dve.bn_stats(stats[:, which, t], src[:, t]).then_inc(S["stat" + done], 1)
                dve.wait_ge(S["stat" + done], (n + 1) * TPK)
                dve.sem_inc(seen, 1)
                for t in range(TPK):
                    dve.bn_aggr(moments[:, which, t], stats[:, which, t]).then_inc(S["aggr" + done], 1)

            def norm(which, src, out, n, done, x_done):
                dve.wait_ge(S["std" + done], n + 1)
                dve.reciprocal(rstd[:, which], std[:, which]).then_inc(S["rstd" + done], 1)
                dve.wait_ge(S["rstd" + done], n + 1)
                for t in range(TPK):
                    dve.tensor_scalar(out[:, t], src[:, t], moments[:, which, t, 0:1], rstd[:, which, t:t + 1],
                                      ALU.subtract, ALU.mult).then_inc(S[x_done], 1)

            def low_halves(n, xT, banks, name):
                for c in range(CD):
                    dve.wait_ge(S[name + "_high"], n * CD + c + 1)
                    dve.tensor_tensor(xT[:, 1, c], banks[c][:], xT[:, 0, c].bitcast(F32), ALU.subtract)\
                       .then_inc(S[name + "_low"], 1)

            def normalise(b, h, tiles):
                if now := lagged(b, h, 0):
                    n, i, new = now
                    for t in tiles:
                        dve.wait_ge(S["att_turned"], n * TPK + t + 1)
                        heads = TR[t % 2][:].rearrange("p (h c) -> p h c", h=H0)
                        dve.reciprocal(rec[:, t % 2], heads[:, :, D0]).then_inc(S["rec_done"], 1)
                        dve.wait_ge(S["rec_done"], n * TPK + t + 1)
                        dve.tensor_tensor(att[:, t].rearrange("p (h c) -> p h c", h=H0), heads[:, :, 0:D0],
                                          rec[:, t % 2].unsqueeze(2).to_broadcast([P, H0, D0]), ALU.mult)\
                           .then_inc(S["normed"], 1)

            def step(b, h):
                gated = lagged(b, h, 1)
                for k in range(HC):
                    if k < 2:
                        normalise(b, h, (2 * k, 2 * k + 1))
                    if k == 3 and (now := lagged(b, h, 2)):
                        low_halves(now[0], x2T, TR, "x2")
                    if k == 5 and (now := lagged(b, h, 0)):
                        low_halves(now[0], att2T, TR, "att2")
                    if gated:
                        n, i, new = gated
                        dve.wait_ge(S["silu"], n * HC + k + 1)
                        dve.wait_ge(S["upped"], n * HC + k + 1)
                        if not (new and i == 0 and k < 2):
                            dve.wait_ge(S["h_low"], n * HC + k - 1)
                        dve.tensor_tensor(hidden[:, k % 2], gate[:, k % 2], PU[k % 2][:], ALU.mult).then_inc(S["hidden"], 1)
                        dve.wait_ge(S["hidden"], n * HC + k + 1)
                        dve.tensor_copy(hT[:, 0, k], hidden[:, k % 2]).then_inc(S["h_high"], 1)
                if now := lagged(b, h, 0):
                    n, i, new = now
                    dve.wait_ge(S["biased"], n + 1)
                    for t in range(TPK):
                        dve.wait_ge(S["projected"], n * TPK + t + 1)
                        dve.tensor_tensor(s1[:, t], xin[:, i, t], PO[t % 2][:, 0:DIM], ALU.add).then_inc(S["summed1"], 1)
                    moments_of(0, s1[:], n, "summed1", "1")
                if now := lagged(b, h, 2):
                    n, i, new = now
                    dve.wait_ge(halves_out, n * 16 + 16)
                    for k in range(4):
                        dve.wait_ge(S["qk_ready"], n * 4 + k + 1)
                        high_half(dve, halves[:, 0, k], QK[k][:]).then_inc(S["hi_done"], 1)
                        dve.wait_ge(S["hi_done"], n * 4 + k + 1)
                        dve.tensor_tensor(halves[:, 1, k], QK[k][:], halves[:, 0, k], ALU.subtract)\
                           .then_inc(S["lo_done"], 1)
                if now := lagged(b, h, 0):
                    n, i, new = now
                    norm(0, s1[:], x1[:, i], n, "1", "x1_done")
                now = lagged(b, h, 1)
                for t in range(TPK):
                    if t == TPK // 2 and (other := lagged(b, h, 0)):
                        low_halves(other[0], x1T, PG, "x1")
                    if now:
                        n, i, new = now
                        dve.wait_ge(S["downed"], n * TPK + t + 1)
                        dve.tensor_tensor(s2[:, t], x1[:, i, t], PO[t % 2][:, 0:DIM], ALU.add).then_inc(S["summed2"], 1)
                if now:
                    moments_of(1, s2[:], now[0], "summed2", "2")
                if now := lagged(b, h, 1):
                    n, i, new = now
                    dve.wait_ge(x2_out[i], stored(b, h, 1))
                    norm(1, s2[:], x2[:, i], n, "2", "x2_done")

            block_pipeline(dve, step, LAG)


def stored(b, h, lag):
    return b * 16 + 16 if h - lag >= 0 else b * 16

def phase_attention1(nc, d, keep, weights, incoming):
    K = len(PAIRS1) * D1
    KM = K + HALVES1
    BUFS = HG1
    RING = 8
    SBANKS, MBANKS = 3, 3
    MAXES = [(j, qt, kh) for j in range(G1) for qt in range(TPB) for kh in range(qt // TPK + 1)]
    UNITS = [(half, kt, j) for half in range(HPS) for kt in range((half + 1) * TPK) for j in range(G1)]
    NM, NU = len(MAXES), len(UNITS)
    TURNS = NM // MBANKS
    ROUNDS = NU // G1
    HALF_ROUNDS = [sum(1 for u in UNITS if u[0] <= half) // G1 for half in range(HPS)]
    AHEAD = 12
    TURN = NM + 2 * MBANKS - 1 - AHEAD
    ROW_DMAS = 16 * HALVES1
    assert NM == NU
    with ExitStack() as ctx:
        a = Alloc(nc, ctx, "d")
        const = keep["const"]
        ident = const[:, C_IDENT:C_IDENT + P]
        qst = [a.sb(f"qst{i}", [P, G1, SEQ], F32R) for i in range(BUFS)]
        kst = [a.sb(f"kst{i}", [P, G1, SEQ], F32R) for i in range(BUFS)]
        vst = [a.sb(f"vst{i}", [P, TPB, G1, VS1]) for i in range(BUFS)]
        probs = a.sb("probs", [P, RING, BLK])
        outT = a.sb("outT", [P, HPS, BLK])
        mx = a.sb("mx", [P, G1, TPB, 2])
        m = a.sb("m", [P, G1, TPB])
        minus = a.sb("minus", [P, G1, TPB])
        mhalves = a.sb("mhalves", [P, P // (G1 * TPB), G1, TPB])
        mrows = a.sb("mrows", [HALVES1 * G1 * TPB, P])
        fixed = a.sb("fixed", [P, 3, P], BF16)
        identb, mask_q, mask_k = (fixed[:, i] for i in range(3))
        PM = [a.ps(f"PM{i}", [P, BLK]) for i in range(MBANKS)]
        PS = [a.ps(f"PS{i}", [P, BLK]) for i in range(SBANKS)]
        PO = [a.ps(f"PO{i}", [P, BLK]) for i in range(HPS)]
        PT = PM[MBANKS - 1][:, 0:P]

        setup, ones_set = a.sem("setup"), a.sem("ones_set")
        q_in = [a.sem(f"q_in{i}") for i in range(BUFS)]
        v_in = [a.sem(f"v_in{i}") for i in range(BUFS)]
        max_scores = a.sem("max_scores")
        max_taken = [a.sem(f"max_taken{i}") for i in range(MBANKS)]
        m_step, m_cut, m_turned, m_copied, rows_in = (
            a.sem(n) for n in ("m_step", "m_cut", "m_turned", "m_copied", "rows_in"))
        scores, exped, pv_done, out_copied = (a.sem(n) for n in ("scores", "exped", "pv_done", "out_copied"))
        out_stored = [a.sem(f"out_stored{i}") for i in range(HPS)]
        block = ctx.enter_context(nc.Block())

        def over_groups(eng, body):
            with eng.Fori(0, BATCH - 1) as b:
                for hg in range(HG1):
                    body(b, hg, 2)
            for hg in range(HG1):
                body(BATCH - 1, hg, min(2, HG1 - 1 - hg))

        def queries(half, kt):
            q0 = max(half * BLK, kt * P)
            return q0, (half + 1) * BLK - q0

        def keys(qt, kh):
            return min(BLK, (qt + 1) * P - kh * BLK)

        @block.sync
        def _(sp):
            def load(b, hg):
                tok = bass.ds(b * SEQ, SEQ)
                for stack, side, first_blk in ((qst, 0, 0), (kst, 1, 2)):
                    for s, pair in enumerate(PAIRS1):
                        rows = d["qk1"][pair[side] * 4 + first_blk + hg // 2, (hg % 2) * 64:(hg % 2) * 64 + 64, tok]
                        sp.dma_start(stack[hg][s * D1:(s + 1) * D1].bitcast(F32), rows.rearrange("(j p) n -> p j n", p=D1))\
                          .then_inc(q_in[hg], 16)
                src = d["v1"][tok, hg * G1 * VS1:(hg + 1) * G1 * VS1].rearrange("(t p) c -> p t c", p=P)
                sp.dma_start(vst[hg][:].rearrange("p t j c -> p t (j c)"), src).then_inc(v_in[hg], 16)

            def rows(g, nxt):
                sp.wait_ge(m_copied, g + 1)
                for i in range(HALVES1):
                    sp.dma_start(qst[nxt][K + i:K + i + 1].bitcast(F32), mrows[i * G1 * TPB:(i + 1) * G1 * TPB, :])\
                      .then_inc(rows_in, 16)

            def store(b, g, hg, half):
                sp.wait_ge(out_copied, g * HPS + half + HPS + 1)
                sp.dma_start(d["att1"][hg, :, bass.ds(b * SEQ + half * BLK, BLK)], outT[:, half])\
                  .then_inc(out_stored[half], 16)

            def group(b, hg, left):
                g = b * HG1 + hg
                if isinstance(b, int) and hg == 1:
                    for i in range(2):
                        sp.wait_ge(out_stored[i], 16 * (HG1 + 1))
                        tok = slice(i * BLK, (i + 1) * BLK)
                        incoming.load_att(sp, d, tok, i)
                        incoming.load_x2(sp, d, tok, i)
                store(b, g, hg, 0)
                if left:
                    rows(g + 1, (hg + 1) % BUFS)
                store(b, g, hg, 1)
                if not isinstance(b, int):
                    sp.wait_ge(pv_done, (g + 1) * ROUNDS + RING // G1)
                    load(b + 1, hg)

            for hg in range(HG1):
                load(0, hg)
            rows(0, 0)
            weights.load_first(sp, d)
            over_groups(sp, group)
            for half in range(HPS):
                sp.wait_ge(out_stored[half], 16 * (BATCH * HG1 + 1))

        @block.tensor
        def _(pe):
            pe.sem_inc(pv_done, RING // G1)
            pe.wait_ge(setup, 2)
            turns = 16 * 2 * len(PAIRS1)

            def max_product(g, buf, u):
                j, qt, kh = MAXES[u]
                w = keys(qt, kh)
                diagonal = kh == qt // TPK
                out = PM[u % MBANKS]
                pe.wait_ge(max_taken[u % MBANKS], g * TURNS + u // MBANKS + 1)
                mm = pe.matmul(out[:, 0:w], qst[buf][0:K, j, qt * P:(qt + 1) * P],
                               kst[buf][0:K, j, kh * BLK:kh * BLK + w], start=True, stop=not diagonal)
                if diagonal:
                    mm = pe.matmul(out[:, w - P:w], identb, mask_q, start=False, stop=True)
                mm.then_inc(max_scores, 1)

            def turn_max(g, behind):
                pe.wait_ge(m_cut, g + 1)
                pe.wait_ge(max_taken[MBANKS - 1], (g + 1) * TURNS + behind + 1)
                pe.transpose(PT, mhalves[:].rearrange("p i j t -> p (i j t)"), ident).then_inc(m_turned, 1)

            def values(g, hg, r):
                half, kt, _ = UNITS[r * G1]
                q0, w = queries(half, kt)
                pe.wait_ge(exped, g * NU + (r + 1) * G1 + SBANKS)
                if kt == 0:
                    pe.wait_ge(out_copied, g * HPS + half + 1)
                for j in range(G1):
                    mm = pe.matmul(PO[half][j * VS1:(j + 1) * VS1, q0 - half * BLK:q0 - half * BLK + w],
                                   vst[hg][:, kt, j, :], probs[:, (r * G1 + j) % RING, 0:w], start=(kt == 0),
                                   stop=(kt == (half + 1) * TPK - 1), tile_position=(0, j * VS1))
                mm.then_inc(pv_done, 1)

            def stream(s):
                late = {TURN + 1: 1, TURN + 2: 2, TURN + 3: 1}
                return AHEAD + s - late.get(s, 0)

            def group(b, hg, left):
                g = b * HG1 + hg

                def ahead(t):
                    n = 1 + t // NM
                    if n > left:
                        return
                    if t == NM:
                        pe.wait_ge(q_in[(hg + 2) % BUFS], (b + (hg + 2) // BUFS) * turns + turns)
                    if t == NM + 2 * MBANKS - 1:
                        pe.wait_ge(m_copied, g + 2)
                    max_product(g + n, (hg + n) % BUFS, t % NM)

                pe.wait_ge(v_in[hg], b * 16 + 16)
                pe.wait_ge(rows_in, (g + 1) * ROW_DMAS)
                for s, (half, kt, j) in enumerate(UNITS):
                    q0, w = queries(half, kt)
                    diagonal = q0 == kt * P
                    pe.wait_ge(exped, g * NU + s + 1)
                    out = PS[s % SBANKS]
                    mm = pe.matmul(out[:, 0:w], kst[hg][0:KM, j, kt * P:(kt + 1) * P], qst[hg][0:KM, j, q0:q0 + w],
                                   start=True, stop=not diagonal)
                    if diagonal:
                        mm = pe.matmul(out[:, 0:P], identb, mask_k, start=False, stop=True)
                    mm.then_inc(scores, 1)
                    if s == TURN and left:
                        turn_max(g + 1, 1 if left > 1 else 0)
                    if s < NU - G1:
                        for t in range(stream(s), stream(s + 1)):
                            ahead(t)
                    if j == G1 - 1 and s >= G1:
                        values(g, hg, s // G1 - 1)
                for t in range(AHEAD + NU - G1, AHEAD + NU):
                    ahead(t)
                values(g, hg, ROUNDS - 1)

            pe.wait_ge(q_in[0], turns)
            for u in range(NM):
                max_product(0, 0, u)
            turn_max(0, 0)
            pe.wait_ge(q_in[1], turns)
            for u in range(AHEAD):
                if u == MBANKS - 1:
                    pe.wait_ge(m_copied, 1)
                max_product(1, 1, u)
            pe.wait_ge(ones_set, BUFS)
            over_groups(pe, group)

        @block.gpsimd
        def _(pool):
            for i in range(BUFS):
                pool.memset(kst[i][K:KM].bitcast(F32), 1.0).then_inc(ones_set, 1)

        @block.scalar
        def _(act):
            act.sem_inc(exped, SBANKS)

            def copy_rows(g):
                act.wait_ge(m_turned, g + 1)
                act.activation(mrows[:], PT[0:HALVES1 * G1 * TPB], ACT.Copy).then_inc(m_copied, 1)

            def group(b, hg, left):
                g = b * HG1 + hg
                for s, (half, kt, j) in enumerate(UNITS):
                    w = queries(half, kt)[1]
                    act.wait_ge(scores, g * NU + s + 1)
                    if j == 0:
                        act.wait_ge(pv_done, g * ROUNDS + s // G1 + 1)
                    act.activation(probs[:, s % RING, 0:w], PS[s % SBANKS][:, 0:w], ACT.Exp).then_inc(exped, 1)
                    if s == TURN and left:
                        act.wait_ge(rows_in, (g + 1) * ROW_DMAS)
                        copy_rows(g + 1)

            copy_rows(0)
            over_groups(act, group)

        @block.vector
        def _(dve):
            for i in range(MBANKS):
                dve.sem_inc(max_taken[i], 1)
            dve.sem_inc(out_copied, HPS)
            for half in range(HPS):
                dve.sem_inc(out_stored[half], 16)
            for i, at in enumerate((C_IDENT, C_MASK_Q, C_MASK_K)):
                dve.tensor_copy(fixed[:, i], const[:, at:at + P])
            dve.memset(mx[:], -3.0e38).then_inc(setup, 1)
            dve.memset(mhalves[:], 0.0).then_inc(setup, 1)
            dve.wait_ge(setup, 2)

            def take(g, u):
                j, qt, kh = MAXES[u]
                dve.wait_ge(max_scores, g * NM + u + 1)
                dve.tensor_reduce(mx[:, j, qt, kh:kh + 1], PM[u % MBANKS][:, 0:keys(qt, kh)], AX.X, ALU.max)\
                   .then_inc(max_taken[u % MBANKS], 1)

            def minus_max(g):
                dve.wait_ge(max_taken[MBANKS - 1], (g + 1) * TURNS + 1)
                dve.tensor_tensor(m[:], mx[:, :, :, 0], mx[:, :, :, 1], ALU.max).then_inc(m_step, 1)
                dve.wait_ge(m_step, g * 3 + 1)
                dve.tensor_scalar(minus[:], m[:], -1.0, None, ALU.mult).then_inc(m_step, 1)
                dve.wait_ge(m_step, g * 3 + 2)
                if not (isinstance(g, int) and g == 0):
                    dve.wait_ge(m_turned, g)
                high_half(dve, mhalves[:, 0], minus[:]).then_inc(m_step, 1)
                dve.wait_ge(m_step, g * 3 + 3)
                dve.tensor_tensor(mhalves[:, 1], minus[:], mhalves[:, 0], ALU.subtract).then_inc(m_cut, 1)

            def copy_out(g, half):
                dve.wait_ge(pv_done, g * ROUNDS + HALF_ROUNDS[half] + RING // G1)
                dve.wait_ge(out_stored[half], g * 16 + 16)
                dve.tensor_copy(outT[:, half], PO[half][:]).then_inc(out_copied, 1)

            def group(b, hg, left):
                g = b * HG1 + hg
                for t in range(AHEAD, AHEAD + NM):
                    if t - AHEAD == (HALF_ROUNDS[0] + 1) * G1 + 1:
                        copy_out(g, 0)
                    if 1 + t // NM <= left:
                        take(g + 1 + t // NM, t % NM)
                    if t == NM - 1 and left:
                        minus_max(g + 1)
                copy_out(g, 1)

            for u in range(NM):
                take(0, u)
            minus_max(0)
            for u in range(AHEAD):
                take(1, u)
            over_groups(dve, group)

E_COPY, E_CONST, E_MLP = 1, 2, 4
MLPS = E - E_MLP
TOP_K = 2
SLOTS = E * CAP
NOWHERE = float(2 * SLOTS)


class Routed:

    def __init__(self, nc, ctx):
        a = Alloc(nc, ctx, "r")
        self.x3 = a.sb("x3", [P, TILES, DIM])
        self.coef = a.sb("coef", [P, TILES * TOP_K])


class Unrouted:

    def __init__(self, nc, ctx):
        a = Alloc(nc, ctx, "i")
        self.attT = a.sb("attT", [P, 2, HG1, BLK])
        self.x2 = a.sb("x2", [P, 2, TPK, DIM])
        self.att_in = [a.sem(f"att_in{i}") for i in range(2)]
        self.x2_in = [a.sem(f"x2_in{i}") for i in range(2)]

    def load_att(self, sp, d, tok, i):
        sp.dma_start(self.attT[:, i], d["att1"][:, :, tok].rearrange("g p n -> p g n")).then_inc(self.att_in[i], 16)

    def load_x2(self, sp, d, tok, i):
        sp.dma_start(self.x2[:, i], d["x2"][tok, :].rearrange("(t p) c -> p t c", p=P)).then_inc(self.x2_in[i], 16)


def phase_route(nc, d, keep, weights, incoming, tokens):
    with ExitStack() as ctx:
        a = Alloc(nc, ctx, "e")
        const = keep["const"]
        ident = const[:, C_IDENT:C_IDENT + P]
        iota = const[:, C_IOTA:C_IOTA + E]
        wout = a.sb("wout", [P, CD, DIM])
        wr = a.sb("wr", [P, CD, E])
        nwc = a.sb("nwc", [P, CD, 1])
        wrn = a.sb("wrn", [P, CD, E])
        br = a.sb("br", [P, E])
        nw = a.sb("nw", [P, DIM])
        before = a.sb("before", [P, P], BF16)
        ones = a.sb("ones", [P, P], BF16)
        eps = a.sb("eps", [P, 1])
        attT, x2, att_in, x2_in = incoming.attT, incoming.x2, incoming.att_in, incoming.x2_in
        rec = a.sb("rec", [P, TPK, H1])
        att = a.sb("att", [P, 2, TPK, DIM])
        att2T = a.sb("att2T", [P, 2, CD, BLK])
        s3 = a.sb("s3", [P, 2, TPK, DIM])
        x3 = a.sb("x3", [P, 2, TPK, DIM])
        square = a.sb("square", [P, TPK, DIM])
        scaled3 = a.sb("scaled3", [P, TPK, DIM])
        xn = a.sb("xn", [P, 2, TPK, SLOT_COLS])
        x3T = a.sb("x3T", [P, 2, CD, BLK])
        stats = a.sb("stats", [P, TPK, 6])
        moments = a.sb("moments", [P, 2, TPK, 2])
        std = a.sb("std", [P, 2, TPK])
        rstd = a.sb("rstd", [P, 2, TPK])
        shift = a.sb("shift", [P, 2, TPK])
        meansq = a.sb("meansq", [P, TPK])
        rms = a.sb("rms", [P, 2, TPK])
        rrms = a.sb("rrms", [P, 2, TPK])
        scaled = a.sb("scaled", [P, TPK, E])
        logits = a.sb("logits", [P, TPK, E])
        top = a.sb("top", [P, TPK])
        below = a.sb("below", [P, TPK, E])
        expd = a.sb("expd", [P, TPK, E])
        total = a.sb("total", [P, TPK])
        rtotal = a.sb("rtotal", [P, TPK])
        prob = a.sb("prob", [P, TPK, E])
        best = a.sb("best", [P, TPK, 8])
        besti = a.sb("besti", [P, TPK, 8], U32)
        expert = a.sb("expert", [P, TPK, TOP_K])
        onehot = a.sb("onehot", [P, TPK, TOP_K, E])
        chosen = a.sb("chosen", [P, TPK, E], BF16)
        count = a.sb("count", [P, 2, TPK + 1, E], BF16)
        ranked = a.sb("ranked", [P, TPK, TOP_K, E])
        rank = a.sb("rank", [P, TPK, TOP_K])
        kept = a.sb("kept", [P, TPK, TOP_K])
        slot = a.sb("slot", [P, TPK, TOP_K])
        place = a.sb("place", [P, TPK, TOP_K])
        holds = a.sb("holds", [P, TPK, TOP_K])
        moves = a.sb("moves", [P, TPK, TOP_K])
        target = a.sb("target", [P, TPK, TOP_K])
        weight = a.sb("weight", [P, TPK, TOP_K])
        wsum = a.sb("wsum", [P, TPK])
        wzero = a.sb("wzero", [P, TPK])
        divisor = a.sb("divisor", [P, TPK])
        rwsum = a.sb("rwsum", [P, TPK])
        to_slot = a.sb("to_slot", [P, 2, TPK, TOP_K], I32)
        coef = a.sb("coef", [P, 2, TPK, TOP_K])
        TR = [a.ps(f"TR{i}", [P, BLK]) for i in range(4)]
        PX = [a.ps(f"PX{i}", [P, BLK]) for i in range(2)]
        PL = a.ps("PL", [P, TPK, E])
        PR = a.ps("PR", [P, TPK, E])

        w_in, prep = a.sem("w_in"), a.sem("prep")
        seen, pool_seen = a.sem("seen"), a.sem("pool_seen")
        names = ("att_turned", "rec_done", "normed", "att2_turned", "att2_copied", "projected", "summed", "stat", "aggr",
                 "std_done", "rstd_step", "rstd_done", "x3_done", "squared", "rms_done", "rrms_done", "scaled3_done", "xn_done", "late_done",
                  "x3_turned",
                 "x3_copied", "logits_ready", "step", "expd_done", "counted", "ranks_ready", "routed", "xn_free")
        S = {n: a.sem(n) for n in names}
        x3_out = [a.sem(f"x3_out{i}") for i in range(2)]
        route_out = [a.sem(f"route_out{i}") for i in range(2)]
        scattered = a.sem("scattered")
        PREP = 4
        TURN_ORDER = (2, 3, 0, 1)
        block = ctx.enter_context(nc.Block())
        ATT, SUM, NORM, ROUTE, STORE = range(5)

        def steps(eng, step, last):
            for p in range(2):
                for h in range(HPS):
                    step(p, h)
            with eng.Fori(2, BATCH) as p:
                for h in range(HPS):
                    step(p, h)
            for h in range(last):
                step(BATCH + h // HPS, h % HPS)

        def at(p, h, stage):
            n, i, used = p * HPS + (h - stage), (h - stage) % HPS, p + (h - stage) // HPS
            if isinstance(n, int) and not 0 <= n < BLOCKS:
                return None
            return n, i, used

        def is_late(n):
            return isinstance(n, int) and n >= BLOCKS - 2

        def wait_if_any(eng, sem, value):
            if not isinstance(value, int) or value > 0:
                eng.wait_ge(sem, value)

        @block.sync
        def _(sp):


            def where(n, size):
                return bass.ds(n * size if isinstance(n, int) else sp.snap(n * size), size)

            def step(p, h):
                loaded = at(p, h, ATT)
                if isinstance(p, int) and p == 0:
                    loaded = None
                if loaded:
                    n, i, used = loaded
                    sp.wait_ge(S["att_turned"], (n - 1) * TPK)
                    incoming.load_att(sp, d, where(n, BLK), i)
                if now := at(p, h, ROUTE):
                    n, i, used = now
                    sp.wait_ge(S["x3_done"], (n + 1) * TPK)
                    sp.dma_start(tokens.x3[:, where(n, TPK), :], x3[:, i])\
                      .then_inc(x3_out[i], 16)
                if loaded:
                    n, i, used = loaded
                    sp.wait_ge(S["summed"], (n - 1) * TPK)
                    incoming.load_x2(sp, d, where(n, BLK), i)
                if now := at(p, h, STORE):
                    n, i, used = now
                    cols = where(n, TPK * TOP_K)
                    sp.wait_ge(S["routed"], n + 1)
                    sp.dma_start(tokens.coef[:, cols], coef[:, i].rearrange("p t k -> p (t k)")).then_inc(route_out[i], 16)
                if isinstance(p, int) and (p, h) == (0, 0):
                    sp.dma_start(wout[:], d["L1_attn_w_out"].rearrange("(c p) n -> p c n", p=P)).then_inc(w_in, 16)
                    sp.dma_start(wr[:], d["L1_ffn_router_weightT"].rearrange("(c p) n -> p c n", p=P)).then_inc(w_in, 16)
                    for c in range(CD):
                        sp.dma_start(nwc[:, c], d["L1_ffn_norm_weight"].rearrange("(c p o) -> c p o", p=P, o=1)[c])\
                          .then_inc(w_in, 16)
                    for out, name in ((br, "router_bias"), (nw, "norm_weight")):
                        sp.dma_start(out[:], d["L1_ffn_" + name].rearrange("(o n) -> o n", o=1).to_broadcast(list(out.shape)))\
                          .then_inc(w_in, 16)

            steps(sp, step, STORE)
            for i in range(2):
                sp.wait_ge(x3_out[i], 16 * (BATCH + 1))
                sp.wait_ge(route_out[i], 16 * (BATCH + 1))

        @block.tensor
        def _(pe):
            def turn(out, src, count):
                for c in range(CD):
                    for t in range(TPK):
                        mm = pe.transpose(out[c][:, t * P:(t + 1) * P], src[:, t, c * P:(c + 1) * P], ident)
                    mm.then_inc(count, 1)

            def turn_heads(i, tiles):
                for t in tiles:
                    for g in range(HG1):
                        mm = pe.transpose(TR[t][:, g * P:(g + 1) * P], attT[:, i, g, t * P:(t + 1) * P], ident)
                    mm.then_inc(S["att_turned"], 1)

            def step(p, h):
                att_block, sum_block, norm_block, route_block = (at(p, h, s) for s in (ATT, SUM, NORM, ROUTE))
                if att_block:
                    n, i, used = att_block
                    pe.wait_ge(att_in[i], used * 16 + 16)
                    wait_if_any(pe, S["normed"], (n - 1) * TPK + CD)
                    wait_if_any(pe, S["x3_copied"], (n - 2) * CD)
                    turn_heads(i, TURN_ORDER[:CD])
                if sum_block:
                    n, i, used = sum_block
                    pe.wait_ge(S["normed"], (n + 1) * TPK)
                    turn(TR, att[:, i], S["att2_turned"])
                if sum_block:
                    n, i, used = sum_block
                    if isinstance(n, int) and n == 0:
                        pe.wait_ge(w_in, 16 * (4 + CD))
                        pe.wait_ge(prep, PREP)
                    pe.wait_ge(S["att2_copied"], (n + 1) * CD)
                    wait_if_any(pe, S["summed"], n * TPK)
                    for t in range(TPK):
                        for c in range(CD):
                            mm = pe.matmul(PX[t // 2][:, t % 2 * DIM:(t % 2 + 1) * DIM], att2T[:, i, c, t * P:(t + 1) * P],
                                           wout[:, c, :], start=(c == 0), stop=(c == CD - 1))
                        mm.then_inc(S["projected"], 1)
                if norm_block:
                    n, i, used = norm_block
                    pe.wait_ge(S["x3_done"], (n + 1) * TPK)
                    if att_block:
                        pe.wait_ge(S["normed"], att_block[0] * TPK + CD)
                    turn(TR[CD:], x3[:, i], S["x3_turned"])
                if att_block:
                    n, i, used = att_block
                    turn_heads(i, TURN_ORDER[CD:])
                if route_block:
                    n, i, used = route_block
                    pe.wait_ge(S["counted"], n + 1)
                    for t in range(TPK):
                        pe.matmul(PR[:, t], before[:], chosen[:, t], start=True, stop=False)
                        mm = pe.matmul(PR[:, t], ones[:], count[:, i, t], start=False, stop=True)
                    mm.then_inc(S["ranks_ready"], 1)
                if norm_block:
                    n, i, used = norm_block
                    pe.wait_ge(S["x3_copied"], (n + 1) * CD)
                    for t in range(TPK):
                        for c in range(CD):
                            mm = pe.matmul(PL[:, t], x3T[:, i, c, t * P:(t + 1) * P], wrn[:, c, :], start=(c == 0),
                                           stop=(c == CD - 1))
                    mm.then_inc(S["logits_ready"], 1)

            steps(pe, step, ROUTE)

        @block.scalar
        def _(act):
            for i in range(2):
                act.sem_inc(x3_out[i], 16)
                act.sem_inc(route_out[i], 16)
            act.wait_ge(prep, PREP)

            def step(p, h):
                sum_block, norm_block, route_block = (at(p, h, s) for s in (SUM, NORM, ROUTE))
                if sum_block:
                    n, i, used = sum_block
                    for c in range(CD):
                        act.wait_ge(S["att2_turned"], n * CD + c + 1)
                        act.activation(att2T[:, i, c], TR[c][:], ACT.Copy).then_inc(S["att2_copied"], 1)
                if route_block:
                    n, i, used = route_block
                    act.wait_ge(S["step"], n * ROUTE_STEPS + 4)
                    act.activation(expd[:], below[:], ACT.Exp).then_inc(S["expd_done"], 1)
                if norm_block:
                    n, i, used = norm_block
                    act.wait_ge(S["rstd_done"], n + 1)
                    act.wait_ge(x3_out[i], used * 16 + 16)
                    wait_if_any(act, S["xn_done"], n)
                    for t in range(TPK):
                        act.activation(x3[:, i, t], s3[:, i, t], ACT.Identity, bias=shift[:, i, t:t + 1],
                                       scale=rstd[:, i, t:t + 1]).then_inc(S["x3_done"], 1)
                if norm_block:
                    n, i, used = norm_block
                    for t in range(TPK):
                        act.wait_ge(S["x3_done"], n * TPK + t + 1)
                        act.activation(square[:, t], x3[:, i, t], ACT.Square, accum_out=meansq[:, t:t + 1])\
                           .then_inc(S["squared"], 1)
                if norm_block:
                    n, i, used = norm_block
                    for c in range(CD):
                        act.wait_ge(S["x3_turned"], n * CD + c + 1)
                        act.activation(x3T[:, i, c], TR[CD + c][:], ACT.Copy).then_inc(S["x3_copied"], 1)
                if sum_block:
                    n, i, used = sum_block
                    act.wait_ge(S["aggr"], (n + 1) * TPK)
                    act.activation(std[:, i], moments[:, i, :, 1], ACT.Sqrt, bias=eps[:, 0:1]).then_inc(S["std_done"], 1)
                if norm_block:
                    n, i, used = norm_block
                    act.wait_ge(S["squared"], (n + 1) * TPK)
                    act.activation(rms[:, i], meansq[:], ACT.Sqrt, bias=eps[:, 0:1], scale=1.0 / DIM)\
                       .then_inc(S["rms_done"], 1)
                if route_block and not is_late(route_block[0]):
                    n, i, used = route_block
                    act.wait_ge(S["rrms_done"], n + 1)
                    act.wait_ge(S["xn_done"], n + 1)
                    for t in range(TPK):
                        act.activation(scaled3[:, t], x3[:, i, t], ACT.Copy, scale=rrms[:, i, t:t + 1])\
                           .then_inc(S["scaled3_done"], 1)

            steps(act, step, ROUTE)

        @block.vector
        def _(dve):
            dve.memset(eps[:], LN_EPS).then_inc(prep, 1)
            dve.memset(ones[:], 1.0)
            dve.memset(count[:], 0.0).then_inc(prep, 1)
            dve.tensor_copy(xn[:, :, :, DIM], const[:, C_NAMES:C_NAMES + 2 * TPK].rearrange("p (i t) -> p i t", i=2))
            dve.tensor_copy(before[:], const[:, C_BEFORE:C_BEFORE + P]).then_inc(prep, 1)
            dve.wait_ge(w_in, 16 * (4 + CD))
            dve.tensor_tensor(wrn[:], wr[:], nwc[:].to_broadcast([P, CD, E]), ALU.mult).then_inc(prep, 1)
            dve.wait_ge(prep, PREP)

            def step(p, h):
                att_block, sum_block, norm_block, route_block = (at(p, h, s) for s in (ATT, SUM, NORM, ROUTE))
                done = 0

                def chain(instructions, meanwhile=None):
                    nonlocal done
                    done += 1
                    if route_block:
                        instructions()[-1].then_inc(S["step"], 1)
                    if meanwhile:
                        meanwhile()
                    if route_block:
                        dve.wait_ge(S["step"], route_block[0] * ROUTE_STEPS + done)

                def head(t):
                    return TR[t][:].rearrange("p (h c) -> p h c", h=H1)

                def head_sums(k):
                    if att_block:
                        n, i, used = att_block
                        dve.wait_ge(S["att_turned"], n * TPK + k + 1)
                        t = TURN_ORDER[k]
                        dve.reciprocal(rec[:, t], head(t)[:, :, D1]).then_inc(S["rec_done"], 1)

                def weigh_heads(k):
                    if att_block:
                        n, i, used = att_block
                        dve.wait_ge(S["rec_done"], n * TPK + k + 1)
                        t = TURN_ORDER[k]
                        dve.tensor_tensor(att[:, i, t].rearrange("p (h c) -> p h c", h=H1), head(t)[:, :, 0:D1],
                                          rec[:, t].unsqueeze(2).to_broadcast([P, H1, D1]), ALU.mult)\
                           .then_inc(S["normed"], 1)

                def late_tokens():
                    n, i, used = route_block
                    dve.wait_ge(S["xn_free"], n + 1)
                    name = xn[:, i, :, DIM]
                    dve.tensor_scalar(name, name, float(2 * BLK * TOP_K), None, ALU.add)
                    for t in range(TPK):
                        mul = dve.scalar_tensor_tensor(out=xn[:, i, t, 0:DIM], in0=x3[:, i, t], scalar=rrms[:, i, t:t + 1],
                                                       in1=nw[:], op0=ALU.mult, op1=ALU.mult)
                    mul.then_inc(S["late_done"], 1)

                def first_heads():
                    for k in range(CD):
                        head_sums(k)
                    for k in range(CD):
                        weigh_heads(k)

                def residual(t):
                    if sum_block:
                        n, i, used = sum_block
                        if t == 0:
                            dve.wait_ge(x2_in[i], used * 16 + 16)
                        dve.wait_ge(S["projected"], n * TPK + t // 2 * 2 + 2)
                        dve.tensor_tensor(s3[:, i, t], x2[:, i, t], PX[t // 2][:, t % 2 * DIM:(t % 2 + 1) * DIM], ALU.add)\
                           .then_inc(S["summed"], 1)

                def statistics(t):
                    if sum_block:
                        n, i, used = sum_block
                        dve.wait_ge(S["summed"], n * TPK + t + 1)
                        dve.bn_stats(stats[:, t], s3[:, i, t]).then_inc(S["stat"], 1)

                if norm_block:
                    n, i, used = norm_block
                    dve.wait_ge(S["std_done"], n + 1)
                    dve.reciprocal(rstd[:, i], std[:, i]).then_inc(S["rstd_step"], 1)
                    dve.wait_ge(S["rstd_step"], n + 1)
                    dve.scalar_tensor_tensor(out=shift[:, i], in0=moments[:, i, :, 0], scalar=-1.0, in1=rstd[:, i],
                                             op0=ALU.mult, op1=ALU.mult).then_inc(S["rstd_done"], 1)
                if route_block:
                    n, i, used = route_block
                    dve.wait_ge(S["rms_done"], n + 1)
                    wait_if_any(dve, S["xn_done"], n)
                    dve.reciprocal(rrms[:, i], rms[:, i]).then_inc(S["rrms_done"], 1)
                    dve.wait_ge(S["rrms_done"], n + 1)
                    dve.wait_ge(S["logits_ready"], n + 1)
                chain(lambda: [dve.tensor_tensor(scaled[:], PL[:], rrms[:, i].unsqueeze(2).to_broadcast([P, TPK, E]),
                                                 ALU.mult)])
                chain(lambda: [dve.tensor_tensor(logits[:], scaled[:], br[:].unsqueeze(1).to_broadcast([P, TPK, E]),
                                                 ALU.add)])
                chain(lambda: [dve.tensor_reduce(top[:], logits[:], AX.X, ALU.max)])
                chain(lambda: [dve.tensor_tensor(below[:], logits[:], top[:].unsqueeze(2).to_broadcast([P, TPK, E]),
                                                 ALU.subtract)],
                      late_tokens if route_block and is_late(route_block[0]) else first_heads)
                if route_block:
                    dve.wait_ge(S["expd_done"], n + 1)
                chain(lambda: [dve.tensor_reduce(total[:], expd[:], AX.X, ALU.add)])
                chain(lambda: [dve.reciprocal(rtotal[:], total[:])])
                chain(lambda: [dve.tensor_tensor(prob[:], expd[:], rtotal[:].unsqueeze(2).to_broadcast([P, TPK, E]), ALU.mult)])
                if route_block:
                    dve.sem_inc(seen, 1)
                chain(lambda: [dve.max(best[:, t], prob[:, t]) for t in range(TPK)])
                if route_block:
                    dve.sem_inc(seen, 1)
                chain(lambda: [dve.max_index(besti[:, t], best[:, t], prob[:, t]) for t in range(TPK)])
                chain(lambda: [dve.tensor_copy(expert[:], besti[:, :, 0:TOP_K])])
                flat = [P, TPK * TOP_K, E]
                chain(lambda: [dve.tensor_tensor(onehot[:].rearrange("p t k e -> p (t k) e"),
                                                 iota.unsqueeze(1).to_broadcast(flat),
                                                 expert[:].rearrange("p t k -> p (t k)").unsqueeze(2).to_broadcast(flat),
                                                 ALU.is_equal),
                               dve.tensor_scalar(holds[:], expert[:], float(E_COPY), None, ALU.is_ge)])
                chain(lambda: [dve.tensor_tensor(chosen[:], onehot[:, :, 0], onehot[:, :, 1], ALU.add)])
                for t in range(TPK):
                    chain(lambda: [dve.tensor_tensor(count[:, i, t + 1], count[:, i, t], chosen[:, t], ALU.add)],
                          lambda: residual(t))
                if route_block:
                    dve.tensor_copy(count[:, 1 - i, 0], count[:, i, TPK]).then_inc(S["counted"], 1)
                for t in range(TPK):
                    statistics(t)
                if sum_block:
                    n, i, used = sum_block
                    dve.wait_ge(S["stat"], (n + 1) * TPK)
                    dve.sem_inc(seen, 1)
                    for t in range(TPK):
                        dve.bn_aggr(moments[:, i, t], stats[:, t]).then_inc(S["aggr"], 1)
                if route_block:
                    n, i, used = route_block
                    dve.wait_ge(S["ranks_ready"], n + 1)
                chain(lambda: [dve.tensor_tensor(ranked[:, :, k], onehot[:, :, k], PR[:], ALU.mult) for k in range(TOP_K)],
                      lambda: head_sums(2))
                chain(lambda: [dve.tensor_reduce(rank[:], ranked[:], AX.X, ALU.add)], lambda: weigh_heads(2))
                chain(lambda: [dve.tensor_scalar(kept[:], rank[:], float(CAP), None, ALU.is_lt),
                               dve.tensor_scalar(place[:], rank[:], float(CAP - 1), None, ALU.min)], lambda: head_sums(3))
                chain(lambda: [dve.scalar_tensor_tensor(out=slot[:], in0=expert[:], scalar=float(CAP), in1=place[:],
                                                        op0=ALU.mult, op1=ALU.add),
                               dve.tensor_tensor(moves[:], holds[:], kept[:], ALU.mult),
                               dve.tensor_tensor(weight[:], best[:, :, 0:TOP_K], kept[:], ALU.mult)],
                      lambda: weigh_heads(3))
                if route_block:
                    dve.wait_ge(route_out[i], used * 16 + 16)
                    dve.wait_ge(S["xn_free"], n + 1)
                chain(lambda: [dve.tensor_scalar(target[:], moves[:], -NOWHERE, NOWHERE, ALU.mult, ALU.add),
                               dve.tensor_copy(xn[:, i, :, DIM + 1], expert[:, :, 0]),
                               dve.tensor_tensor(wsum[:], weight[:, :, 0], weight[:, :, 1], ALU.add)])
                chain(lambda: [dve.tensor_tensor(to_slot[:, i], target[:], slot[:], ALU.add),
                               dve.tensor_scalar(wzero[:], wsum[:], 0.0, None, ALU.is_le)])
                chain(lambda: [dve.tensor_tensor(divisor[:], wsum[:], wzero[:], ALU.add)])
                chain(lambda: [dve.reciprocal(rwsum[:], divisor[:])])
                if route_block:
                    dve.tensor_tensor(coef[:, i], weight[:], rwsum[:].unsqueeze(2).to_broadcast([P, TPK, TOP_K]), ALU.mult)\
                       .then_inc(S["routed"], 1)
                assert done == ROUTE_STEPS, done

            steps(dve, step, ROUTE)

        @block.gpsimd
        def _(pool):
            pool.sem_inc(S["xn_free"], 2)
            pool.sem_inc(S["xn_done"], 1)
            pool.wait_ge(prep, PREP)

            def step(p, h):
                if now := at(p, h, ROUTE):
                    n, i, used = now
                    if not is_late(n):
                        pool.wait_ge(S["scaled3_done"], (n + 1) * TPK)
                        pool.sem_inc(pool_seen, 1)
                        name = xn[:, i, :, DIM]
                        pool.tensor_scalar(name, name, float(2 * BLK * TOP_K), None, ALU.add)
                        pool.tensor_tensor(xn[:, i, :, 0:DIM], scaled3[:], nw[:].unsqueeze(1).to_broadcast([P, TPK, DIM]),
                                           ALU.mult).then_inc(S["xn_done"], 1)
                    if not isinstance(n, int) or n > 0:
                        pool.wait_ge(scattered, n * 16 * TPK * TOP_K)
                        pool.sem_inc(S["xn_free"], 1)
                    if is_late(n):
                        pool.wait_ge(S["late_done"], n - (BLOCKS - 2) + 1)
                    else:
                        pool.wait_ge(S["xn_done"], n + 2)
                    pool.wait_ge(S["routed"], n + 1)
                    pool.sem_inc(pool_seen, 1)
                    for t in range(TPK):
                        for k in range(TOP_K):
                            pool.indirect_dma_start(out=d["slots"], out_offset=bass.IndirectOffsetOnAxis(
                                ap=to_slot[:, i, t, k:k + 1].bitcast(U32), axis=0), in_=xn[:, i, t], in_offset=None,
                                bounds_check=SLOTS - 1, oob_is_err=False).then_inc(scattered, 16)

            steps(pool, step, ROUTE)
            pool.wait_ge(scattered, BLOCKS * 16 * TPK * TOP_K)


ROUTE_STEPS = 24
FFN = 1024
FC = FFN // P


class ExpertWeights:

    def __init__(self, nc, ctx):
        a = Alloc(nc, ctx, "w")
        self.w1 = a.sb("w1", [P, 2, CD, FFN])
        self.w2 = a.sb("w2", [P, 2, FC, DIM])
        self.b1 = a.sb("b1", [P, 2, FC])
        self.b2 = a.sb("b2", [P, 2, DIM])
        self.w1_in = [a.sem(f"w1_in{i}") for i in range(2)]
        self.w2_in = [a.sem(f"w2_in{i}") for i in range(2)]

    def load_up(self, eng, d, one, i):
        eng.dma_start(self.w1[:, i], d["L1_ffn_fc1T"][one].rearrange("o (c p) f -> p (o c) f", p=P))\
           .then_inc(self.w1_in[i], 16)
        eng.dma_start(self.b1[:, i], d["L1_ffn_fc1_biasT"][one].rearrange("o p c -> p (o c)")).then_inc(self.w1_in[i], 16)

    def load_first(self, eng, d):
        for e in range(2):
            self.load_up(eng, d, bass.ds(e, 1), e)
            self.load_down(eng, d, bass.ds(e, 1), e)

    def load_down(self, eng, d, one, i):
        eng.dma_start(self.w2[:, i], d["L1_ffn_fc2T"][one].rearrange("o (c p) n -> p (o c) n", p=P))\
           .then_inc(self.w2_in[i], 16)
        eng.dma_start(self.b2[:, i], d["L1_ffn_fc2_bias"][one].to_broadcast([P, DIM])).then_inc(self.w2_in[i], 16)


def phase_experts(nc, d, keep, weights):
    ST = CAP // P
    PLAIN = E_MLP - E_COPY
    with ExitStack() as ctx:
        a = Alloc(nc, ctx, "f")
        ident = keep["const"][:, C_IDENT:C_IDENT + P]
        w1, w2, b1, b2 = weights.w1, weights.w2, weights.b1, weights.b2
        w1_high, w1_low = (a.sb(f"w1_{half}", [P, CD, FFN], F32R) for half in ("high", "low"))
        w2_high, w2_low = (a.sb(f"w2_{half}", [P, 2, FC, DIM], F32R) for half in ("high", "low"))
        x = a.sb("x", [P, 2, ST, SLOT_COLS])
        plain = a.sb("plain", [P, PLAIN, ST, SLOT_COLS])
        constant = a.sb("constant", [P, E_MLP - E_CONST, DIM])
        plain_second, plain_names, plain_far = (a.sb("plain_" + n, [P, PLAIN, ST]) for n in ("second", "names", "far"))
        plain_to = a.sb("plain_to", [P, PLAIN, ST], I32)
        second, names, far = (a.sb(n, [P, ST]) for n in ("second", "names", "far"))
        to = a.sb("to", [P, 2, ST], I32)
        xT = a.sb("xT", [P, HALVES1, CD, CAP], F32R)
        h_high, h_low = (a.sb(f"h_{half}", [P, FC, CAP], F32R) for half in ("high", "low"))
        h = a.sb("h", [P, 4, CAP])
        y = a.sb("y", [P, 2, ST, DIM])
        TR = [a.ps(f"TR{i}", [P, CAP]) for i in range(CD)]
        PH = [a.ps(f"PH{i}", [P, CAP]) for i in range(4)]
        PY = [a.ps(f"PY{i}", [P, DIM]) for i in range(2)]
        x_in = [a.sem(f"x_in{i}") for i in range(2)]
        turned, x_high, x_low, w1_cut, w1_done, w2_cut, w2_done, h_ready, h_done, h_cut, h_left, y_ready, y_done = (
            a.sem(n) for n in ("turned", "x_high", "x_low", "w1_cut", "w1_done", "w2_cut", "w2_done", "h_ready", "h_done",
                               "h_cut", "h_left", "y_ready", "y_done"))
        plain_in, plain_step, plain_ready, name_step, to_ready, y_free, pool_seen, sent = (
            a.sem(n) for n in ("plain_in", "plain_step", "plain_ready", "name_step", "to_ready", "y_free", "pool_seen", "sent"))
        block = ctx.enter_context(nc.Block())

        def over_experts(eng, body, after_first=None):
            for i in range(2):
                body(0, i)
            if after_first:
                after_first()
            with eng.Fori(1, MLPS // 2) as e:
                for i in range(2):
                    body(e, i)

        def is_first(s, i):
            return first(s) and i == 0

        @block.sync
        def _(sp):
            def load(s, i):
                n = s * 2 + i
                e = n if isinstance(s, int) else sp.snap(n)
                at = bass.ds(e * CAP + E_MLP * CAP if isinstance(s, int) else sp.snap(n * CAP + E_MLP * CAP), CAP)
                one = bass.ds(e, 1)
                if not first(s):
                    sp.wait_ge(turned, (n - 1) * CD)
                    sp.wait_ge(to_ready, n - 1)
                sp.dma_start(x[:, i], d["slots"][at, :].rearrange("(t p) c -> p t c", p=P)).then_inc(x_in[i], 16)
                if not first(s):
                    sp.wait_ge(h_cut, (n - 1) * FC)
                    weights.load_up(sp, d, one, i)
                    sp.wait_ge(y_done, (n - 1) * ST)
                    weights.load_down(sp, d, one, i)

            def load_plain():
                rows = d["slots"][E_COPY * CAP:E_MLP * CAP, :].rearrange("(e t p) c -> p e t c", e=PLAIN, p=P)
                for e in range(PLAIN):
                    sp.dma_start(plain[:, e], rows[:, e]).then_inc(plain_in, 16)
                for e in range(E_MLP - E_CONST):
                    sp.dma_start(constant[:, e], d["L1_ffn_constant_vectors"][e:e + 1, :].to_broadcast([P, DIM]))\
                      .then_inc(plain_in, 16)

            over_experts(sp, load, load_plain)

        @block.tensor
        def _(pe):
            def turn(s, i):
                n = s * 2 + i
                pe.wait_ge(x_in[i], (s + 1) * 16)
                for c in range(CD):
                    if not is_first(s, i):
                        pe.wait_ge(x_low, (n - 1) * CD + c + 1)
                    for t in range(ST):
                        mm = pe.transpose(TR[c][:, t * P:(t + 1) * P], x[:, i, t, c * P:(c + 1) * P], ident)
                    mm.then_inc(turned, 1)

            def up(s, i):
                n = s * 2 + i
                pe.wait_ge(x_low, (n + 1) * CD)
                pe.wait_ge(w1_done, n + 1)
                for f in range(FC):
                    if not (is_first(s, i) and f < 4):
                        pe.wait_ge(h_cut, n * FC + f - 3)
                    at = slice(f * P, (f + 1) * P)
                    for k, (w, half) in enumerate(((w1_high, 0), (w1_high, 1), (w1_low, 0))):
                        for c in range(CD):
                            mm = pe.matmul(PH[f % 4][:], w[:, c, at], xT[:, half, c, :], start=(k == 0 and c == 0),
                                           stop=(k == 2 and c == CD - 1))
                    mm.then_inc(h_ready, 1)

            def down(n, i, new):
                pe.wait_ge(w2_done, n + 1)
                for t in range(ST):
                    if not (new and t < 2):
                        pe.wait_ge(y_done, n * ST + t - 1)
                    at = slice(t * P, (t + 1) * P)
                    for f in range(FC):
                        if t == 0:
                            pe.wait_ge(h_left, n * FC + f + 1)
                        for k, (hidden, w) in enumerate(((h_high, w2_high), (h_low, w2_high), (h_high, w2_low))):
                            mm = pe.matmul(PY[t % 2][:], hidden[:, f, at], w[:, i, f, :], start=(f == 0 and k == 0),
                                           stop=(f == FC - 1 and k == 2))
                    mm.then_inc(y_ready, 1)

            def body(s, i):
                turn(s, i)
                if not is_first(s, i):
                    down(s * 2 + i - 1, 1 - i, first(s) and i == 1)
                up(s, i)

            over_experts(pe, body)
            down(MLPS - 1, (MLPS - 1) % 2, False)

        @block.scalar
        def _(act):
            def body(s, i):
                n = s * 2 + i
                for c in range(CD):
                    act.wait_ge(turned, n * CD + c + 1)
                    act.activation(xT[:, 0, c], TR[c][:], ACT.Copy).then_inc(x_high, 1)
                for f in range(FC):
                    act.wait_ge(h_ready, n * FC + f + 1)
                    if not (is_first(s, i) and f < 4):
                        act.wait_ge(h_left, n * FC + f - 3)
                    act.activation(h[:, f % 4], PH[f % 4][:], ACT.Gelu, bias=b1[:, i, f:f + 1]).then_inc(h_done, 1)
                    act.activation(h_high[:, f], PH[f % 4][:], ACT.Gelu, bias=b1[:, i, f:f + 1]).then_inc(h_cut, 1)

            over_experts(act, body)

        @block.gpsimd
        def _(pool):
            pool.sem_inc(y_free, 2)

            def send(src, index):
                pool.indirect_dma_start(out=d["answers"], out_offset=bass.IndirectOffsetOnAxis(ap=index.bitcast(U32), axis=0),
                                        in_=src, in_offset=None, bounds_check=TOKENS * TOP_K - 1, oob_is_err=False)\
                    .then_inc(sent, 16)

            def body(s, i):
                n = s * 2 + i
                pool.wait_ge(to_ready, n + 1)
                for t in range(ST):
                    pool.wait_ge(y_done, n * ST + t + 1)
                    pool.sem_inc(pool_seen, 1)
                    send(y[:, i, t], to[:, i, t:t + 1])
                pool.wait_ge(sent, n * ST * 16 + (PLAIN + 1) * ST * 16)
                pool.sem_inc(y_free, 1)

            pool.wait_ge(plain_in, 16 * (PLAIN + E_MLP - E_CONST))
            pool.wait_ge(plain_ready, PLAIN)
            for e in range(PLAIN):
                for t in range(ST):
                    send(plain[:, e, t, 0:DIM] if e == 0 else constant[:, e - 1], plain_to[:, e, t:t + 1])
            over_experts(pool, body)

        @block.vector
        def _(dve):
            def cut_weights(w, high, low, arrived, times, cut, done, n):
                def take_high():
                    dve.wait_ge(arrived, times)
                    dve.tensor_copy(high, w).then_inc(cut, 1)

                def leave_low():
                    dve.wait_ge(cut, n + 1)
                    dve.tensor_tensor(low, w, high.bitcast(F32), ALU.subtract).then_inc(done, 1)
                return [take_high, leave_low]


            def destinations(rows, expert, second, far, names, to, step, steps_before, ready):
                dve.tensor_scalar(far, rows[:, :, DIM], 0.0, NOWHERE, ALU.is_le, ALU.mult)
                dve.tensor_scalar(second, rows[:, :, DIM + 1], expert, -1.0, ALU.not_equal, ALU.add).then_inc(step, 1)
                dve.wait_ge(step, steps_before + 1)
                dve.tensor_tensor(names, rows[:, :, DIM], second, ALU.add).then_inc(step, 1)
                dve.wait_ge(step, steps_before + 2)
                dve.tensor_tensor(to, names, far, ALU.add).then_inc(ready, 1)

            def numbers(n):
                return keep["const"][:, bass.ds(C_IOTA + E_MLP + n if isinstance(n, int) else dve.snap(n + (C_IOTA + E_MLP)), 1)]

            def plain_destinations():
                dve.wait_ge(plain_in, 16 * (PLAIN + E_MLP - E_CONST))
                for e in range(PLAIN):
                    destinations(plain[:, e], float(E_COPY + e), plain_second[:, e], plain_far[:, e], plain_names[:, e],
                                 plain_to[:, e], plain_step, 2 * e, plain_ready)

            def sums(n, i, t):
                if t == 0:
                    dve.wait_ge(y_free, n + 1)
                dve.wait_ge(y_ready, n * ST + t + 1)
                dve.tensor_tensor(y[:, i, t], b2[:, i], PY[t % 2][:], ALU.add).then_inc(y_done, 1)

            def body(s, i):
                n = s * 2 + i
                cuts = (cut_weights(w1[:, i], w1_high[:], w1_low[:], weights.w1_in[i], (s + 1) * 32, w1_cut, w1_done, n)
                        + cut_weights(w2[:, i], w2_high[:, i], w2_low[:, i], weights.w2_in[i], (s + 1) * 32, w2_cut, w2_done, n))
                if is_first(s, i):
                    for cut in cuts[:2]:
                        cut()
                for c in range(CD):
                    dve.wait_ge(x_high, n * CD + c + 1)
                    dve.tensor_tensor(xT[:, 1, c], TR[c][:], xT[:, 0, c].bitcast(F32), ALU.subtract).then_inc(x_low, 1)
                for t in range(ST):
                    if not (is_first(s, i) and t < 2):
                        cuts[t]()
                    if not is_first(s, i):
                        sums(n - 1, 1 - i, t)
                dve.wait_ge(y_free, n + 1)
                destinations(x[:, i], numbers(n), second[:], far[:], names[:], to[:, i], name_step, n * 2, to_ready)
                for f in range(FC):
                    dve.wait_ge(h_cut, n * FC + f + 1)
                    dve.tensor_tensor(h_low[:, f], h[:, f % 4], h_high[:, f].bitcast(F32), ALU.subtract)\
                       .then_inc(h_left, 1)

            over_experts(dve, body, plain_destinations)
            for t in range(ST):
                sums(MLPS - 1, (MLPS - 1) % 2, t)


def phase_combine(nc, d, keep, tokens):
    with ExitStack() as ctx:
        a = Alloc(nc, ctx, "g")
        x3, coef = tokens.x3, tokens.coef
        AHEAD = 3
        got = a.sb("got", [P, TILES, TOP_K, DIM])
        y = a.sb("y", [P, TILES, DIM])
        eps = a.sb("eps", [P, 1])
        stats = a.sb("stats", [P, TILES, 6])
        moments = a.sb("moments", [P, TILES, 2])
        std = a.sb("std", [P, TILES])
        rstd = a.sb("rstd", [P, TILES])
        shift = a.sb("shift", [P, TILES])
        prep, out_done = a.sem("prep"), a.sem("out_done")
        block_in = [a.sem(f"block_in{i}") for i in range(BLOCKS)]
        weighted, with_first, summed, stat, aggr, std_done, rstd_step, rstd_done, y_done = (
            a.sem(n) for n in ("weighted", "with_first", "summed", "stat", "aggr", "std_done", "rstd_step", "rstd_done",
                               "y_done"))
        block = ctx.enter_context(nc.Block())

        def tiles(n):
            return slice(n * TPK, (n + 1) * TPK)

        @block.sync
        def _(sp):
            answers = d["answers"].rearrange("(n t p k) c -> n p t (k c)", n=BLOCKS, p=P, k=TOP_K)
            for n in range(BLOCKS):
                sp.dma_start(got[:, tiles(n)].rearrange("p t k c -> p t (k c)"), answers[n]).then_inc(block_in[n], 16)
            for n in range(BLOCKS):
                sp.wait_ge(y_done, (n + 1) * TPK)
                sp.dma_start(d["out"][n * BLK:(n + 1) * BLK, :].rearrange("(t p) c -> p t c", p=P), y[:, tiles(n)])\
                  .then_inc(out_done, 16)
            sp.wait_ge(out_done, 16 * BLOCKS)

        @block.scalar
        def _(act):
            def weigh(n):
                if n < BLOCKS:
                    act.wait_ge(block_in[n], 16)
                    for t in range(n * TPK, (n + 1) * TPK):
                        act.activation(got[:, t, 0], got[:, t, 0], ACT.Copy, scale=coef[:, TOP_K * t:TOP_K * t + 1])\
                           .then_inc(weighted, 1)

            for n in range(AHEAD):
                weigh(n)
            act.wait_ge(prep, 1)
            def norm(n):
                act.wait_ge(rstd_done, n + 1)
                for t in range(n * TPK, (n + 1) * TPK):
                    act.activation(y[:, t], got[:, t, 1], ACT.Identity, bias=shift[:, t:t + 1], scale=rstd[:, t:t + 1])\
                       .then_inc(y_done, 1)

            for n in range(BLOCKS):
                act.wait_ge(aggr, (n + 1) * TPK)
                act.activation(std[:, tiles(n)], moments[:, tiles(n), 1], ACT.Sqrt, bias=eps[:, 0:1]).then_inc(std_done, 1)
                weigh(n + AHEAD)
                if n:
                    norm(n - 1)
            norm(BLOCKS - 1)

        @block.gpsimd
        def _(pool):
            for n in range(BLOCKS):
                pool.wait_ge(weighted, (n + 1) * TPK)
                pool.tensor_tensor(x3[:, tiles(n)], x3[:, tiles(n)], got[:, tiles(n), 0], ALU.add).then_inc(with_first, 1)

        @block.vector
        def _(dve):
            dve.memset(eps[:], LN_EPS).then_inc(prep, 1)

            def total(n):
                dve.wait_ge(with_first, n + 1)
                for t in range(n * TPK, (n + 1) * TPK):
                    dve.scalar_tensor_tensor(out=got[:, t, 1], in0=got[:, t, 1], scalar=coef[:, TOP_K * t + 1:TOP_K * t + 2],
                                             in1=x3[:, t], op0=ALU.mult, op1=ALU.add).then_inc(summed, 1)
                for t in range(n * TPK, (n + 1) * TPK):
                    dve.wait_ge(summed, t + 1)
                    dve.bn_stats(stats[:, t], got[:, t, 1]).then_inc(stat, 1)
                for t in range(n * TPK, (n + 1) * TPK):
                    dve.wait_ge(stat, t + 1)
                    dve.bn_aggr(moments[:, t], stats[:, t]).then_inc(aggr, 1)

            def scale(n):
                dve.wait_ge(std_done, n + 1)
                dve.reciprocal(rstd[:, tiles(n)], std[:, tiles(n)]).then_inc(rstd_step, 1)
                dve.wait_ge(rstd_step, n + 1)
                dve.scalar_tensor_tensor(out=shift[:, tiles(n)], in0=moments[:, tiles(n), 0], scalar=-1.0,
                                         in1=rstd[:, tiles(n)], op0=ALU.mult, op1=ALU.mult).then_inc(rstd_done, 1)

            for n in range(BLOCKS):
                total(n)
                if n:
                    scale(n - 1)
            scale(BLOCKS - 1)


def program(nc, d):
    with ExitStack() as ctx:
        keep = {"const": ctx.enter_context(nc.sbuf_tensor("const", [P, C_COLS], F32))}
        with ExitStack() as layer0:
            weights = Layer0Weights(nc, layer0)
            with ExitStack() as attention:
                stacks = Stacks0(nc, attention)
                phase_qkv0(nc, d, keep, stacks)
                phase_attention0(nc, d, keep, weights, stacks)
            phase_ffn0(nc, d, keep, weights)
        with ExitStack() as layer1:
            weights = ExpertWeights(nc, layer1)
            tokens = Routed(nc, layer1)
            with ExitStack() as routing:
                incoming = Unrouted(nc, routing)
                phase_attention1(nc, d, keep, weights, incoming)
                phase_route(nc, d, keep, weights, incoming, tokens)
            phase_experts(nc, d, keep, weights)
            phase_combine(nc, d, keep, tokens)


def layout(inputs):
    a = {name: np.ascontiguousarray(inputs[name]) for name in inputs}
    out = {"constants": constants()}
    x = a["L0_attn_x"].reshape(TOKENS, DIM)
    out["x"] = x
    out["xT"] = x.T
    out["L0_wqkvT"] = a["L0_attn_w_qkv"].T
    out["L0_wprojT"] = a["L0_attn_w_proj"].T
    for name in ("b_proj", "q_gamma", "q_beta", "k_gamma", "k_beta"):
        out["L0_attn_" + name] = a["L0_attn_" + name]
    for name in ("w_gate", "w_up", "w_down"):
        out["L0_ffn_" + name + "T"] = a["L0_ffn_" + name].T
    for name in ("L1_attn_w_qkv", "L1_attn_w_out", "L1_attn_head_scales", "L1_ffn_norm_weight", "L1_ffn_router_bias",
                 "L1_ffn_fc2_bias", "L1_ffn_constant_vectors"):
        out[name] = a[name]
    out["L1_ffn_router_weightT"] = a["L1_ffn_router_weight"].T
    out["L1_ffn_fc1_biasT"] = a["L1_ffn_fc1_bias"].reshape(MLPS, FC, P).transpose(0, 2, 1)
    out["L1_ffn_fc1T"] = a["L1_ffn_fc1_weight"].transpose(0, 2, 1)
    out["L1_ffn_fc2T"] = a["L1_ffn_fc2_weight"].transpose(0, 2, 1)
    return {name: np.ascontiguousarray(v) for name, v in out.items()}


SCRATCH = {
    "qk0": ([PARTS * QK_BLK, P, TOKENS], BF16),
    "v0": ([TOKENS, H0 * VS0], F32),
    "att0": ([HG0, P, TOKENS], F32),
    "x2": ([TOKENS, DIM], F32),
    "qk1": ([HALVES1 * 4, P, TOKENS], F32),
    "v1": ([TOKENS, H1 * VS1], F32),
    "att1": ([HG1, P, TOKENS], F32),
    "slots": ([E * CAP, SLOT_COLS], F32),
    "answers": ([TOKENS * TOP_K, DIM], F32),
}


def kernel(**inputs):
    import concourse.bacc as bacc
    from concourse.bass_utils import run_bass_kernel_spmd

    nc = bacc.Bacc("TRN2", target_bir_lowering=False, num_devices=1)
    arrays = layout(inputs)
    d = {name: nc.dram_tensor(name, v.shape, mybir.dt.from_np(v.dtype), kind="ExternalInput").ap()
         for name, v in arrays.items()}
    for name, (shape, dt) in SCRATCH.items():
        d[name] = nc.dram_tensor(name, shape, dt).ap()
    d["out"] = nc.dram_tensor("out", [TOKENS, DIM], F32, kind="ExternalOutput").ap()
    program(nc, d)
    result = run_bass_kernel_spmd(nc, [arrays], core_ids=[0])
    return result.results[0]["out"].reshape(BATCH, SEQ, DIM)
```
